# Optimizing a Trainium2 kernel written in Bass

```python
import numpy as np
import jax
import jax.numpy as jnp

def _softmax(x, axis=-1):
    return jax.nn.softmax(x, axis=axis)

def _gelu(x):
    return jax.nn.gelu(x, approximate=True)

def _silu(x):
    return jax.nn.silu(x)

def _sigmoid(x):
    return jax.nn.sigmoid(x)

def _layernorm(x, axis=-1, eps=1e-05):
    m = jnp.mean(x, axis=axis, keepdims=True)
    v = jnp.var(x, axis=axis, keepdims=True)
    return (x - m) / jnp.sqrt(v + eps)

def _scatter_add(tgt, idx, src, axis=0):
    return tgt.at[idx].add(src)

def _segment_sum(src, seg, n):
    return jax.ops.segment_sum(src, seg, n)
kernel_name = 'mk_vit_tower_cls_d4_tok_img4096_r4_b7037b'

def setup_inputs(seed: int=0):
    np.random.seed(seed)
    _w = jnp.asarray

    def _rec_inputs():
        import jax
        import jax.numpy as jnp
        _rk = jax.random.key(seed)
        x = -0.0043416 + 0.998921 * jax.random.normal(jax.random.fold_in(_rk, 1), (32, 64, 64, 2), jnp.float32)
        cls_tok = 0.02 * jax.random.normal(jax.random.fold_in(_rk, 5), (1, 1, 1024), jnp.float32)
        return (x, cls_tok)
    x, cls_tok = _rec_inputs()

    def _L0_tok_setup():
        import jax, jax.numpy as jnp
        import numpy as np
        H, N, CH = (64, 64, 1)
        key = jax.random.key(seed)
        k1, k2, k3 = jax.random.split(key, 3)
        A_abslog = jnp.log(jax.random.uniform(k1, (H, N), dtype=jnp.float32, minval=0.5, maxval=0.999))
        A_phase = jax.random.uniform(k2, (H, N), dtype=jnp.float32, minval=-np.pi, maxval=np.pi)
        C = jax.random.normal(k3, (CH, H, N, 2), dtype=jnp.float32)
        return {'A_abslog': A_abslog, 'A_phase': A_phase, 'C': C, 'L': 1024}
    _L0_tok_all = _L0_tok_setup()
    _L0_tok_in = {k: v for k, v in _L0_tok_all.items() if k in ('A_abslog', 'A_phase')}
    del _L0_tok_all

    def _L0_attn_setup():
        import jax, jax.numpy as jnp
        import numpy as np
        B, S, E, H = (2, 512, 1024, 32)
        D = E // H
        ROPE_BASE = 10000.0
        MASK_VAL = -66504.0

        def _rope(x, cos, sin):
            x1, x2 = jnp.split(x, 2, axis=-1)
            return jnp.concatenate([x1 * cos - x2 * sin, x2 * cos + x1 * sin], axis=-1)
        key = jax.random.key(seed)
        k1, k2, k3, k4, k5 = jax.random.split(key, 5)
        return {'hidden_states': jax.random.normal(k1, (B, S, E), dtype=jnp.float32), 'qkv_w': jax.random.normal(k2, (E, 3 * E), dtype=jnp.float32) * 0.02, 'qkv_b': jax.random.normal(k3, (3 * E,), dtype=jnp.float32) * 0.02, 'out_w': jax.random.normal(k4, (E, E), dtype=jnp.float32) * 0.02, 'out_b': jax.random.normal(k5, (E,), dtype=jnp.float32) * 0.02}
    _L0_attn_all = _L0_attn_setup()
    _L0_attn_in = {k: v for k, v in _L0_attn_all.items() if k in ('qkv_w', 'qkv_b', 'out_w', 'out_b')}
    del _L0_attn_all

    def _L0_ffn_setup():
        import jax, jax.numpy as jnp
        import numpy as np
        D_IN = 1024
        D_OUT = 1024
        RANK = 16
        NUM_EXPERTS = 8
        TOP_K = 2
        SCALING = 32.0 / RANK
        key = jax.random.key(seed)
        ks = jax.random.split(key, 6)
        x = jax.random.normal(ks[0], (4, 512, D_IN), dtype=jnp.float32)
        W_base = jax.random.normal(ks[1], (D_OUT, D_IN), dtype=jnp.float32) * (1.0 / np.sqrt(D_IN))
        b_base = jax.random.normal(ks[2], (D_OUT,), dtype=jnp.float32) * 0.01
        W_router = jax.random.normal(ks[3], (NUM_EXPERTS, D_IN), dtype=jnp.float32) * 0.01
        A_stack = jax.random.uniform(ks[4], (NUM_EXPERTS, RANK, D_IN), dtype=jnp.float32, minval=-1.0, maxval=1.0) * (1.0 / np.sqrt(D_IN))
        B_stack = jax.random.normal(ks[5], (NUM_EXPERTS, D_OUT, RANK), dtype=jnp.float32) * 0.02
        return {'x': x, 'W_base': W_base, 'b_base': b_base, 'W_router': W_router, 'A_stack': A_stack, 'B_stack': B_stack}
    _L0_ffn_all = _L0_ffn_setup()
    _L0_ffn_in = {k: v for k, v in _L0_ffn_all.items() if k in ('W_base', 'b_base', 'W_router', 'A_stack', 'B_stack')}
    del _L0_ffn_all

    def _L1_attn_setup():
        import jax, jax.numpy as jnp
        import numpy as np
        HDC_DIM = 1024
        N_HEADS = 4
        HEAD_DIM = HDC_DIM // N_HEADS

        def _ste_sign(w):
            alpha = jnp.mean(jnp.abs(w), axis=-1, keepdims=True)
            hard = alpha * jnp.sign(w)
            hard = jnp.where(hard == 0, alpha, hard)
            return jax.lax.stop_gradient(hard - w) + w
        key = jax.random.key(seed)
        kx, kq, kk, kv = jax.random.split(key, 4)
        B, T = (4, 512)
        x = jax.random.normal(kx, (B, T, HDC_DIM), dtype=jnp.float32)
        bv_q = jax.random.normal(kq, (N_HEADS, HEAD_DIM), dtype=jnp.float32) * 0.02
        bv_k = jax.random.normal(kk, (N_HEADS, HEAD_DIM), dtype=jnp.float32) * 0.02
        bv_v = jax.random.normal(kv, (N_HEADS, HEAD_DIM), dtype=jnp.float32) * 0.02
        return {'x': x, 'bv_q': bv_q, 'bv_k': bv_k, 'bv_v': bv_v}
    _L1_attn_all = _L1_attn_setup()
    _L1_attn_in = {k: v for k, v in _L1_attn_all.items() if k in ('bv_q', 'bv_k', 'bv_v')}
    del _L1_attn_all

    def _L1_ffn_setup():
        import jax, jax.numpy as jnp
        import numpy as np
        R = 16
        LORA_ALPHA = 16
        SCALING = LORA_ALPHA / R
        key = jax.random.key(seed)
        kx, kr, ka = jax.random.split(key, 3)
        B, S, D, DO, E = (4, 512, 1024, 1024, 8)
        x = jax.random.normal(kx, (B, S, D), dtype=jnp.float32)
        bound_r = 1.0 / np.sqrt(D)
        route_w = jax.random.uniform(kr, (E, D), jnp.float32, -bound_r, bound_r)
        bound_a = 1.0 / np.sqrt(D)
        A = jax.random.uniform(ka, (E, R, D), jnp.float32, -bound_a, bound_a)
        kb = jax.random.fold_in(key, 7)
        Bw = jax.random.normal(kb, (E, DO, R), dtype=jnp.float32) * 0.02
        return {'x': x, 'route_w': route_w, 'A': A, 'Bw': Bw}
    _L1_ffn_all = _L1_ffn_setup()
    _L1_ffn_in = {k: v for k, v in _L1_ffn_all.items() if k in ('route_w', 'A', 'Bw')}
    del _L1_ffn_all

    def _L2_attn_setup():
        import jax, jax.numpy as jnp
        import numpy as np
        import math
        D_MODEL = 512
        D_STATE = 16
        EXPAND = 2
        D_INNER = D_MODEL * EXPAND
        DT_RANK = math.ceil(D_MODEL / 16)
        BATCH, SEQ_LEN = (2, 128)
        key = jax.random.key(seed)
        ks = jax.random.split(key, 6)
        x = jax.random.normal(ks[0], (BATCH, SEQ_LEN, D_INNER), dtype=jnp.float32)
        A_log = jnp.log(jax.random.uniform(ks[1], (D_INNER, D_STATE), minval=0.5, maxval=16.0, dtype=jnp.float32))
        D = jnp.ones((D_INNER,), dtype=jnp.float32)
        x_proj_w = 0.02 * jax.random.normal(ks[2], (DT_RANK + 2 * D_STATE, D_INNER), dtype=jnp.float32)
        dt_init_std = DT_RANK ** (-0.5)
        dt_proj_w = jax.random.uniform(ks[3], (D_INNER, DT_RANK), minval=-dt_init_std, maxval=dt_init_std, dtype=jnp.float32)
        dt = jnp.exp(jax.random.uniform(ks[4], (D_INNER,), dtype=jnp.float32) * (math.log(0.1) - math.log(0.001)) + math.log(0.001))
        dt = jnp.clip(dt, 0.0001, None)
        dt_proj_b = dt + jnp.log(-jnp.expm1(-dt))
        return {'x': x, 'A_log': A_log, 'D': D, 'x_proj_w': x_proj_w, 'dt_proj_w': dt_proj_w, 'dt_proj_b': dt_proj_b}
    _L2_attn_all = _L2_attn_setup()
    _L2_attn_in = {k: v for k, v in _L2_attn_all.items() if k in ('A_log', 'D', 'x_proj_w', 'dt_proj_w', 'dt_proj_b')}
    del _L2_attn_all

    def _L2_ffn_setup():
        import math
        import jax, jax.numpy as jnp
        import numpy as np
        SCALING = 16.0 / 32.0

        def real_fourier_orthogonal_multiply(c):
            n = c.shape[-1]
            sqrt_n = math.sqrt(n)
            pair_scale = math.sqrt(n / 2.0)
            max_f = (n - 1) // 2
            work = c.astype(jnp.float32)
            dc = (work[..., 0] * sqrt_n)[..., None].astype(jnp.complex64)
            cos = work[..., 1:1 + 2 * max_f:2] * pair_scale
            sin = work[..., 2:2 + 2 * max_f:2] * pair_scale
            mid = (cos - 1j * sin).astype(jnp.complex64)
            parts = [dc, mid]
            if n % 2 == 0:
                parts.append((work[..., -1] * sqrt_n)[..., None].astype(jnp.complex64))
            spectrum = jnp.concatenate(parts, axis=-1)
            return jnp.fft.irfft(spectrum, n=n, axis=-1).astype(c.dtype)
        key = jax.random.key(seed)
        ks = jax.random.split(key, 9)
        B, S, D_in, D_out, R0, R1, E = (4, 512, 1024, 1024, 32, 8, 3)
        x = jax.random.normal(ks[0], (B, S, D_in), dtype=jnp.float32)
        W_base = jax.random.normal(ks[1], (D_out, D_in), dtype=jnp.float32) * 0.02
        b_base = jax.random.normal(ks[2], (D_out,), dtype=jnp.float32) * 0.02
        enc0 = jax.random.normal(ks[3], (R0, D_in), dtype=jnp.float32) * 0.02
        enc1 = jax.random.normal(ks[4], (R1, D_in), dtype=jnp.float32) * 0.02
        coefs0 = jax.random.normal(ks[5], (E, D_out, R0), dtype=jnp.float32) * 0.02
        coefs1 = jax.random.normal(ks[6], (E, D_out, R1), dtype=jnp.float32) * 0.02
        mask0 = jax.random.randint(ks[7], (E, D_out, R0), 0, 2).astype(bool)
        mask1 = jax.random.randint(ks[8], (E, D_out, R1), 0, 2).astype(bool)
        return dict(x=x, W_base=W_base, b_base=b_base, enc0=enc0, enc1=enc1, coefs0=coefs0, coefs1=coefs1, mask0=mask0, mask1=mask1)
    _L2_ffn_all = _L2_ffn_setup()
    _L2_ffn_in = {k: v for k, v in _L2_ffn_all.items() if k in ('W_base', 'b_base', 'enc0', 'enc1', 'coefs0', 'coefs1', 'mask0', 'mask1')}
    del _L2_ffn_all

    def _L3_attn_setup():
        import jax, jax.numpy as jnp
        import numpy as np
        EMBED = 1024
        H = 32
        KV = 8
        D = EMBED // H
        REP = H // KV

        def _rope(t, cos, sin):
            t = t.reshape(*t.shape[:-1], 2, D // 2)
            t1, t2 = (t[..., 0, :], t[..., 1, :])
            return jnp.concatenate([t1 * cos - t2 * sin, t1 * sin + t2 * cos], axis=-1)
        key = jax.random.key(seed)
        ks = jax.random.split(key, 7)
        B, S = (1, 512)
        x = jax.random.normal(ks[0], (B, S, EMBED), dtype=jnp.float32)
        wq = jax.random.normal(ks[1], (EMBED, EMBED), dtype=jnp.float32) * 0.02
        bq = jax.random.normal(ks[2], (EMBED,), dtype=jnp.float32) * 0.02
        wk = jax.random.normal(ks[3], (EMBED, KV * D), dtype=jnp.float32) * 0.02
        bk = jax.random.normal(ks[4], (KV * D,), dtype=jnp.float32) * 0.02
        wv = jax.random.normal(ks[5], (EMBED, KV * D), dtype=jnp.float32) * 0.02
        bv = jax.random.normal(ks[6], (KV * D,), dtype=jnp.float32) * 0.02
        return {'x': x, 'wq': wq, 'bq': bq, 'wk': wk, 'bk': bk, 'wv': wv, 'bv': bv}
    _L3_attn_all = _L3_attn_setup()
    _L3_attn_in = {k: v for k, v in _L3_attn_all.items() if k in ('wq', 'bq', 'wk', 'bk', 'wv', 'bv')}
    del _L3_attn_all

    def _L3_ffn_setup():
        import jax, jax.numpy as jnp
        import numpy as np
        import math
        B, S, IN, OUT = (4, 512, 1024, 1024)
        E, R, K = (8, 64, 128)
        SCALE = 64.0 / 64.0
        MULTIPLIER = 1.0
        key = jax.random.key(seed)
        ks = jax.random.split(key, 6)
        return {'x': jax.random.normal(ks[0], (B, S, IN), jnp.float32), 'W_org': jax.random.normal(ks[1], (OUT, IN), jnp.float32) * 0.02, 'lora_down': jax.random.normal(ks[2], (E, IN, R), jnp.float32) * 0.02, 'lora_up': jax.random.normal(ks[3], (E, R, OUT), jnp.float32) * 0.02, 'lora_keys': jax.random.normal(ks[4], (E, K), jnp.float32), 'Wq': jax.random.normal(ks[5], (K, IN), jnp.float32) * 0.02}
    _L3_ffn_all = _L3_ffn_setup()
    _L3_ffn_in = {k: v for k, v in _L3_ffn_all.items() if k in ('W_org', 'lora_down', 'lora_up', 'lora_keys', 'Wq')}
    del _L3_ffn_all
    return {'x': x, 'cls_tok': cls_tok, 'L0_tok_A_abslog': _L0_tok_in['A_abslog'], 'L0_tok_A_phase': _L0_tok_in['A_phase'], 'L0_attn_qkv_w': _L0_attn_in['qkv_w'], 'L0_attn_qkv_b': _L0_attn_in['qkv_b'], 'L0_attn_out_w': _L0_attn_in['out_w'], 'L0_attn_out_b': _L0_attn_in['out_b'], 'L0_ffn_W_base': _L0_ffn_in['W_base'], 'L0_ffn_b_base': _L0_ffn_in['b_base'], 'L0_ffn_W_router': _L0_ffn_in['W_router'], 'L0_ffn_A_stack': _L0_ffn_in['A_stack'], 'L0_ffn_B_stack': _L0_ffn_in['B_stack'], 'L1_attn_bv_q': _L1_attn_in['bv_q'], 'L1_attn_bv_k': _L1_attn_in['bv_k'], 'L1_attn_bv_v': _L1_attn_in['bv_v'], 'L1_ffn_route_w': _L1_ffn_in['route_w'], 'L1_ffn_A': _L1_ffn_in['A'], 'L1_ffn_Bw': _L1_ffn_in['Bw'], 'L2_attn_A_log': _L2_attn_in['A_log'], 'L2_attn_D': _L2_attn_in['D'], 'L2_attn_x_proj_w': _L2_attn_in['x_proj_w'], 'L2_attn_dt_proj_w': _L2_attn_in['dt_proj_w'], 'L2_attn_dt_proj_b': _L2_attn_in['dt_proj_b'], 'L2_ffn_W_base': _L2_ffn_in['W_base'], 'L2_ffn_b_base': _L2_ffn_in['b_base'], 'L2_ffn_enc0': _L2_ffn_in['enc0'], 'L2_ffn_enc1': _L2_ffn_in['enc1'], 'L2_ffn_coefs0': _L2_ffn_in['coefs0'], 'L2_ffn_coefs1': _L2_ffn_in['coefs1'], 'L2_ffn_mask0': _L2_ffn_in['mask0'], 'L2_ffn_mask1': _L2_ffn_in['mask1'], 'L3_attn_wq': _L3_attn_in['wq'], 'L3_attn_bq': _L3_attn_in['bq'], 'L3_attn_wk': _L3_attn_in['wk'], 'L3_attn_bk': _L3_attn_in['bk'], 'L3_attn_wv': _L3_attn_in['wv'], 'L3_attn_bv': _L3_attn_in['bv'], 'L3_ffn_W_org': _L3_ffn_in['W_org'], 'L3_ffn_lora_down': _L3_ffn_in['lora_down'], 'L3_ffn_lora_up': _L3_ffn_in['lora_up'], 'L3_ffn_lora_keys': _L3_ffn_in['lora_keys'], 'L3_ffn_Wq': _L3_ffn_in['Wq']}

def reference(x, cls_tok, L0_tok_A_abslog, L0_tok_A_phase, L0_attn_qkv_w, L0_attn_qkv_b, L0_attn_out_w, L0_attn_out_b, L0_ffn_W_base, L0_ffn_b_base, L0_ffn_W_router, L0_ffn_A_stack, L0_ffn_B_stack, L1_attn_bv_q, L1_attn_bv_k, L1_attn_bv_v, L1_ffn_route_w, L1_ffn_A, L1_ffn_Bw, L2_attn_A_log, L2_attn_D, L2_attn_x_proj_w, L2_attn_dt_proj_w, L2_attn_dt_proj_b, L2_ffn_W_base, L2_ffn_b_base, L2_ffn_enc0, L2_ffn_enc1, L2_ffn_coefs0, L2_ffn_coefs1, L2_ffn_mask0, L2_ffn_mask1, L3_attn_wq, L3_attn_bq, L3_attn_wk, L3_attn_bk, L3_attn_wv, L3_attn_bv, L3_ffn_W_org, L3_ffn_lora_down, L3_ffn_lora_up, L3_ffn_lora_keys, L3_ffn_Wq):
    import jax
    import jax.numpy as jnp

    def _L0_tok_ref(A_abslog, A_phase, C, L):
        import jax, jax.numpy as jnp
        import numpy as np
        H, N, CH = (64, 64, 1)
        A = jnp.exp(A_abslog + 1j * A_phase)
        dtA = jnp.log(A)
        Cc = C[..., 0] + 1j * C[..., 1]
        Cc = Cc * (A - 1.0) / dtA
        t = jnp.arange(L, dtype=jnp.float32)
        K = jnp.exp(dtA[:, :, None] * t)
        K = jnp.einsum('chn,hnl->chl', Cc, K)
        return 2.0 * K.real

    def _L0_attn_ref(hidden_states, qkv_w, qkv_b, out_w, out_b):
        import jax, jax.numpy as jnp
        import numpy as np
        B, S, E, H = (2, 512, 1024, 32)
        D = E // H
        ROPE_BASE = 10000.0
        MASK_VAL = -66504.0

        def _rope(x, cos, sin):
            x1, x2 = jnp.split(x, 2, axis=-1)
            return jnp.concatenate([x1 * cos - x2 * sin, x2 * cos + x1 * sin], axis=-1)
        b, s, e = hidden_states.shape
        qkv = hidden_states @ qkv_w + qkv_b
        q, k, v = jnp.split(qkv, 3, axis=-1)
        q = q.reshape(b, s, H, D)
        k = k.reshape(b, s, H, D)
        v = v.reshape(b, s, H, D)
        half = D // 2
        inv_freq = 1.0 / ROPE_BASE ** (jnp.arange(0, half, dtype=jnp.float32) / half)
        ang = jnp.arange(s, dtype=jnp.float32)[:, None] * inv_freq[None, :]
        cos = jnp.cos(ang)[None, :, None, :]
        sin = jnp.sin(ang)[None, :, None, :]
        q = _rope(q, cos, sin)
        k = _rope(k, cos, sin)
        scale = 1.0 / jnp.sqrt(jnp.asarray(D, dtype=hidden_states.dtype))
        scores = jnp.einsum('bqhd,bkhd->bhqk', q, k) * scale
        causal = jnp.tril(jnp.ones((s, s), dtype=scores.dtype))
        scores = scores + (1.0 - causal) * MASK_VAL
        probs = jax.nn.softmax(scores, axis=-1)
        ctx = jnp.einsum('bhqk,bkhd->bqhd', probs, v).reshape(b, s, e)
        return ctx @ out_w + out_b

    def _L0_ffn_ref(x, W_base, b_base, W_router, A_stack, B_stack):
        import jax, jax.numpy as jnp
        import numpy as np
        D_IN = 1024
        D_OUT = 1024
        RANK = 16
        NUM_EXPERTS = 8
        TOP_K = 2
        SCALING = 32.0 / RANK
        orig_shape = x.shape
        xf = x.reshape(-1, D_IN)
        logits = xf @ W_router.T
        probs = jax.nn.softmax(logits, axis=-1)
        topk_p, topk_i = jax.lax.top_k(probs, TOP_K)
        topk_p = topk_p / jnp.sum(topk_p, axis=-1, keepdims=True)
        combine = jnp.sum(jax.nn.one_hot(topk_i, NUM_EXPERTS, dtype=xf.dtype) * topk_p[..., None], axis=1)
        h = jnp.einsum('nd,erd->ner', xf, A_stack)
        h = h * combine[..., None]
        lora_out = jnp.einsum('ner,eor->no', h, B_stack) * SCALING
        base_out = xf @ W_base.T + b_base
        out = base_out + lora_out
        return out.reshape(orig_shape[:-1] + (D_OUT,))

    def _L1_attn_ref(x, bv_q, bv_k, bv_v):
        import jax, jax.numpy as jnp
        import numpy as np
        HDC_DIM = 1024
        N_HEADS = 4
        HEAD_DIM = HDC_DIM // N_HEADS

        def _ste_sign(w):
            alpha = jnp.mean(jnp.abs(w), axis=-1, keepdims=True)
            hard = alpha * jnp.sign(w)
            hard = jnp.where(hard == 0, alpha, hard)
            return jax.lax.stop_gradient(hard - w) + w
        B, T, D = x.shape
        H, HD = (N_HEADS, HEAD_DIM)
        scale = HD ** (-0.5)
        q_bind = _ste_sign(bv_q)
        k_bind = _ste_sign(bv_k)
        v_bind = _ste_sign(bv_v)
        xh = x.reshape(B, T, H, HD)
        Q = xh * q_bind
        K = xh * k_bind
        V = xh * v_bind
        scores = jnp.einsum('bthd,bshd->bhts', Q, K) * scale
        causal = jnp.tril(jnp.ones((T, T), dtype=bool))
        attn = jnp.where(causal, jax.nn.sigmoid(scores * 4.0), 0.0)
        out = jnp.einsum('bhts,bshd->bthd', attn, V)
        return out.reshape(B, T, D)

    def _L1_ffn_ref(x, route_w, A, Bw):
        import jax, jax.numpy as jnp
        import numpy as np
        R = 16
        LORA_ALPHA = 16
        SCALING = LORA_ALPHA / R
        logits = jnp.einsum('bsd,ed->bse', x, route_w)
        topk_v, topk_idx = jax.lax.top_k(logits, 1)
        E = logits.shape[-1]
        route_weight = jax.nn.one_hot(topk_idx[..., 0], E, dtype=logits.dtype) * topk_v
        h = jnp.einsum('bsd,erd->bser', x, A)
        wh = route_weight[..., None] * h
        out = jnp.einsum('bser,eor->bso', wh, Bw) * SCALING
        return out

    def _L2_attn_ref(x, A_log, D, x_proj_w, dt_proj_w, dt_proj_b):
        import jax, jax.numpy as jnp
        import numpy as np
        import math
        D_MODEL = 512
        D_STATE = 16
        EXPAND = 2
        D_INNER = D_MODEL * EXPAND
        DT_RANK = math.ceil(D_MODEL / 16)
        BATCH, SEQ_LEN = (2, 128)
        A = -jnp.exp(A_log)
        xp = jnp.einsum('bld,rd->blr', x, x_proj_w)
        dt_in = xp[..., :DT_RANK]
        B = xp[..., DT_RANK:DT_RANK + D_STATE]
        C = xp[..., DT_RANK + D_STATE:]
        dt = jax.nn.softplus(jnp.einsum('blr,dr->bld', dt_in, dt_proj_w) + dt_proj_b)
        dA = jnp.exp(dt[..., None] * A)
        dBx = dt[..., None] * B[:, :, None, :] * x[..., None]

        def step(h, inp):
            dA_t, dBx_t, C_t = inp
            h = dA_t * h + dBx_t
            y = jnp.einsum('bdn,bn->bd', h, C_t)
            return (h, y)
        h0 = jnp.zeros((x.shape[0], D_INNER, D_STATE), dtype=x.dtype)
        _, ys = jax.lax.scan(step, h0, (jnp.moveaxis(dA, 1, 0), jnp.moveaxis(dBx, 1, 0), jnp.moveaxis(C, 1, 0)))
        y = jnp.moveaxis(ys, 0, 1) + D * x
        return y

    def _L2_ffn_ref(x, W_base, b_base, enc0, enc1, coefs0, coefs1, mask0, mask1):
        import math
        import jax, jax.numpy as jnp
        import numpy as np
        SCALING = 16.0 / 32.0

        def real_fourier_orthogonal_multiply(c):
            n = c.shape[-1]
            sqrt_n = math.sqrt(n)
            pair_scale = math.sqrt(n / 2.0)
            max_f = (n - 1) // 2
            work = c.astype(jnp.float32)
            dc = (work[..., 0] * sqrt_n)[..., None].astype(jnp.complex64)
            cos = work[..., 1:1 + 2 * max_f:2] * pair_scale
            sin = work[..., 2:2 + 2 * max_f:2] * pair_scale
            mid = (cos - 1j * sin).astype(jnp.complex64)
            parts = [dc, mid]
            if n % 2 == 0:
                parts.append((work[..., -1] * sqrt_n)[..., None].astype(jnp.complex64))
            spectrum = jnp.concatenate(parts, axis=-1)
            return jnp.fft.irfft(spectrum, n=n, axis=-1).astype(c.dtype)
        base = jnp.einsum('bsd,od->bso', x, W_base) + b_base
        e0 = jnp.einsum('bsd,rd->bsr', x, enc0)
        e1 = jnp.einsum('bsd,rd->bsr', x, enc1)
        w0 = coefs0 * mask0.astype(coefs0.dtype)
        w1 = coefs1 * mask1.astype(coefs1.dtype)
        decoded = jnp.einsum('bsr,eor->ebso', e0, w0) + jnp.einsum('bsr,eor->ebso', e1, w1)
        transformed = real_fourier_orthogonal_multiply(decoded)
        update = transformed.sum(axis=0)
        return base + update * SCALING

    def _L3_attn_ref(x, wq, bq, wk, bk, wv, bv):
        import jax, jax.numpy as jnp
        import numpy as np
        EMBED = 1024
        H = 32
        KV = 8
        D = EMBED // H
        REP = H // KV

        def _rope(t, cos, sin):
            t = t.reshape(*t.shape[:-1], 2, D // 2)
            t1, t2 = (t[..., 0, :], t[..., 1, :])
            return jnp.concatenate([t1 * cos - t2 * sin, t1 * sin + t2 * cos], axis=-1)
        B, S, E = x.shape
        xq = (x @ wq + bq).reshape(B, S, H, D)
        xk = (x @ wk + bk).reshape(B, S, KV, D)
        xv = (x @ wv + bv).reshape(B, S, KV, D)
        inv_freq = 1.0 / 10000.0 ** (jnp.arange(0, D, 2, dtype=jnp.float32) / D)
        ang = jnp.arange(S, dtype=jnp.float32)[:, None] * inv_freq[None, :]
        cos, sin = (jnp.cos(ang)[:, None, :], jnp.sin(ang)[:, None, :])
        q = _rope(xq, cos, sin)
        k = _rope(xk, cos, sin)
        k = jnp.repeat(k, REP, axis=2)
        v = jnp.repeat(xv, REP, axis=2)
        scores = jnp.einsum('bqhd,bkhd->bhqk', q, k) / jnp.sqrt(jnp.float32(D))
        probs = jax.nn.softmax(scores.astype(jnp.float32), axis=-1)
        out = jnp.einsum('bhqk,bkhd->bqhd', probs, v).reshape(B, S, E)
        return out

    def _L3_ffn_ref(x, W_org, lora_down, lora_up, lora_keys, Wq):
        import jax, jax.numpy as jnp
        import numpy as np
        import math
        B, S, IN, OUT = (4, 512, 1024, 1024)
        E, R, K = (8, 64, 128)
        SCALE = 64.0 / 64.0
        MULTIPLIER = 1.0
        base = jnp.einsum('bsi,oi->bso', x, W_org)
        q = jnp.einsum('bi,ki->bk', x.mean(axis=1), Wq)
        scores = jnp.einsum('bk,ek->be', q, lora_keys) / math.sqrt(K)
        coeffs = jax.nn.softmax(scores, axis=-1)
        h = jnp.einsum('bsi,eir->bser', x, lora_down)
        delta = jnp.einsum('be,bser,ero->bso', coeffs, h, lora_up)
        return base + delta * (SCALE * MULTIPLIER)
    h = _L0_tok_ref(L0_tok_A_abslog, L0_tok_A_phase, x, 1024)
    h = jnp.concatenate([jnp.broadcast_to(cls_tok, (h.shape[0], 1, h.shape[2])), h], axis=1)
    h = h + _L0_attn_ref(_layernorm(h, axis=-1), L0_attn_qkv_w, L0_attn_qkv_b, L0_attn_out_w, L0_attn_out_b)
    h = h + _L0_ffn_ref(_layernorm(h, axis=-1), L0_ffn_W_base, L0_ffn_b_base, L0_ffn_W_router, L0_ffn_A_stack, L0_ffn_B_stack)
    h = h + _L1_attn_ref(_layernorm(h, axis=-1), L1_attn_bv_q, L1_attn_bv_k, L1_attn_bv_v)
    h = h + _L1_ffn_ref(_layernorm(h, axis=-1), L1_ffn_route_w, L1_ffn_A, L1_ffn_Bw)
    h = h + _L2_attn_ref(_layernorm(h, axis=-1), L2_attn_A_log, L2_attn_D, L2_attn_x_proj_w, L2_attn_dt_proj_w, L2_attn_dt_proj_b)
    h = h + _L2_ffn_ref(_layernorm(h, axis=-1), L2_ffn_W_base, L2_ffn_b_base, L2_ffn_enc0, L2_ffn_enc1, L2_ffn_coefs0, L2_ffn_coefs1, L2_ffn_mask0, L2_ffn_mask1)
    h = h + _L3_attn_ref(_layernorm(h, axis=-1), L3_attn_wq, L3_attn_bq, L3_attn_wk, L3_attn_bk, L3_attn_wv, L3_attn_bv)
    h = h + _L3_ffn_ref(_layernorm(h, axis=-1), L3_ffn_W_org, L3_ffn_lora_down, L3_ffn_lora_up, L3_ffn_lora_keys, L3_ffn_Wq)
    return h

_drawn_inputs = setup_inputs


def setup_inputs(seed=0):
    import zlib

    import numpy as np

    out = dict(_drawn_inputs(seed))
    spreads = {'L2_attn_D': (1.0, 0.2)}
    factors = {'L0_attn_qkv_b': 3.706,
     'L0_ffn_b_base': 8.0,
     'L1_attn_bv_q': 64.0,
     'L1_attn_bv_k': 33.013,
     'L2_attn_A_log': 3.728,
     'L2_attn_dt_proj_w': 5.426,
     'L2_ffn_b_base': 8.0,
     'L2_ffn_enc0': 4.027,
     'L2_ffn_enc1': 8.0,
     'L2_ffn_coefs0': 3.887,
     'L2_ffn_coefs1': 8.0,
     'L3_attn_wq': 3.24,
     'L3_attn_bq': 8.0,
     'L3_attn_wk': 2.765,
     'L3_attn_bk': 28.655,
     'L3_attn_bv': 8.0,
     'L3_ffn_lora_down': 5.095,
     'L3_ffn_lora_up': 5.103,
     'L3_ffn_lora_keys': 8.0,
     'L3_ffn_Wq': 8.0}
    for name, (base, spread) in spreads.items():
        noise = np.random.default_rng([zlib.crc32(name.encode()), seed]).standard_normal(out[name].shape)
        drawn = base * np.exp(spread * noise) if base else spread * noise
        out[name] = jnp.asarray(drawn.astype(out[name].dtype))
    for name, factor in factors.items():
        out[name] = (out[name] * factor).astype(out[name].dtype)
    return out
```

```python
from contextlib import ExitStack

import numpy as np

import concourse.bass as bass
from concourse import mybir

F32 = mybir.dt.float32
U8 = mybir.dt.uint8
ALU = mybir.AluOpType
ACT = mybir.ActivationFunctionType
AX = mybir.AxisListType

P = 128
IMAGES, GRID, STATES = 32, 64, 64
S = GRID + 1
D = 1024
KT = D // P
CB = 4
CT = CB * S
NC = IMAGES // CB
CW = KT * CT
HEADS, HD = 32, 32
EPS = 1e-5
EXPERTS, RANK = 8, 16
SSM, DTR = 16, 32
ENC = 40
MIXR = 64
KEYS = 128
HDH = 4
LAYERS = 8

MAGIC = 12582912.0
TWO_PI = 6.283185307179586
PI_HEAD = 6.28125
PI_MID = 0.0019350051879882812
PI_TAIL = TWO_PI - PI_HEAD - PI_MID
SIN_MAX = 3.1415925
TOK_ANG1, TOK_ANG2, N_TOK_V = 7, 46, 76


class Steps:

    def __init__(self, sem):
        self.sem, self.base, self.names, self.here = sem, 0, [], 0

    def layer(self, names, rounds=NC):
        self.names, self.rounds, self.here = list(names), rounds, 0
        assert len(set(self.names)) == len(self.names)

    def at(self, name, c=0):
        return c * len(self.names) + (self.base + self.names.index(name) + 1)

    def prev(self, name, c):
        return c * len(self.names) + (self.base + self.names.index(name) + 1 - len(self.names))

    def own(self, c=0):
        return c * len(self.names) + (self.base + self.here)

    def done(self, name):
        assert self.names[self.here] == name, (self.names[self.here], name)
        self.here += 1
        return self.sem

    def close(self):
        assert self.here == len(self.names), (self.here, self.names)
        self.base += self.rounds * len(self.names)
        self.names, self.here = [], 0


def constant_table():
    parts, at = [], {}

    def put(name, a):
        a = np.asarray(a, np.float32)
        full = np.zeros((P, a.shape[1]), np.float32)
        full[:a.shape[0]] = a
        at[name] = (sum(p.shape[1] for p in parts), a.shape[1])
        parts.append(full)

    p = np.arange(P)
    put("ident", np.eye(P))
    put("mean", np.full((P, P), 1.0 / D))
    rot = np.zeros((P, P))
    for i in range(P):
        if i % HD < HD // 2:
            rot[i + HD // 2, i] = -1.0
        else:
            rot[i - HD // 2, i] = 1.0
    put("rotate", rot)
    half = HD // 2
    freq = (1.0 / np.float32(10000.0) ** (np.arange(half, dtype=np.float32) / half)).astype(np.float32)
    angle = (np.arange(S, dtype=np.float32)[None, :] * freq[p % half][:, None]).astype(np.float64)
    scale = 1.0 / np.sqrt(HD)
    put("cos_k", np.cos(angle))
    put("sin_k", np.sin(angle))
    put("cos_q", np.cos(angle) * scale)
    put("sin_q", np.sin(angle) * scale)
    s = np.arange(S)
    put("causal", np.where(s[None, :] > s[:, None], -66504.0, 0.0))
    put("causal_t", s[:, None] <= s[None, :])
    e = np.arange(EXPERTS)
    put("earlier", np.tile((e[None, :] < e[:, None]).reshape(1, -1), (P, 1)))
    put("spread2", (e[:, None] == (p // RANK)[None, :]) * 2.0)
    put("spread1", e[:, None] == (p // RANK)[None, :])
    for j in range(EXPERTS * MIXR // P):
        put(f"mix{j}", e[:, None] == (p // MIXR + j * (P // MIXR))[None, :])
    put("upper", (p < STATES)[:, None])
    put("lower", (p >= STATES)[:, None])
    put("shift", np.where(p < STATES, np.pi / 2, 0.0)[:, None])
    put("turn", np.where(p < STATES, 0.25, 0.0)[:, None])
    put("eps", np.full((P, 1), EPS))
    put("count", np.tile(np.arange(P), (P, 1)))
    return np.concatenate(parts, 1), at


CONST, CONST_AT = constant_table()

H_AT = 0
C_AT = H_AT + NC * CW
B_AT = C_AT + CONST.shape[1]
BIAS_NAMES = dict(qkv_b=24, out_b=8, base0_b=8, dt_b=8, skip=8, base2_b=8, q_b=8, k_b=2, v_b=2, cls=8)
BIAS_AT, _n = {}, 0
for _k, _v in BIAS_NAMES.items():
    BIAS_AT[_k] = (_n, _v)
    _n += _v
BIAS_W = _n
BIND_AT = B_AT + BIAS_W
LN_AT = BIND_AT + 24
W_AT = LN_AT + 5 * CT + 2 * CW
WORDS = 57040
STOP_AFTER = LAYERS


def rope_names(tiles):
    return [f"{x}{m}" for m in tiles for x in ("rs", "rr")]


def build(nc, T):
    ctx = ExitStack()
    with ctx:
        A = ctx.enter_context(nc.sbuf_tensor("arena", [P, WORDS], F32))
        PS = ctx.enter_context(nc.psum_tensor("banks", [P, 8, 512], F32))
        hD = nc.dram_tensor("h_scratch", (NC, P, CW), F32, kind="Internal").ap()
        bcD = nc.dram_tensor("bc_scratch", (2 * SSM, CT), F32, kind="Internal").ap()

        def sem(name):
            return ctx.enter_context(nc.semaphore(name))

        V = Steps(sem("vector_steps"))
        AC = Steps(sem("scalar_steps"))
        G = Steps(sem("gpsimd_steps"))
        PE = Steps(sem("tensor_steps"))
        LV = Steps(sem("layernorm_vector_steps"))
        LA = Steps(sem("layernorm_scalar_steps"))
        LP = Steps(sem("layernorm_tensor_steps"))
        ln_rounds = 1 + LAYERS * NC
        LV.layer(["sum", "center", "sumsq", "n1", "n2", "n3", "out"], ln_rounds)
        LA.layer(["square", "log", "seed"], ln_rounds)
        LP.layer(["mean", "var"], ln_rounds)
        consts_in = sem("constants_loaded")
        tok_in = sem("token_inputs_loaded")
        w_early = sem("qk_weights_loaded")
        h_out = sem("h_stored")
        h_in = sem("h_loaded")
        w_in = [sem(f"weights_loaded_{i}") for i in range(LAYERS)]
        h_back = sem("h_back_loaded")
        bc_out = sem("bc_stored")
        bc_in = sem("bc_loaded")
        out_done = sem("output_stored")

        def const(name, rows=P):
            o, w = CONST_AT[name]
            return A[0:rows, C_AT + o:C_AT + o + w]

        def bias(name, i):
            o = B_AT + BIAS_AT[name][0] + i
            return A[:, o:o + 1]

        def words(at, *shape, rows=P):
            n = int(np.prod(shape))
            v = A[0:rows, at:at + n]
            if len(shape) == 2:
                return v.rearrange("p (a b) -> p a b", a=shape[0])
            if len(shape) == 3:
                return v.rearrange("p (a b c) -> p a b c", a=shape[0], b=shape[1])
            return v

        ident, mean_w = const("ident"), const("mean")

        s1 = words(LN_AT, CT)
        s2 = words(LN_AT + CT, CT)
        lv = words(LN_AT + 2 * CT, CT)
        rs = words(LN_AT + 3 * CT, CT)
        nt = words(LN_AT + 4 * CT, CT)
        xc_at = LN_AT + 5 * CT
        xn_at = xc_at + CW
        xc = words(xc_at, KT, CT)
        xn = words(xn_at, KT, CT)
        mean_ps = PS[:, 0, 0:CT]

        def over_tiles(ap2):
            return ap2.unsqueeze(1).broadcast_to([P, KT, CT])

        def h_chunk(c):
            return A[:, bass.ds(c * CW, CW)].rearrange("p (k t) -> p k t", k=KT)

        def h_tile(c, m):
            return A[:, bass.ds(c * CW + m * CT, CT)]

        def ln_v1(v, n, src):
            LV.here = 0
            if not (isinstance(n, int) and n == 0):
                v.wait_ge(LP.sem, LP.at("var", n) - 2)
            v.tensor_reduce(s1, src.rearrange("p k t -> p t k"), AX.X, ALU.add).then_inc(LV.done("sum"), 1)

        def ln_v2(v, n, src):
            v.wait_ge(LP.sem, LP.at("mean", n))
            v.tensor_tensor(xc, src, over_tiles(mean_ps), ALU.subtract).then_inc(LV.done("center"), 1)

        def ln_v3(v, n, sq):
            v.wait_ge(LA.sem, LA.at("square", n))
            v.tensor_reduce(s2, sq.rearrange("p k t -> p t k"), AX.X, ALU.add).then_inc(LV.done("sumsq"), 1)

        def ln_v4(v, n):
            v.wait_ge(LA.sem, LA.at("seed", n))
            v.scalar_tensor_tensor(out=nt, in0=mean_ps, scalar=EPS, in1=rs, op0=ALU.add, op1=ALU.mult
                                   ).then_inc(LV.done("n1"), 1)
            v.wait_ge(LV.sem, LV.own(n))
            v.scalar_tensor_tensor(out=nt, in0=nt, scalar=-0.5, in1=rs, op0=ALU.mult, op1=ALU.mult
                                   ).then_inc(LV.done("n2"), 1)
            v.wait_ge(LV.sem, LV.own(n))
            v.scalar_tensor_tensor(out=rs, in0=nt, scalar=1.5, in1=rs, op0=ALU.add, op1=ALU.mult
                                   ).then_inc(LV.done("n3"), 1)

        def ln_v5(v, n, read=()):
            for s, at in read:
                v.wait_ge(s, at)
            v.wait_ge(LV.sem, LV.own(n))
            v.tensor_tensor(xn, xc, over_tiles(rs), ALU.mult).then_inc(LV.done("out"), 1)

        def ln_a1(a, n, sq):
            LA.here = 0
            a.wait_ge(LV.sem, LV.at("center", n))
            a.activation(sq, xc, ACT.Square).then_inc(LA.done("square"), 1)

        def ln_a2(a, n):
            a.wait_ge(LP.sem, LP.at("var", n))
            a.activation(lv, mean_ps, ACT.Ln, bias=const("eps")).then_inc(LA.done("log"), 1)
            a.wait_ge(LA.sem, LA.own(n))
            a.wait_ge(LV.sem, LV.at("center", n))
            a.activation(rs, lv, ACT.Exp, scale=-0.5).then_inc(LA.done("seed"), 1)

        def ln_p1(pe, n):
            LP.here = 0
            pe.wait_ge(LV.sem, LV.at("sum", n))
            pe.matmul(mean_ps, mean_w, s1, start=True, stop=True).then_inc(LP.done("mean"), 1)

        def ln_p2(pe, n):
            pe.wait_ge(LV.sem, LV.at("sumsq", n))
            pe.matmul(mean_ps, mean_w, s2, start=True, stop=True).then_inc(LP.done("var"), 1)

        def gemm(pe, out, w_of, kts, first=True, last=True, x=xn):
            for i, k in enumerate(kts):
                mm = pe.matmul(out, w_of(k), x[:, k, :], start=first and i == 0,
                               stop=last and i == len(kts) - 1)
            return mm


        def own(e, steps, c=0):
            e.wait_ge(steps.sem, steps.own(c))

        TOK = xc_at
        NA = D // P
        e1 = words(TOK, GRID, P)
        ang = words(TOK + 8192, GRID, P)
        kk = words(TOK + 16384, GRID, P)
        al, th = words(TOK + 24576, GRID), words(TOK + 24640, GRID)
        cr = words(TOK + 24704, GRID, IMAGES)
        ci = words(TOK + 26752, GRID, IMAGES)
        small = [words(TOK + 28800 + 512 * i, GRID, NA) for i in range(10)]
        col = [words(TOK + 33920 + GRID * i, GRID) for i in range(9)]
        assert TOK + 33920 + 9 * GRID <= WORDS
        HG = 8
        g_re = [words(TOK + 8192 + i * 2048, HG, IMAGES, NA) for i in range(2)]
        g_im = [words(TOK + 8192 + (2 + i) * 2048, HG, IMAGES, NA) for i in range(2)]
        hT = words(H_AT, NC, KT, CT)
        zero = words(LN_AT, 8)

        V.layer([f"v{i}" for i in range(N_TOK_V)] + [f"{x}{i}" for i in range(GRID // HG) for x in ("gre", "g")]
                + ["cls"], 1)
        AC.layer(["sin1", "exp1", "sin2r", "sin2i", "sinA", "cosA", "exp2", "expA"]
                 + [f"put{i}" for i in range(GRID)], 1)
        G.layer(["scaled", "e1"] + [f"gim{i}" for i in range(GRID // HG)], 1)
        PE.layer([f"tok{i}" for i in range(GRID)], 1)

        with nc.Block() as block:
            @block.sync
            def _(sp):
                sp.dma_start(A[:, C_AT:C_AT + CONST.shape[1]], T["const"]).then_inc(consts_in, 16)
                for name, (o, w) in BIAS_AT.items():
                    sp.dma_start(A[:, B_AT + o:B_AT + o + w], T[name]).then_inc(consts_in, 16)
                for ap, name in ((al, "abslog"), (th, "phase")):
                    sp.dma_start(ap, T[name]).then_inc(tok_in, 16)
                for ap, name in ((cr, "x_re"), (ci, "x_im")):
                    sp.dma_start(ap, T[name].rearrange("p (a b) -> p a b", a=GRID)).then_inc(tok_in, 16)

            @block.vector
            def _(v):
                n = [0]

                def step(make):
                    own(v, V)
                    make().then_inc(V.done(f"v{n[0]}"), 1)
                    n[0] += 1

                def reduce_angle(x, k, turn, shift):
                    step(lambda: v.tensor_scalar(k, x, 1.0 / TWO_PI, turn, ALU.mult, ALU.add))
                    step(lambda: v.tensor_scalar(k, k, MAGIC, MAGIC, ALU.add, ALU.subtract))
                    for part in (PI_HEAD, PI_MID, PI_TAIL):
                        step(lambda: v.scalar_tensor_tensor(out=x, in0=k, scalar=-part, in1=x,
                                                            op0=ALU.mult, op1=ALU.add))
                    step(lambda: v.tensor_scalar(x, x, shift, SIN_MAX, ALU.add, ALU.min))
                    step(lambda: v.tensor_scalar(x, x, -SIN_MAX, None, ALU.max))

                v.wait_ge(consts_in, 16 * (1 + len(BIAS_AT)))
                v.wait_ge(tok_in, 16 * 4)
                parts = const("count").unsqueeze(1).broadcast_to([P, GRID, P])
                blocks = const("count")[:, 0:NA].unsqueeze(1).broadcast_to([P, GRID, NA])
                wide = lambda x, w: x.unsqueeze(2).broadcast_to([P, GRID, w])
                v.tensor_tensor(ang, wide(th, P), parts, ALU.mult).then_inc(V.done("v0"), 1)
                n[0] = 1
                reduce_angle(ang, kk, const("turn"), const("shift"))
                i_ang = n[0]
                t128, k128, a2, k2, a2c, m2, cosA, sinA, x2, y2 = small
                step(lambda: v.tensor_scalar(col[0], th, 128.0, None, ALU.mult))
                step(lambda: v.tensor_scalar(col[1], col[0], 1.0 / TWO_PI, None, ALU.mult))
                step(lambda: v.tensor_scalar(col[1], col[1], MAGIC, MAGIC, ALU.add, ALU.subtract))
                for part in (PI_HEAD, PI_MID, PI_TAIL):
                    step(lambda: v.scalar_tensor_tensor(out=col[0], in0=col[1], scalar=-part, in1=col[0],
                                                        op0=ALU.mult, op1=ALU.add))
                step(lambda: v.tensor_tensor(a2, wide(col[0], NA), blocks, ALU.mult))
                step(lambda: v.tensor_copy(a2c, a2))
                reduce_angle(a2, k2, 0.0, 0.0)
                reduce_angle(a2c, k2, 0.25, np.pi / 2)
                step(lambda: v.tensor_tensor(m2, wide(al, NA), blocks, ALU.mult))
                step(lambda: v.tensor_copy(col[2], th))
                step(lambda: v.tensor_copy(col[3], th))
                sub = [x.unsqueeze(2) for x in (col[2], col[3], col[4])]
                reduce_angle(sub[0], sub[2], 0.0, 0.0)
                reduce_angle(sub[1], sub[2], 0.25, np.pi / 2)
                assert (i_ang - 1, n[0] - 1) == (TOK_ANG1, TOK_ANG2), (i_ang, n[0])
                v.wait_ge(AC.sem, AC.at("expA"))
                sA, cA, eA = col[5], col[6], col[7]
                step(lambda: v.tensor_tensor(sA, sA, eA, ALU.mult))
                step(lambda: v.tensor_tensor(cA, cA, eA, ALU.mult))
                step(lambda: v.tensor_scalar(cA, cA, 1.0, None, ALU.subtract))
                step(lambda: v.tensor_tensor(col[0], al, al, ALU.mult))
                step(lambda: v.tensor_tensor(col[1], th, th, ALU.mult))
                step(lambda: v.tensor_tensor(col[0], col[0], col[1], ALU.add))
                step(lambda: v.reciprocal(col[0], col[0]))
                fr, fi = col[2], col[3]
                step(lambda: v.tensor_tensor(fr, cA, al, ALU.mult))
                step(lambda: v.tensor_tensor(col[1], sA, th, ALU.mult))
                step(lambda: v.tensor_tensor(fr, fr, col[1], ALU.add))
                step(lambda: v.tensor_tensor(fr, fr, col[0], ALU.mult))
                step(lambda: v.tensor_tensor(fi, sA, al, ALU.mult))
                step(lambda: v.tensor_tensor(col[1], cA, th, ALU.mult))
                step(lambda: v.tensor_tensor(fi, fi, col[1], ALU.subtract))
                step(lambda: v.tensor_tensor(fi, fi, col[0], ALU.mult))
                step(lambda: v.tensor_tensor(cosA, cosA, m2, ALU.mult))
                step(lambda: v.tensor_tensor(sinA, sinA, m2, ALU.mult))
                step(lambda: v.tensor_tensor(x2, cosA, wide(fr, NA), ALU.mult))
                step(lambda: v.tensor_tensor(k2, sinA, wide(fi, NA), ALU.mult))
                step(lambda: v.tensor_tensor(x2, x2, k2, ALU.subtract))
                step(lambda: v.tensor_tensor(y2, sinA, wide(fr, NA), ALU.mult))
                step(lambda: v.tensor_tensor(k2, cosA, wide(fi, NA), ALU.mult))
                step(lambda: v.tensor_tensor(y2, y2, k2, ALU.add))
                u_re, u_im = a2, a2c
                step(lambda: v.tensor_scalar(u_re, x2, const("upper"), 2.0, ALU.mult, ALU.mult))
                step(lambda: v.tensor_scalar(k2, y2, const("lower"), -2.0, ALU.mult, ALU.mult))
                step(lambda: v.tensor_tensor(u_re, u_re, k2, ALU.add))
                step(lambda: v.tensor_scalar(u_im, y2, const("upper"), -2.0, ALU.mult, ALU.mult))
                step(lambda: v.tensor_scalar(k2, x2, const("lower"), -2.0, ALU.mult, ALU.mult))
                step(lambda: v.tensor_tensor(u_im, u_im, k2, ALU.add))
                assert n[0] == N_TOK_V, n[0]
                for i in range(GRID // HG):
                    if i == 0:
                        v.wait_ge(G.sem, G.at("e1"))
                    else:
                        own(v, V)
                    if i >= 2:
                        v.wait_ge(PE.sem, PE.at(f"tok{HG * (i - 1) - 1}"))
                    v.tensor_tensor(g_re[i % 2], cr[:, HG * i:HG * i + HG, :].unsqueeze(3).broadcast_to([P, HG, IMAGES, NA]),
                                    u_re[:, HG * i:HG * i + HG, :].unsqueeze(2).broadcast_to([P, HG, IMAGES, NA]),
                                    ALU.mult).then_inc(V.done(f"gre{i}"), 1)
                    own(v, V)
                    v.wait_ge(G.sem, G.at(f"gim{i}"))
                    v.tensor_tensor(g_re[i % 2], g_re[i % 2], g_im[i % 2], ALU.add).then_inc(V.done(f"g{i}"), 1)
                first = hT.rearrange("p c k (b s) -> p c k b s", b=CB)[:, :, :, :, 0]
                own(v, V)
                v.tensor_copy(first.rearrange("p c k b -> p k c b"),
                              A[:, B_AT + BIAS_AT["cls"][0]:B_AT + BIAS_AT["cls"][0] + KT].unsqueeze(2).unsqueeze(3)
                              .broadcast_to([P, KT, NC, CB])).then_inc(V.done("cls"), 1)

            @block.gpsimd
            def _(g):
                g.wait_ge(consts_in, 16 * (1 + len(BIAS_AT)))
                g.wait_ge(tok_in, 16 * 4)
                g.wait_ge(V.sem, V.at(f"v{TOK_ANG1}"))
                g.tensor_tensor(kk, al.unsqueeze(2).broadcast_to([P, GRID, P]),
                                const("count").unsqueeze(1).broadcast_to([P, GRID, P]),
                                ALU.mult).then_inc(G.done("scaled"), 1)
                g.wait_ge(AC.sem, AC.at("exp1"))
                g.tensor_tensor(e1, kk, ang, ALU.mult).then_inc(G.done("e1"), 1)
                g.wait_ge(G.sem, G.own())
                for i in range(GRID // HG):
                    if i == 0:
                        g.wait_ge(V.sem, V.at(f"v{N_TOK_V - 1}"))
                    if i >= 2:
                        g.wait_ge(V.sem, V.at(f"g{i - 2}"))
                    g.tensor_tensor(g_im[i % 2], ci[:, HG * i:HG * i + HG, :].unsqueeze(3).broadcast_to([P, HG, IMAGES, NA]),
                                    small[4][:, HG * i:HG * i + HG, :].unsqueeze(2).broadcast_to([P, HG, IMAGES, NA]),
                                    ALU.mult).then_inc(G.done(f"gim{i}"), 1)

            @block.scalar
            def _(a):
                t128, k128, a2, k2, a2c, m2, cosA, sinA, x2, y2 = small
                a.wait_ge(V.sem, V.at(f"v{TOK_ANG1}"))
                a.activation(ang, ang, ACT.Sin).then_inc(AC.done("sin1"), 1)
                a.wait_ge(G.sem, G.at("scaled"))
                a.activation(kk, kk, ACT.Exp).then_inc(AC.done("exp1"), 1)
                a.wait_ge(V.sem, V.at(f"v{TOK_ANG2}"))
                a.activation(sinA, a2, ACT.Sin).then_inc(AC.done("sin2r"), 1)
                a.activation(cosA, a2c, ACT.Sin).then_inc(AC.done("sin2i"), 1)
                a.activation(col[5], col[2], ACT.Sin).then_inc(AC.done("sinA"), 1)
                a.activation(col[6], col[3], ACT.Sin).then_inc(AC.done("cosA"), 1)
                a.activation(m2, m2, ACT.Exp, scale=128.0).then_inc(AC.done("exp2"), 1)
                a.activation(col[7], al, ACT.Exp).then_inc(AC.done("expA"), 1)
                for hh in range(GRID):
                    a.wait_ge(PE.sem, PE.at(f"tok{hh}"))
                    dst = hT.rearrange("p c k (b s) -> p c k b s", b=CB)[:, :, :, :, 1 + hh]
                    a.activation(dst.rearrange("p c k b -> p c b k"),
                                 PS[:, hh % 8, 0:IMAGES * NA].rearrange("p (c b k) -> p c b k", c=NC, b=CB),
                                 ACT.Copy).then_inc(AC.done(f"put{hh}"), 1)

            @block.tensor
            def _(pe):
                pe.wait_ge(G.sem, G.at("e1"))
                for hh in range(GRID):
                    if hh % HG == 0:
                        pe.wait_ge(V.sem, V.at(f"g{hh // HG}"))
                    if hh >= 8:
                        pe.wait_ge(AC.sem, AC.at(f"put{hh - 8}"))
                    pe.matmul(PS[:, hh % 8, 0:IMAGES * NA], e1[:, hh, :],
                              g_re[hh // HG % 2][:, hh % HG].rearrange("p b k -> p (b k)"), start=True, stop=True
                              ).then_inc(PE.done(f"tok{hh}"), 1)

        for t in (V, AC, G, PE):
            t.close()

        def finish(extra=()):
            with nc.Block() as block:
                @block.sync
                def _(sp):
                    for s, at in extra:
                        sp.wait_ge(s, at)
                    sp.dma_start(T["out"].rearrange("c p w -> p c w"),
                                 A[:, 0:NC * CW].rearrange("p (c w) -> p c w", c=NC)).then_inc(out_done, 16)
                    sp.wait_ge(out_done, 16)

        if STOP_AFTER == 0:
            return finish()

        GROUPS = 2 * CB
        GH, QT = HEADS // 2, 4
        qT = words(W_AT + 2 * KT * D, KT, CT)
        kT = words(W_AT + 2 * KT * D + CW, KT, CT)
        vT_at = W_AT + 2 * KT * D + 2 * CW
        vT = words(vT_at, KT, CT)
        hbuf_at = vT_at + CW
        hbuf = words(hbuf_at, KT, CT)
        sq = words(hbuf_at + CW, KT, CT)
        vb_at = hbuf_at + 2 * CW
        s_at = vb_at + 2 * D
        pt_at = s_at + 2 * GH * S
        pt_buf = [words(pt_at + i * QT * S, QT * S, rows=S) for i in range(2)]
        rt_at = pt_at + 2 * QT * S
        turned = [words(rt_at + i * CT, CT) for i in range(4)]
        SB = 3
        s_buf = [words((s_at, s_at + GH * S, rt_at)[i], QT, QT, S, rows=S) for i in range(SB)]
        mx = [words(rt_at + 4 * CT + 16 * i, GH, rows=S) for i in range(SB)]
        rsum = [words(rt_at + 4 * CT + 16 * (SB + i), GH, rows=S) for i in range(SB)]
        assert GH * S <= 4 * CT and rt_at + 4 * CT + 32 * SB <= WORDS
        s_ps = PS[0:S, 1:5, 0:QT * S].rearrange("p j (m k) -> p j m k", m=QT)

        def heads16(x):
            return x.rearrange("p (j m) -> p j m", j=QT).unsqueeze(3).broadcast_to([S, QT, QT, S])

        def rope_v(v, c, m, x):
            v.wait_ge(PE.sem, PE.at(f"rot{m}", c))
            sin = const("sin_q" if m < KT else "sin_k")
            v.tensor_tensor(turned[2 + m % 2].rearrange("p (b s) -> p b s", b=CB),
                            PS[:, 5 + m % 2, 0:CT].rearrange("p (b s) -> p b s", b=CB),
                            sin.unsqueeze(1).broadcast_to([P, CB, S]), ALU.mult).then_inc(V.done(f"rs{m}"), 1)
            own(v, V, c)
            v.wait_ge(G.sem, G.at(f"rc{m}", c))
            v.tensor_tensor(x, turned[m % 2], turned[2 + m % 2], ALU.add).then_inc(V.done(f"rr{m}"), 1)

        def rope_g(g, c, m, x):
            g.wait_ge(AC.sem, AC.at(f"ev{m}", c))
            if m >= 2:
                g.wait_ge(V.sem, V.at(f"rr{m - 2}", c))
            cos = const("cos_q" if m < KT else "cos_k")
            g.tensor_tensor(turned[m % 2].rearrange("p (b s) -> p b s", b=CB),
                            x.rearrange("p (b s) -> p b s", b=CB),
                            cos.unsqueeze(1).broadcast_to([P, CB, S]), ALU.mult).then_inc(G.done(f"rc{m}"), 1)

        def rope_p(pe, c, m, x):
            pe.wait_ge(AC.sem, AC.at(f"ev{m}", c))
            if m >= 2:
                pe.wait_ge(V.sem, V.at(f"rs{m - 2}", c))
            pe.matmul(PS[:, 5 + m % 2, 0:CT], const("rotate"), x, start=True, stop=True).then_inc(PE.done(f"rot{m}"), 1)

        def soft_top(v, c, g, causal):
            v.wait_ge(PE.sem, PE.at(f"S{g}", c))
            if g >= SB:
                v.wait_ge(PE.sem, PE.at(f"P{g - SB}_3", c))
            if causal:
                v.tensor_tensor(s_buf[g % SB], s_ps,
                                const("causal", S).unsqueeze(1).unsqueeze(1).broadcast_to([S, QT, QT, S]),
                                ALU.add).then_inc(V.done(f"mask{g}"), 1)
                own(v, V, c)
                v.tensor_reduce(mx[g % SB], s_buf[g % SB], AX.X, ALU.max).then_inc(V.done(f"max{g}"), 1)
            else:
                v.tensor_reduce(mx[g % SB], s_ps, AX.X, ALU.max).then_inc(V.done(f"max{g}"), 1)
                own(v, V, c)
                v.tensor_tensor(s_buf[g % SB], s_ps, heads16(mx[g % SB]), ALU.subtract).then_inc(V.done(f"mask{g}"), 1)

        def soft_sum(v, c, g):
            v.wait_ge(AC.sem, AC.at(f"exp{g}", c))
            v.tensor_reduce(rsum[g % SB], s_buf[g % SB], AX.X, ALU.add).then_inc(V.done(f"sum{g}"), 1)
            own(v, V, c)
            v.reciprocal(rsum[g % SB], rsum[g % SB]).then_inc(V.done(f"rcp{g}"), 1)

        def soft_shift(gp, c, g):
            gp.wait_ge(V.sem, V.at(f"max{g}", c))
            gp.tensor_tensor(s_buf[g % SB], s_buf[g % SB], heads16(mx[g % SB]), ALU.subtract
                             ).then_inc(G.done(f"shift{g}"), 1)

        def soft_norm(gp, c, g):
            gp.wait_ge(V.sem, V.at(f"rcp{g}", c))
            gp.tensor_tensor(s_buf[g % SB], s_buf[g % SB], heads16(rsum[g % SB]), ALU.mult
                             ).then_inc(G.done(f"norm{g}"), 1)

        def soft_exp(a, c, g, causal):
            if causal:
                a.wait_ge(G.sem, G.at(f"shift{g}", c))
            else:
                a.wait_ge(V.sem, V.at(f"mask{g}", c))
            a.activation(s_buf[g % SB], s_buf[g % SB], ACT.Exp).then_inc(AC.done(f"exp{g}"), 1)

        LAG = 2

        def probs_names(i):
            pts = [f"pt{i - LAG}_{u}" for u in range(QT)] if i >= LAG else []
            return pts[:3] + ([f"exp{i}"] if i < GROUPS else []) + pts[3:]

        def probs_a(a, c, i, causal):
            g = i - LAG
            for u in range(QT):
                if u == 3 and i < GROUPS:
                    soft_exp(a, c, i, causal)
                if g < 0:
                    continue
                a.wait_ge(PE.sem, PE.at(f"P{g}_{u}", c))
                if u < 2 and g > 0:
                    a.wait_ge(PE.sem, PE.at(f"O{g - 1}", c))
                if u >= 2:
                    a.wait_ge(PE.sem, PE.at(f"O{g}_{u - 2}", c))
                a.activation(pt_buf[u % 2], PS[0:S, 5 + u % 2, 0:QT * S], ACT.Copy).then_inc(AC.done(f"pt{g}_{u}"), 1)

        def scores_p(pe, c, g, half_k):
            b, half = g // 2, g % 2
            if g > 0:
                pe.wait_ge(V.sem, V.at(f"mask{g - 1}", c))
            for u in range(QT):
                for j in range(4):
                    t = half * QT + u
                    k = half if half_k else t
                    rows = slice(32 * j, 32 * j + 32)
                    mm = pe.matmul(PS[0:S, 1 + j, u * S:(u + 1) * S], qT[rows, t, b * S:(b + 1) * S],
                                   kT[rows, k, b * S:(b + 1) * S], start=True, stop=True)
            mm.then_inc(PE.done(f"S{g}"), 1)

        def values_p(pe, c, g, v_of, out_of, free_sem, free_at, bank_waits):
            pe.wait_ge(G.sem, G.at(f"norm{g}", c))

            def product(u):
                pe.wait_ge(AC.sem, AC.at(f"pt{g}_{u}", c))
                if u == 0 and free_at is not None:
                    pe.wait_ge(free_sem, free_at)
                for j in range(4):
                    mm = pe.matmul(out_of(u, j), v_of(u, j), pt_buf[u % 2][:, j * S:(j + 1) * S],
                                   start=True, stop=True)
                mm.then_inc(PE.done(f"O{g}_{u}" if u < 3 else f"O{g}"), 1)

            for u in range(QT):
                if u < 2:
                    for s, at in bank_waits(u):
                        pe.wait_ge(s, at)
                else:
                    pe.wait_ge(AC.sem, AC.at(f"pt{g}_{u - 2}", c))
                for j in range(4):
                    mm = pe.transpose(PS[0:S, 5 + u % 2, j * S:(j + 1) * S], s_buf[g % SB][:, j, u, :],
                                      const("ident", S)[:, 0:S])
                mm.then_inc(PE.done(f"P{g}_{u}"), 1)
                if u > 0:
                    product(u - 1)
            product(3)

        def value_names(g):
            return [f"P{g}_0", f"P{g}_1", f"O{g}_0", f"P{g}_2", f"O{g}_1", f"P{g}_3", f"O{g}_2", f"O{g}"]

        w_qk = words(H_AT, KT, 2 * D)
        w_v = words(W_AT, KT, D)
        w_out = words(W_AT + KT * D, KT, D)
        ctxT = vT
        v_tok = [words(vb_at + i * D, D, rows=S) for i in range(2)]
        NQ = 3 * KT

        V.layer([f"{x}{m}" for m in range(2 * KT) for x in ("rs", "rr")]
                + [x for g in range(GROUPS + 1) for x in
                   ([f"sum{g - 1}", f"rcp{g - 1}"] if g else []) + ([f"mask{g}", f"max{g}"] if g < GROUPS else [])]
                + [f"res{m}" for m in range(KT)])
        AC.layer([f"ev{m}" for m in range(NQ)] + [x for g in range(GROUPS + LAG) for x in
                 ([f"vt{g // 2}"] if g % 2 == 0 and g < GROUPS else []) + probs_names(g)
                 + ([f"ctx{g - LAG}"] if g >= LAG else [])])
        G.layer([f"rc{m}" for m in range(2 * KT)] + [x for g in range(GROUPS + 1) for x in
                ([f"norm{g - 1}"] if g else []) + ([f"shift{g}"] if g < GROUPS else [])])
        pe_names = []
        for m in range(NQ + 2):
            pe_names += ([f"qkv{m}"] if m < NQ else []) + ([f"rot{m - 2}"] if 2 <= m < 2 * KT + 2 else [])
        for g in range(GROUPS + LAG):
            pe_names += [f"Vt{g // 2}"] if g % 2 == 0 and g < GROUPS else []
            pe_names += [f"S{g}"] if g < GROUPS else []
            pe_names += value_names(g - LAG) if g >= LAG else []
        PE.layer(pe_names + [f"proj{m}" for m in range(KT)])

        with nc.Block() as block:
            @block.sync
            def _(sp):
                sp.dma_start(hD.rearrange("c p w -> p c w"),
                             A[:, 0:NC * CW].rearrange("p (c w) -> p c w", c=NC)).then_inc(h_out, 16)
                w3 = T["qkv_w"].rearrange("p (k n) -> p k n", k=KT)
                sp.dma_start(w_v, w3[:, :, 2 * D:]).then_inc(w_in[0], 16)
                sp.dma_start(w_out, T["out_w"].rearrange("p (k n) -> p k n", k=KT)).then_inc(w_in[0], 16)
                sp.wait_ge(h_out, 16)
                sp.dma_start(hbuf, hD[0].rearrange("p (k t) -> p k t", k=KT)).then_inc(h_in, 16)
                sp.dma_start(w_qk, w3[:, :, 0:2 * D]).then_inc(w_in[0], 16)
                sp.wait_ge(LV.sem, LV.at("center", 0))
                sp.wait_ge(h_in, 16)
                sp.dma_start(hbuf, hD[1].rearrange("p (k t) -> p k t", k=KT)).then_inc(h_in, 16)
                def turn(c, after_next):
                    sp.wait_ge(LV.sem, LV.at("center", c + 1))
                    sp.wait_ge(h_in, c * 32 + 32)
                    sp.dma_start(hbuf, hD[bass.ds(c, 1)].rearrange("c p (k t) -> p (c k) t", k=KT)
                                 ).then_inc(h_in, 16)
                    sp.wait_ge(V.sem, V.at("res7", c))
                    sp.dma_start(hD[bass.ds(c, 1)].rearrange("c p (k t) -> p (c k) t", k=KT), hbuf
                                 ).then_inc(h_out, 16)
                    sp.wait_ge(h_out, c * 16 + 32)
                    if after_next is not None:
                        sp.dma_start(hbuf, hD[bass.ds(after_next, 1)].rearrange("c p (k t) -> p (c k) t", k=KT)
                                     ).then_inc(h_in, 16)

                with sp.Fori(0, NC - 2) as c:
                    turn(c, c + 2)
                turn(NC - 2, 0)
                turn(NC - 1, None)
                sp.wait_ge(PE.sem, PE.at("qkv23", NC - 1))
                sp.dma_start(A[:, 0:NC * CW].rearrange("p (c w) -> p c w", c=NC),
                             hD.rearrange("c p w -> p c w")).then_inc(h_back, 16)
                sp.wait_ge(h_in, 16 * (1 + 2 * NC))
                sp.wait_ge(h_back, 16)

            @block.vector
            def _(v):
                v.wait_ge(h_in, 16)
                ln_v1(v, 0, hbuf)
                ln_v2(v, 0, hbuf)
                ln_v3(v, 0, sq)
                ln_v4(v, 0)
                ln_v5(v, 0)
                with v.Fori(0, NC) as c:
                    V.here = 0
                    for m in range(2 * KT):
                        rope_v(v, c, m, (qT if m < KT else kT)[:, m % KT, :])
                        if m == 3:
                            v.wait_ge(h_in, c * 32 + 32)
                            ln_v1(v, c + 1, hbuf)
                        if m == 7:
                            ln_v2(v, c + 1, hbuf)
                        if m == 11:
                            ln_v3(v, c + 1, sq)
                        if m == 15:
                            ln_v4(v, c + 1)
                            ln_v5(v, c + 1, [(PE.sem, PE.at("qkv23", c))])
                    for g in range(GROUPS + 1):
                        if g:
                            soft_sum(v, c, g - 1)
                        if g < GROUPS:
                            soft_top(v, c, g, True)
                    v.wait_ge(h_in, c * 32 + 48)
                    for m in range(KT):
                        v.wait_ge(PE.sem, PE.at(f"proj{m}", c))
                        v.scalar_tensor_tensor(out=hbuf[:, m, :], in0=PS[:, 1 + m % 4, 0:CT], scalar=bias("out_b", m),
                                               in1=hbuf[:, m, :], op0=ALU.add, op1=ALU.add
                                               ).then_inc(V.done(f"res{m}"), 1)

            @block.gpsimd
            def _(g):
                with g.Fori(0, NC) as c:
                    G.here = 0
                    for m in range(2 * KT):
                        rope_g(g, c, m, (qT if m < KT else kT)[:, m % KT, :])
                    for i in range(GROUPS + 1):
                        if i:
                            soft_norm(g, c, i - 1)
                        if i < GROUPS:
                            soft_shift(g, c, i)

            @block.scalar
            def _(a):
                ln_a1(a, 0, sq)
                ln_a2(a, 0)
                with a.Fori(0, NC) as c:
                    AC.here = 0
                    for m in range(NQ):
                        a.wait_ge(PE.sem, PE.at(f"qkv{m}", c))
                        x = (qT, kT, vT)[m // KT]
                        a.activation(x[:, m % KT, :], PS[:, 1 + m % 4, 0:CT], ACT.Identity, bias=bias("qkv_b", m)
                                     ).then_inc(AC.done(f"ev{m}"), 1)
                        if m == 13:
                            ln_a1(a, c + 1, sq)
                        if m == 20:
                            ln_a2(a, c + 1)
                    for g in range(GROUPS + LAG):
                        if g % 2 == 0 and g < GROUPS:
                            b = g // 2
                            a.wait_ge(PE.sem, PE.at(f"Vt{b}", c))
                            if b >= 2:
                                a.wait_ge(PE.sem, PE.at(f"O{2 * b - 3}", c))
                            a.activation(v_tok[b % 2].rearrange("p (n w) -> p n w", n=2), PS[0:S, 5:7, :], ACT.Copy
                                         ).then_inc(AC.done(f"vt{b}"), 1)
                        probs_a(a, c, g, True)
                        if g >= LAG:
                            b, half = (g - LAG) // 2, (g - LAG) % 2
                            a.wait_ge(PE.sem, PE.at(f"O{g - LAG}", c))
                            a.activation(ctxT[:, half * QT:half * QT + QT, b * S:(b + 1) * S],
                                         PS[:, 7, 0:QT * S].rearrange("p (u t) -> p u t", u=QT), ACT.Copy
                                         ).then_inc(AC.done(f"ctx{g - LAG}"), 1)

            @block.tensor
            def _(pe):
                ln_p1(pe, 0)
                ln_p2(pe, 0)
                pe.wait_ge(w_in[0], 48)
                with pe.Fori(0, NC) as c:
                    PE.here = 0
                    pe.wait_ge(LV.sem, LV.at("out", c))
                    for m in range(NQ + 2):
                        if m < NQ:
                            if m >= 4:
                                pe.wait_ge(AC.sem, AC.at(f"ev{m - 4}", c))
                            else:
                                pe.wait_ge(V.sem, V.prev(f"res{m + 4}", c))
                            w = w_qk if m < 2 * KT else w_v
                            o = (m % (2 * KT)) * P
                            gemm(pe, PS[:, 1 + m % 4, 0:CT], lambda k: w[:, k, o:o + P], range(KT)
                                 ).then_inc(PE.done(f"qkv{m}"), 1)
                        if m == 8:
                            ln_p1(pe, c + 1)
                        if m == 18:
                            ln_p2(pe, c + 1)
                        if 2 <= m < 2 * KT + 2:
                            rope_p(pe, c, m - 2, (qT if m - 2 < KT else kT)[:, (m - 2) % KT, :])
                    pe.wait_ge(V.sem, V.at("rr15", c))
                    for g in range(GROUPS + LAG):
                        if g % 2 == 0 and g < GROUPS:
                            b = g // 2
                            if b == 0:
                                pe.wait_ge(AC.sem, AC.at("ev23", c))
                            elif 2 * b <= LAG:
                                pe.wait_ge(AC.sem, AC.at(f"vt{b - 1}", c))
                            else:
                                pe.wait_ge(AC.sem, AC.at(f"pt{2 * b - LAG - 1}_3", c))
                            for k in range(KT):
                                mm = pe.transpose(PS[0:S, 5 + k // 4, k % 4 * P:k % 4 * P + P],
                                                  vT[:, k, b * S:(b + 1) * S], ident)
                            mm.then_inc(PE.done(f"Vt{b}"), 1)
                        if g < GROUPS:
                            scores_p(pe, c, g, False)
                        if g >= LAG:
                            values_p(pe, c, g - LAG,
                                     lambda u, j, q=g - LAG: v_tok[q // 2 % 2][:, (q % 2 * 16 + 4 * u + j) * HD:
                                                                           (q % 2 * 16 + 4 * u + j) * HD + HD],
                                     lambda u, j: PS[32 * j:32 * j + 32, 7, u * S:(u + 1) * S],
                                     AC.sem, AC.at(f"ctx{g - LAG - 1}", c) if g > LAG else None,
                                     lambda u, q=g: [(AC.sem, AC.at(f"vt{q // 2}", c))] if q % 2 == 0 and q < GROUPS
                                     else [(AC.sem, AC.at(f"pt{q - LAG - 1}_{2 + u}", c))])
                    pe.wait_ge(AC.sem, AC.at("ctx7", c))
                    for m in range(KT):
                        if m >= 4:
                            pe.wait_ge(V.sem, V.at(f"res{m - 4}", c))
                        gemm(pe, PS[:, 1 + m % 4, 0:CT], lambda k: w_out[:, k, m * P:m * P + P], range(KT), x=ctxT
                             ).then_inc(PE.done(f"proj{m}"), 1)

        for t in (V, AC, G, PE):
            t.close()
        if STOP_AFTER == 1:
            return finish()

        sq2_at = WORDS - CW
        sq2 = words(sq2_at, KT, CT)
        FREE_END = sq2_at

        def following(e, c):
            return e.snap((c + 1) & 7)

        def routed(layer, top, base_name, router_name, a_name, b_name, bias_name, spread):
            w_base = words(W_AT, KT, D)
            w_a = words(W_AT + KT * D, KT, P)
            w_b = words(W_AT + KT * D + D, D)
            w_r = words(W_AT + KT * D + 2 * D, KT, EXPERTS)
            o = W_AT + KT * D + 2 * D + KT * EXPERTS
            h_a, comb_t, wh = words(o, CT), words(o + CT, CT, rows=EXPERTS), words(o + 2 * CT, CT)
            o += 3 * CT
            pair = [words(o + 256 * i, CB, EXPERTS, EXPERTS, rows=S) for i in range(2)]
            o += 512
            lg, rank, ex, comb = (words(o + 32 * i, CB, EXPERTS, rows=S) for i in range(4))
            top_l, den = (words(o + 128 + 4 * i, CB, rows=S) for i in range(2))
            assert o + 136 <= FREE_END
            base = base_name is not None
            LAG = 3

            V.layer(["lg", "gt", "eq", "tie", "both", "rank", "sel"]
                    + (["top", "off", "kept", "den", "rden"] if top == 2 else []) + ["comb", "wh"]
                    + [f"res{m}" for m in range(KT)])
            AC.layer(["ha"] + (["ex"] if top == 2 else []) + ["ct"])
            pe_names = ["router", "hA"]
            order = []
            for m in range(KT + LAG):
                if m < KT and base:
                    order.append(("base", m))
                if m == 1:
                    order.append(("comb", 0))
                if m == 2:
                    order.append(("spread", 0))
                if m >= LAG:
                    order.append(("lora", m - LAG))
            PE.layer(pe_names + [f"{x}{m}" for x, m in order])

            with nc.Block() as block:
                @block.sync
                def _(sp):
                    if base:
                        sp.dma_start(w_base, T[base_name].rearrange("p (k n) -> p k n", k=KT)).then_inc(w_in[layer], 16)
                    sp.dma_start(w_a, T[a_name].rearrange("p (k n) -> p k n", k=KT)).then_inc(w_in[layer], 16)
                    sp.dma_start(w_b, T[b_name]).then_inc(w_in[layer], 16)
                    sp.dma_start(w_r, T[router_name].rearrange("p (k n) -> p k n", k=KT)).then_inc(w_in[layer], 16)

                @block.vector
                def _(v):
                    with v.Fori(0, NC) as c:
                        V.here = 0
                        n = c + (layer * NC + 1)
                        c1 = following(v, c)
                        ln_v1(v, n, h_chunk(c1))
                        v.wait_ge(PE.sem, PE.at("router", c))
                        v.tensor_copy(lg, PS[0:S, 1, 0:CB * EXPERTS].rearrange("p (b e) -> p b e", b=CB)
                                      ).then_inc(V.done("lg"), 1)
                        other = lg.unsqueeze(2).broadcast_to([S, CB, EXPERTS, EXPERTS])
                        self_ = lg.unsqueeze(3).broadcast_to([S, CB, EXPERTS, EXPERTS])
                        own(v, V, c)
                        v.tensor_tensor(pair[0], other, self_, ALU.is_gt).then_inc(V.done("gt"), 1)
                        v.tensor_tensor(pair[1], other, self_, ALU.is_equal).then_inc(V.done("eq"), 1)
                        own(v, V, c)
                        v.tensor_tensor(pair[1], pair[1],
                                        const("earlier", S).rearrange("p (e j) -> p e j", e=EXPERTS).unsqueeze(1)
                                        .broadcast_to([S, CB, EXPERTS, EXPERTS]), ALU.mult).then_inc(V.done("tie"), 1)
                        own(v, V, c)
                        v.tensor_tensor(pair[0], pair[0], pair[1], ALU.add).then_inc(V.done("both"), 1)
                        own(v, V, c)
                        v.tensor_reduce(rank, pair[0], AX.X, ALU.add).then_inc(V.done("rank"), 1)
                        own(v, V, c)
                        v.tensor_scalar(rank, rank, float(top), None, ALU.is_lt).then_inc(V.done("sel"), 1)
                        if top == 2:
                            v.tensor_reduce(top_l, lg, AX.X, ALU.max).then_inc(V.done("top"), 1)
                            own(v, V, c)
                            v.tensor_tensor(ex, lg, top_l.unsqueeze(2).broadcast_to([S, CB, EXPERTS]), ALU.subtract
                                            ).then_inc(V.done("off"), 1)
                            v.wait_ge(AC.sem, AC.at("ex", c))
                            v.tensor_tensor(ex, ex, rank, ALU.mult).then_inc(V.done("kept"), 1)
                            own(v, V, c)
                            v.tensor_reduce(den, ex, AX.X, ALU.add).then_inc(V.done("den"), 1)
                            own(v, V, c)
                            v.reciprocal(den, den).then_inc(V.done("rden"), 1)
                            own(v, V, c)
                            v.tensor_tensor(comb, ex, den.unsqueeze(2).broadcast_to([S, CB, EXPERTS]), ALU.mult
                                            ).then_inc(V.done("comb"), 1)
                        else:
                            own(v, V, c)
                            v.tensor_tensor(comb, lg, rank, ALU.mult).then_inc(V.done("comb"), 1)
                        ln_v2(v, n, h_chunk(c1))
                        v.wait_ge(PE.sem, PE.at("spread0", c))
                        v.tensor_tensor(wh, h_a, PS[:, 2, 0:CT], ALU.mult).then_inc(V.done("wh"), 1)
                        ln_v3(v, n, sq2)
                        for m in range(KT):
                            v.wait_ge(PE.sem, PE.at(f"lora{m}", c))
                            hm, ps = h_tile(c, m), PS[:, 3 + m % 5, 0:CT]
                            if bias_name:
                                v.scalar_tensor_tensor(out=hm, in0=ps, scalar=bias(bias_name, m), in1=hm, op0=ALU.add,
                                                       op1=ALU.add).then_inc(V.done(f"res{m}"), 1)
                            else:
                                v.tensor_tensor(hm, ps, hm, ALU.add).then_inc(V.done(f"res{m}"), 1)
                            if m == 3:
                                ln_v4(v, n)
                                ln_v5(v, n, [(PE.sem, PE.at("base7" if base else "hA", c))])

                @block.scalar
                def _(a):
                    with a.Fori(0, NC) as c:
                        AC.here = 0
                        n = c + (layer * NC + 1)
                        a.wait_ge(PE.sem, PE.at("hA", c))
                        a.activation(h_a, PS[:, 2, 0:CT], ACT.Copy).then_inc(AC.done("ha"), 1)
                        if top == 2:
                            a.wait_ge(V.sem, V.at("off", c))
                            a.activation(ex, ex, ACT.Exp).then_inc(AC.done("ex"), 1)
                        a.wait_ge(PE.sem, PE.at("comb0", c))
                        a.activation(comb_t, PS[0:EXPERTS, 1, 0:CT], ACT.Copy).then_inc(AC.done("ct"), 1)
                        ln_a1(a, n, sq2)
                        ln_a2(a, n)

                @block.tensor
                def _(pe):
                    pe.wait_ge(w_in[layer], 16 * (3 + base))
                    with pe.Fori(0, NC) as c:
                        PE.here = 0
                        n = c + (layer * NC + 1)
                        pe.wait_ge(LV.sem, LV.at("out", n - 1))
                        pe.wait_ge(AC.sem, AC.prev("ct", c))
                        for b in range(CB):
                            for k in range(KT):
                                mm = pe.matmul(PS[0:S, 1, b * EXPERTS:(b + 1) * EXPERTS], xn[:, k, b * S:(b + 1) * S],
                                               w_r[:, k, :], start=k == 0, stop=k == KT - 1)
                        mm.then_inc(PE.done("router"), 1)
                        pe.wait_ge(V.sem, V.prev("wh", c))
                        gemm(pe, PS[:, 2, 0:CT], lambda k: w_a[:, k, :], range(KT)).then_inc(PE.done("hA"), 1)
                        for what, m in order:
                            bank = PS[:, 3 + m % 5, 0:CT]
                            first = what == "base" or (what == "lora" and not base)
                            if first:
                                if m >= 5:
                                    pe.wait_ge(V.sem, V.at(f"res{m - 5}", c))
                                else:
                                    pe.wait_ge(V.sem, V.prev(f"res{min(m + 5, 7)}", c))
                            if what == "base":
                                gemm(pe, bank, lambda k: w_base[:, k, m * P:m * P + P], range(KT), last=False
                                     ).then_inc(PE.done(f"base{m}"), 1)
                            elif what == "comb":
                                pe.wait_ge(V.sem, V.at("comb", c))
                                for b in range(CB):
                                    mm = pe.transpose(PS[0:EXPERTS, 1, b * S:(b + 1) * S], comb[:, b, :],
                                                      const("ident", S)[:, 0:S])
                                mm.then_inc(PE.done("comb0"), 1)
                                ln_p1(pe, n)
                            elif what == "spread":
                                pe.wait_ge(AC.sem, AC.at("ct", c))
                                pe.matmul(PS[:, 2, 0:CT], const(spread, EXPERTS), comb_t, start=True, stop=True
                                          ).then_inc(PE.done("spread0"), 1)
                            else:
                                if m == 0:
                                    pe.wait_ge(V.sem, V.at("wh", c))
                                pe.matmul(bank, w_b[:, m * P:m * P + P], wh, start=not base, stop=True
                                          ).then_inc(PE.done(f"lora{m}"), 1)
                                if m == 0:
                                    ln_p2(pe, n)

            for t in (V, AC, G, PE):
                t.close()

        G.layer([])
        routed(1, 2, "base0_w", "router0", "a0", "b0", "base0_b", "spread2")
        if STOP_AFTER == 2:
            return finish()

        rows = {x: words(W_AT + 256 * i, 256, rows=HDH) for i, x in enumerate("qkv")}
        t_abs, t_pos, t_neg = (words(W_AT + 768 + 256 * i, 256, rows=HDH) for i in range(3))
        alpha = words(W_AT + 1536, 1, rows=HDH)
        bind = {x: A[:, BIND_AT + 8 * i:BIND_AT + 8 * i + 8] for i, x in enumerate("qkv")}
        V.layer([f"{x}{s}" for x in "qkv" for s in ("pos", "neg", "al", "mean", "sign", "hard", "zero", "fill", "diff",
                                                     "sum", "col")], 1)
        PE.layer([f"{x}t" for x in "qkv"], 1)
        with nc.Block() as block:
            @block.sync
            def _(sp):
                for x in "qkv":
                    sp.dma_start(rows[x], T[f"bind_{x}"]).then_inc(w_in[2], 16)

            @block.vector
            def _(v):
                v.wait_ge(w_in[2], 48)
                for x in "qkv":
                    w = rows[x]
                    own(v, V)
                    v.tensor_scalar(t_pos, w, 0.0, None, ALU.is_gt).then_inc(V.done(f"{x}pos"), 1)
                    own(v, V)
                    v.tensor_scalar(t_neg, w, 0.0, None, ALU.is_lt).then_inc(V.done(f"{x}neg"), 1)
                    own(v, V)
                    v.tensor_reduce(alpha, w, AX.X, ALU.add, apply_absolute_value=True).then_inc(V.done(f"{x}al"), 1)
                    own(v, V)
                    v.tensor_scalar(alpha, alpha, 1.0 / 256, None, ALU.mult).then_inc(V.done(f"{x}mean"), 1)
                    own(v, V)
                    v.tensor_tensor(t_pos, t_pos, t_neg, ALU.subtract).then_inc(V.done(f"{x}sign"), 1)
                    own(v, V)
                    v.tensor_scalar(t_pos, t_pos, alpha, None, ALU.mult).then_inc(V.done(f"{x}hard"), 1)
                    own(v, V)
                    v.tensor_scalar(t_neg, t_pos, 0.0, alpha, ALU.is_equal, ALU.mult).then_inc(V.done(f"{x}zero"), 1)
                    own(v, V)
                    v.tensor_tensor(t_pos, t_pos, t_neg, ALU.add).then_inc(V.done(f"{x}fill"), 1)
                    own(v, V)
                    v.tensor_tensor(t_pos, t_pos, w, ALU.subtract).then_inc(V.done(f"{x}diff"), 1)
                    own(v, V)
                    v.tensor_tensor(w, t_pos, w, ALU.add).then_inc(V.done(f"{x}sum"), 1)
                    v.wait_ge(PE.sem, PE.at(f"{x}t"))
                    v.tensor_copy(bind[x].rearrange("p (h f) -> p f h", f=2),
                                  PS[:, 1, 0:2 * HDH].rearrange("p (f h) -> p f h", f=2)).then_inc(V.done(f"{x}col"), 1)

            @block.tensor
            def _(pe):
                for x in "qkv":
                    pe.wait_ge(V.sem, V.at(f"{x}sum"))
                    for f in range(2):
                        mm = pe.transpose(PS[:, 1, f * HDH:(f + 1) * HDH], rows[x][:, f * P:(f + 1) * P],
                                          const("ident", HDH)[:, 0:HDH])
                    mm.then_inc(PE.done(f"{x}t"), 1)

        for t in (V, PE):
            t.close()

        o = W_AT
        q3, k3, v3 = (words(o + i * CW, KT, CT) for i in range(3))
        v3_tok = [words(o + 3 * CW + i * D, D, rows=S) for i in range(CB)]
        att = words(o + 3 * CW + CB * D, CB, HDH, S, rows=S)
        V.layer(["Q", "K", "one", "rec", "keep"] + [f"res{m}" for m in range(KT)])
        G.layer(["V"])
        AC.layer(["ex"] + [f"vt{b}" for b in range(CB)])
        PE.layer(["S"] + [f"Vt{b}" for b in range(CB)] + [f"O{m}" for m in range(KT)])
        LAYER = 2
        with nc.Block() as block:
            @block.vector
            def _(v):
                with v.Fori(0, NC) as c:
                    V.here = 0
                    n = c + (LAYER * NC + 1)
                    c1 = following(v, c)
                    wide = lambda x: bind[x].unsqueeze(2).broadcast_to([P, KT, CT])
                    v.wait_ge(PE.sem, PE.prev("S", c))
                    v.tensor_tensor(q3, xn, wide("q"), ALU.mult).then_inc(V.done("Q"), 1)
                    v.tensor_tensor(k3, xn, wide("k"), ALU.mult).then_inc(V.done("K"), 1)
                    ln_v1(v, n, h_chunk(c1))
                    ln_v2(v, n, h_chunk(c1))
                    v.wait_ge(AC.sem, AC.at("ex", c))
                    v.tensor_scalar(att, att, 1.0, None, ALU.add).then_inc(V.done("one"), 1)
                    own(v, V, c)
                    v.reciprocal(att, att).then_inc(V.done("rec"), 1)
                    own(v, V, c)
                    v.tensor_tensor(att, att, const("causal_t", S).unsqueeze(1).unsqueeze(1)
                                    .broadcast_to([S, CB, HDH, S]), ALU.mult).then_inc(V.done("keep"), 1)
                    ln_v3(v, n, sq2)
                    ln_v4(v, n)
                    ln_v5(v, n, [(G.sem, G.at("V", c))])
                    for m in range(KT):
                        v.wait_ge(PE.sem, PE.at(f"O{m}", c))
                        v.tensor_tensor(h_tile(c, m), PS[:, 5 + m % 3, 0:CT], h_tile(c, m), ALU.add
                                        ).then_inc(V.done(f"res{m}"), 1)

            @block.gpsimd
            def _(g):
                with g.Fori(0, NC) as c:
                    G.here = 0
                    g.wait_ge(LV.sem, LV.at("out", c + LAYER * NC))
                    g.wait_ge(PE.sem, PE.prev("Vt3", c))
                    g.tensor_tensor(v3, xn, bind["v"].unsqueeze(2).broadcast_to([P, KT, CT]), ALU.mult
                                    ).then_inc(G.done("V"), 1)

            @block.scalar
            def _(a):
                with a.Fori(0, NC) as c:
                    AC.here = 0
                    n = c + (LAYER * NC + 1)
                    a.wait_ge(PE.sem, PE.at("S", c))
                    a.wait_ge(PE.sem, PE.prev("O7", c))
                    a.activation(att.rearrange("p b h s -> p b (h s)"), PS[0:S, 1:5, 0:HDH * S], ACT.Exp, scale=-0.25
                                 ).then_inc(AC.done("ex"), 1)
                    ln_a1(a, n, sq2)
                    for b in range(CB):
                        a.wait_ge(PE.sem, PE.at(f"Vt{b}", c))
                        a.activation(v3_tok[b].rearrange("p (n w) -> p n w", n=2), PS[0:S, 5:7, :], ACT.Copy
                                     ).then_inc(AC.done(f"vt{b}"), 1)
                    ln_a2(a, n)

            @block.tensor
            def _(pe):
                with pe.Fori(0, NC) as c:
                    PE.here = 0
                    n = c + (LAYER * NC + 1)
                    pe.wait_ge(V.sem, V.at("K", c))
                    for b in range(CB):
                        for hd in range(HDH):
                            for f in range(2):
                                k = 2 * hd + f
                                mm = pe.matmul(PS[0:S, 1 + b, hd * S:(hd + 1) * S], k3[:, k, b * S:(b + 1) * S],
                                               q3[:, k, b * S:(b + 1) * S], start=f == 0, stop=f == 1)
                    mm.then_inc(PE.done("S"), 1)
                    ln_p1(pe, n)
                    pe.wait_ge(G.sem, G.at("V", c))
                    for b in range(CB):
                        if b:
                            pe.wait_ge(AC.sem, AC.at(f"vt{b - 1}", c))
                        else:
                            pe.wait_ge(V.sem, V.prev("res7", c))
                        for k in range(KT):
                            mm = pe.transpose(PS[0:S, 5 + k // 4, k % 4 * P:k % 4 * P + P], v3[:, k, b * S:(b + 1) * S],
                                              ident)
                        mm.then_inc(PE.done(f"Vt{b}"), 1)
                    ln_p2(pe, n)
                    pe.wait_ge(V.sem, V.at("keep", c))
                    pe.wait_ge(AC.sem, AC.at("vt3", c))
                    for m in range(KT):
                        if m >= 3:
                            pe.wait_ge(V.sem, V.at(f"res{m - 3}", c))
                        for b in range(CB):
                            mm = pe.matmul(PS[:, 5 + m % 3, b * S:(b + 1) * S], v3_tok[b][:, m * P:m * P + P],
                                           att[:, b, m // 2, :], start=True, stop=True)
                        mm.then_inc(PE.done(f"O{m}"), 1)

        for t in (V, AC, G, PE):
            t.close()
        if STOP_AFTER == 3:
            return finish()

        G.layer([])
        routed(3, 1, None, "router1", "a1", "b1", None, "spread1")
        if STOP_AFTER == 4:
            return finish()

        o = W_AT
        w_xp = words(o, KT, DTR + 2 * SSM)
        w_dt = words(o + 512, D, rows=DTR)
        neg_a = words(o + 1536, KT, SSM)
        xp = words(o + 1664, CT, rows=DTR + 2 * SSM)
        BC_AT = o + 1664 + CT
        BC_W = 2 * SSM * CT
        o = BC_AT + 2 * BC_W
        dt, ux = words(o, KT, CT), words(o + CW, KT, CT)
        o += 2 * CW
        UN = 4
        UW = UN * CT
        NU = SSM // UN
        da = [words(o + i * UW, UN, CB, S) for i in range(2)]
        st_at = o + 2 * UW
        st = [words(st_at + i * UW, UN, CT) for i in range(3)]
        st_flat = [words(st_at + i * UW, UW) for i in range(3)]
        da_flat = [words(o + i * UW, UW) for i in range(2)]
        soft = words(st_at, KT, CT)
        assert st_at + 3 * UW <= FREE_END
        LAYER5 = 4
        XP, XA = Steps(sem("scan_input_tensor_steps")), Steps(sem("scan_input_scalar_steps"))
        XP.layer(["xp"], NC + 1)
        XA.layer(["xp"], NC + 1)

        def xp_p(pe, c):
            pe.wait_ge(LV.sem, LV.at("out", c + LAYER5 * NC))
            XP.here = 0
            gemm(pe, PS[0:DTR + 2 * SSM, 7, 0:CT], lambda k: w_xp[:, k, :], range(KT)).then_inc(XP.done("xp"), 1)

        def xp_a(a, c):
            XA.here = 0
            a.wait_ge(XP.sem, XP.at("xp", c))
            a.activation(xp, PS[0:DTR + 2 * SSM, 7, 0:CT], ACT.Copy).then_inc(XA.done("xp"), 1)

        V.layer(["neg", "zero0", "zero1"], 1)
        AC.layer(["a"], 1)
        with nc.Block() as block:
            @block.sync
            def _(sp):
                sp.dma_start(w_xp, T["xproj"].rearrange("p (k n) -> p k n", k=KT)).then_inc(w_in[4], 16)
                sp.dma_start(w_dt, T["dtw"]).then_inc(w_in[4], 16)
                sp.dma_start(neg_a, T["a_log"].rearrange("p (k n) -> p k n", k=KT)).then_inc(w_in[4], 16)

            @block.scalar
            def _(a):
                a.wait_ge(w_in[4], 48)
                a.activation(neg_a, neg_a, ACT.Exp).then_inc(AC.done("a"), 1)
                xp_a(a, 0)

            @block.vector
            def _(v):
                v.wait_ge(AC.sem, AC.at("a"))
                v.tensor_scalar(neg_a, neg_a, -1.0, None, ALU.mult).then_inc(V.done("neg"), 1)
                for i in range(2):
                    v.memset(da[i][:, :, :, 0], 0.0).then_inc(V.done(f"zero{i}"), 1)

            @block.tensor
            def _(pe):
                pe.wait_ge(w_in[4], 48)
                xp_p(pe, 0)

        for t in (V, AC):
            t.close()

        units = [(m, q) for m in range(KT) for q in range(NU)]
        V.layer([f"z{m}" for m in range(KT)] + ["dt", "u"] + [f"skip{m}" for m in range(KT)]
                + [x for m, q in units for x in ([f"scan{m}_{q}", f"hc{m}_{q}"]
                                                 + ([f"res{m - 1}"] if q == 1 and m else []))] + ["res7"])
        AC.layer(["abs", "exp", "log"] + [f"da{m}_{q}" for m, q in units])
        G.layer([f"bx{m}_{q}" for m, q in units])
        PE.layer([f"dt{m}" for m in range(KT)] + [f"y{m}_{q}" for m, q in units])

        with nc.Block() as block:
            @block.sync
            def _(sp):
                def spread(r, slot):
                    sp.wait_ge(XA.sem, XA.at("xp", r))
                    sp.dma_start(bcD, xp[DTR:, :]).then_inc(bc_out, 16)
                    sp.wait_ge(bc_out, r * 16 + 16)
                    sp.dma_start(A[:, BC_AT + slot * BC_W:BC_AT + (slot + 1) * BC_W],
                                 bcD.rearrange("n t -> (n t)").unsqueeze(0).broadcast_to([P, BC_W])
                                 ).then_inc(bc_in, 16)

                spread(0, 0)
                with sp.Fori(1, NC - 1, 2) as r:
                    spread(r, 1)
                    spread(r + 1, 0)
                spread(NC - 1, 1)

            @block.gpsimd
            def _(g):
                def chunk(c, slot):
                    G.here = 0
                    g.wait_ge(bc_in, c * 16 + 16)
                    g.wait_ge(V.sem, V.at("u", c))
                    for i, (m, q) in enumerate(units):
                        if i >= 3:
                            mm_, qq_ = units[i - 3]
                            g.wait_ge(PE.sem, PE.at(f"y{mm_}_{qq_}", c))
                        g.tensor_tensor(st[i % 3], ux[:, m, :].unsqueeze(1).broadcast_to([P, UN, CT]),
                                        words(BC_AT + slot * BC_W + q * UW, UN, CT), ALU.mult
                                        ).then_inc(G.done(f"bx{m}_{q}"), 1)

                with g.Fori(0, NC, 2) as c:
                    chunk(c, 0)
                    chunk(c + 1, 1)

            @block.vector
            def _(v):
                with v.Fori(0, NC) as c:
                    V.here = 0
                    n = c + (LAYER5 * NC + 1)
                    c1 = following(v, c)
                    slot = v.snap(c & 1)
                    for m in range(KT):
                        v.wait_ge(PE.sem, PE.at(f"dt{m}", c))
                        v.tensor_scalar(dt[:, m, :], PS[:, 1 + m % 3, 0:CT], bias("dt_b", m), None, ALU.add
                                        ).then_inc(V.done(f"z{m}"), 1)
                    v.wait_ge(AC.sem, AC.at("log", c))
                    v.scalar_tensor_tensor(out=dt, in0=dt, scalar=0.0, in1=soft, op0=ALU.max, op1=ALU.add
                                           ).then_inc(V.done("dt"), 1)
                    own(v, V, c)
                    v.tensor_tensor(ux, dt, xn, ALU.mult).then_inc(V.done("u"), 1)
                    for m in range(KT):
                        v.scalar_tensor_tensor(out=h_tile(c, m), in0=xn[:, m, :], scalar=bias("skip", m),
                                               in1=h_tile(c, m), op0=ALU.mult, op1=ALU.add
                                               ).then_inc(V.done(f"skip{m}"), 1)
                    for i, (m, q) in enumerate(units):
                        v.wait_ge(AC.sem, AC.at(f"da{m}_{q}", c))
                        v.wait_ge(G.sem, G.at(f"bx{m}_{q}", c))
                        v.tensor_tensor_scan(st_flat[i % 3], da_flat[i % 2], st_flat[i % 3], 0.0, ALU.mult, ALU.add
                                             ).then_inc(V.done(f"scan{m}_{q}"), 1)
                        own(v, V, c)
                        v.tensor_tensor(st_flat[i % 3], st_flat[i % 3],
                                        A[:, bass.ds(slot * BC_W + (BC_AT + SSM * CT + q * UW), UW)], ALU.mult
                                        ).then_inc(V.done(f"hc{m}_{q}"), 1)
                        if q == 1 and m:
                            v.wait_ge(PE.sem, PE.at(f"y{m - 1}_{NU - 1}", c))
                            v.tensor_tensor(h_tile(c, m - 1), PS[:, 4 + (m - 1) % 3, 0:CT], h_tile(c, m - 1), ALU.add
                                            ).then_inc(V.done(f"res{m - 1}"), 1)
                        if (m, q) == (0, 1):
                            ln_v1(v, n, h_chunk(c1))
                        if (m, q) == (0, 3):
                            ln_v2(v, n, h_chunk(c1))
                        if (m, q) == (1, 3):
                            ln_v3(v, n, sq2)
                        if (m, q) == (3, 1):
                            ln_v4(v, n)
                            ln_v5(v, n)
                    v.wait_ge(PE.sem, PE.at(f"y7_{NU - 1}", c))
                    v.tensor_tensor(h_tile(c, 7), PS[:, 4 + 7 % 3, 0:CT], h_tile(c, 7), ALU.add
                                    ).then_inc(V.done("res7"), 1)

            @block.scalar
            def _(a):
                with a.Fori(0, NC) as c:
                    AC.here = 0
                    n = c + (LAYER5 * NC + 1)
                    a.wait_ge(V.sem, V.at("z7", c))
                    a.wait_ge(PE.sem, PE.prev("y7_3", c))
                    a.activation(soft, dt, ACT.Abs).then_inc(AC.done("abs"), 1)
                    own(a, AC, c)
                    a.activation(soft, soft, ACT.Exp, scale=-1.0).then_inc(AC.done("exp"), 1)
                    own(a, AC, c)
                    a.activation(soft, soft, ACT.Ln, bias=1.0).then_inc(AC.done("log"), 1)
                    a.wait_ge(V.sem, V.at("dt", c))
                    for i, (m, q) in enumerate(units):
                        if i >= 2:
                            mm_, qq_ = units[i - 2]
                            a.wait_ge(V.sem, V.at(f"scan{mm_}_{qq_}", c))
                        x = dt[:, m, :].rearrange("p (b s) -> p b s", b=CB)[:, :, 1:]
                        for k in range(UN):
                            ins = a.activation(da[i % 2][:, k, :, 1:], x, ACT.Exp,
                                               scale=neg_a[:, m, q * UN + k:q * UN + k + 1])
                        ins.then_inc(AC.done(f"da{m}_{q}"), 1)
                        if (m, q) == (1, 1):
                            ln_a1(a, n, sq2)
                        if (m, q) == (3, 0):
                            ln_a2(a, n)
                        if (m, q) == (4, 2):
                            a.wait_ge(bc_out, c * 16 + 16)
                            xp_a(a, c + 1)

            @block.tensor
            def _(pe):
                with pe.Fori(0, NC) as c:
                    PE.here = 0
                    n = c + (LAYER5 * NC + 1)
                    pe.wait_ge(XA.sem, XA.at("xp", c))
                    for m in range(KT):
                        if m >= 3:
                            pe.wait_ge(V.sem, V.at(f"z{m - 3}", c))
                        pe.matmul(PS[:, 1 + m % 3, 0:CT], w_dt[:, m * P:m * P + P], xp[0:DTR, :], start=True, stop=True
                                  ).then_inc(PE.done(f"dt{m}"), 1)
                    for i, (m, q) in enumerate(units):
                        if q == 0 and m >= 3:
                            pe.wait_ge(V.sem, V.at(f"res{m - 3}", c))
                        pe.wait_ge(V.sem, V.at(f"hc{m}_{q}", c))
                        for k in range(UN):
                            mm = pe.matmul(PS[:, 4 + m % 3, 0:CT], ident, st[i % 3][:, k, :], start=q == 0 and k == 0,
                                           stop=q == NU - 1 and k == UN - 1)
                        mm.then_inc(PE.done(f"y{m}_{q}"), 1)
                        if (m, q) == (0, 2):
                            ln_p1(pe, n)
                        if (m, q) == (2, 2):
                            ln_p2(pe, n)
                        if (m, q) == (4, 0):
                            pe.wait_ge(XA.sem, XA.at("xp", c))
                            xp_p(pe, c + 1)

        for t in (V, AC, G, PE, XP, XA):
            t.close()
        if STOP_AFTER == 5:
            return finish()

        o = W_AT
        w_base = words(o, KT, D)
        w_enc = words(o + KT * D, KT, ENC)
        w_wave = words(o + KT * D + KT * ENC, D, rows=ENC)
        enc_s = words(o + KT * D + KT * ENC + D, CT, rows=ENC)
        o += KT * D + KT * ENC + D + CT
        fourier = words(o, KT, D)
        coef = words(o + KT * D, KT, 3, ENC)
        mask_f = words(o + KT * D + KT * 3 * ENC, KT, 3, ENC)
        mask_u = A[:, o + KT * D + 2 * KT * 3 * ENC:o + KT * D + 2 * KT * 3 * ENC + KT * 3 * ENC // 4].bitcast(U8)
        w_sum = words(o + KT * D + 2 * KT * 3 * ENC + KT * 3 * ENC // 4, KT, ENC)
        V.layer(["mask", "kept", "sum"], 1)
        PE.layer(["wave"], 1)
        AC.layer(["wave"], 1)
        with nc.Block() as block:
            @block.sync
            def _(sp):
                sp.dma_start(coef.rearrange("p k e r -> p (k e r)"), T["coef"]).then_inc(w_in[5], 16)
                sp.dma_start(mask_u.bitcast(mybir.dt.int32), T["mask"]).then_inc(w_in[5], 16)
                sp.dma_start(fourier, T["fourier"].rearrange("p (k n) -> p k n", k=KT)).then_inc(w_in[5], 16)
                sp.dma_start(w_enc, T["enc"].rearrange("p (k n) -> p k n", k=KT)).then_inc(w_in[5], 16)
                sp.dma_start(w_base, T["base2_w"].rearrange("p (k n) -> p k n", k=KT)).then_inc(w_in[5], 16)

            @block.vector
            def _(v):
                v.wait_ge(w_in[5], 80)
                v.tensor_copy(mask_f.rearrange("p k e r -> p (k e r)"), mask_u).then_inc(V.done("mask"), 1)
                own(v, V)
                v.tensor_tensor(coef, coef, mask_f, ALU.mult).then_inc(V.done("kept"), 1)
                own(v, V)
                v.tensor_reduce(w_sum, coef.rearrange("p k e r -> p k r e"), AX.X, ALU.add).then_inc(V.done("sum"), 1)

            @block.tensor
            def _(pe):
                pe.wait_ge(V.sem, V.at("sum"))
                for n in range(2):
                    for k in range(KT):
                        mm = pe.matmul(PS[0:ENC, 1 + n, :], w_sum[:, k, :], fourier[:, k, 512 * n:512 * n + 512],
                                       start=k == 0, stop=k == KT - 1)
                mm.then_inc(PE.done("wave"), 1)

            @block.scalar
            def _(a):
                a.wait_ge(PE.sem, PE.at("wave"))
                a.activation(w_wave.rearrange("p (n w) -> p n w", n=2), PS[0:ENC, 1:3, :], ACT.Copy, scale=0.5
                             ).then_inc(AC.done("wave"), 1)

        for t in (V, AC, PE):
            t.close()
        V.layer([f"res{m}" for m in range(KT)])
        AC.layer(["enc"])
        PE.layer(["enc"] + [f"out{m}" for m in range(KT)])
        with nc.Block() as block:
            @block.vector
            def _(v):
                with v.Fori(0, NC) as c:
                    V.here = 0
                    n = c + (5 * NC + 1)
                    c1 = following(v, c)
                    ln_v1(v, n, h_chunk(c1))
                    ln_v2(v, n, h_chunk(c1))
                    for m in range(KT):
                        v.wait_ge(PE.sem, PE.at(f"out{m}", c))
                        v.scalar_tensor_tensor(out=h_tile(c, m), in0=PS[:, 2 + m % 4, 0:CT], scalar=bias("base2_b", m),
                                               in1=h_tile(c, m), op0=ALU.add, op1=ALU.add).then_inc(V.done(f"res{m}"), 1)
                        if m == 2:
                            ln_v3(v, n, sq2)
                        if m == 4:
                            ln_v4(v, n)
                    ln_v5(v, n, [(PE.sem, PE.at("out7", c))])

            @block.scalar
            def _(a):
                with a.Fori(0, NC) as c:
                    AC.here = 0
                    n = c + (5 * NC + 1)
                    a.wait_ge(PE.sem, PE.at("enc", c))
                    a.wait_ge(PE.sem, PE.prev("out7", c))
                    a.activation(enc_s, PS[0:ENC, 1, 0:CT], ACT.Copy).then_inc(AC.done("enc"), 1)
                    ln_a1(a, n, sq2)
                    ln_a2(a, n)

            @block.tensor
            def _(pe):
                with pe.Fori(0, NC) as c:
                    PE.here = 0
                    n = c + (5 * NC + 1)
                    pe.wait_ge(LV.sem, LV.at("out", n - 1))
                    pe.wait_ge(AC.sem, AC.prev("enc", c))
                    gemm(pe, PS[0:ENC, 1, 0:CT], lambda k: w_enc[:, k, :], range(KT)).then_inc(PE.done("enc"), 1)
                    for m in range(KT):
                        bank = PS[:, 2 + m % 4, 0:CT]
                        if m >= 4:
                            pe.wait_ge(V.sem, V.at(f"res{m - 4}", c))
                        else:
                            pe.wait_ge(V.sem, V.prev(f"res{m + 4}", c))
                        gemm(pe, bank, lambda k: w_base[:, k, m * P:m * P + P], range(KT), last=False)
                        if m == 0:
                            pe.wait_ge(AC.sem, AC.at("enc", c))
                        pe.matmul(bank, w_wave[:, m * P:m * P + P], enc_s, start=False, stop=True
                                  ).then_inc(PE.done(f"out{m}"), 1)
                        if m == 1:
                            ln_p1(pe, n)
                        if m == 4:
                            ln_p2(pe, n)

        for t in (V, AC, PE):
            t.close()
        if STOP_AFTER == 6:
            return finish()

        w_q = words(W_AT, KT, D)
        w_k = words(W_AT + KT * D, KT, 256)
        w_v7 = words(W_AT + KT * D + KT * 256, KT, 256)
        v7 = words(vb_at, CB, 256, rows=S)
        NQ7, NR7 = 12, 10
        V.layer([f"{x}{m}" for m in range(NR7) for x in ("rs", "rr")]
                + [x for g in range(GROUPS + LAG + 1) for x in
                   ([f"sum{g - 1}", f"rcp{g - 1}"] if 0 < g <= GROUPS else [])
                   + ([f"ctx{g - LAG - 1}"] if g > LAG else []) + ([f"max{g}", f"mask{g}"] if g < GROUPS else [])])
        AC.layer([f"ev{m}" for m in range(NQ7)] + ["vt0"] + [x for g in range(GROUPS + LAG)
                                                                       for x in probs_names(g)])
        G.layer([f"rc{m}" for m in range(NR7)] + [f"norm{g}" for g in range(GROUPS)])
        pe_names = []
        for m in range(NQ7 + 2):
            pe_names += ([f"qkv{m}"] if m < NQ7 else []) + ([f"rot{m - 2}"] if 2 <= m < NR7 + 2 else [])
        pe_names.append("Vt0")
        for g in range(GROUPS + LAG):
            pe_names += ([f"S{g}"] if g < GROUPS else []) + (value_names(g - LAG) if g >= LAG else [])
        PE.layer(pe_names)
        with nc.Block() as block:
            @block.sync
            def _(sp):
                sp.dma_start(w_q, T["q_w"].rearrange("p (k n) -> p k n", k=KT)).then_inc(w_in[6], 16)
                sp.dma_start(w_k, T["k_w"].rearrange("p (k n) -> p k n", k=KT)).then_inc(w_in[6], 16)
                sp.dma_start(w_v7, T["v_w"].rearrange("p (k n) -> p k n", k=KT)).then_inc(w_in[6], 16)

            @block.vector
            def _(v):
                with v.Fori(0, NC) as c:
                    V.here = 0
                    n = c + (6 * NC + 1)
                    c1 = following(v, c)
                    ln_v1(v, n, h_chunk(c1))
                    for m in range(NR7):
                        rope_v(v, c, m, (qT if m < KT else kT)[:, m % KT, :])
                        if m == 3:
                            ln_v2(v, n, h_chunk(c1))
                        if m == 6:
                            ln_v3(v, n, sq)
                        if m == 9:
                            ln_v4(v, n)
                            ln_v5(v, n, [(PE.sem, PE.at("qkv11", c))])
                    for g in range(GROUPS + LAG + 1):
                        if 0 < g <= GROUPS:
                            soft_sum(v, c, g - 1)
                        if g > LAG:
                            done = g - LAG - 1
                            b, half = done // 2, done % 2
                            dst = h_chunk(c)[:, half * 4:half * 4 + 4, b * S:(b + 1) * S]
                            v.wait_ge(PE.sem, PE.at(f"O{done}", c))
                            v.tensor_tensor(dst, PS[:, 7, 0:4 * S].rearrange("p (j t) -> p j t", j=4), dst, ALU.add
                                            ).then_inc(V.done(f"ctx{done}"), 1)
                        if g < GROUPS:
                            soft_top(v, c, g, False)

            @block.gpsimd
            def _(g):
                with g.Fori(0, NC) as c:
                    G.here = 0
                    for m in range(NR7):
                        rope_g(g, c, m, (qT if m < KT else kT)[:, m % KT, :])
                    for i in range(GROUPS):
                        soft_norm(g, c, i)

            @block.scalar
            def _(a):
                with a.Fori(0, NC) as c:
                    AC.here = 0
                    n = c + (6 * NC + 1)
                    for m in range(NQ7):
                        x, name, i = ((qT, "q_b", m) if m < KT else (kT, "k_b", m - KT) if m < NR7
                                      else (vT, "v_b", m - NR7))
                        a.wait_ge(PE.sem, PE.at(f"qkv{m}", c))
                        a.activation(x[:, i, :], PS[:, 1 + m % 4, 0:CT], ACT.Identity, bias=bias(name, i)
                                     ).then_inc(AC.done(f"ev{m}"), 1)
                        if m == 8:
                            ln_a1(a, n, sq)
                    a.wait_ge(PE.sem, PE.at("Vt0", c))
                    a.activation(v7.rearrange("p (n b) w -> p n (b w)", n=2), PS[0:S, 5:7, :], ACT.Copy
                                 ).then_inc(AC.done("vt0"), 1)
                    ln_a2(a, n)
                    for g in range(GROUPS + LAG):
                        probs_a(a, c, g, False)

            @block.tensor
            def _(pe):
                pe.wait_ge(w_in[6], 48)
                with pe.Fori(0, NC) as c:
                    PE.here = 0
                    n = c + (6 * NC + 1)
                    pe.wait_ge(LV.sem, LV.at("out", n - 1))
                    for m in range(NQ7 + 2):
                        if m < NQ7:
                            if m >= 4:
                                pe.wait_ge(AC.sem, AC.at(f"ev{m - 4}", c))
                            else:
                                pe.wait_ge(V.sem, V.prev("mask7", c))
                            w, i = (w_q, m) if m < KT else (w_k, m - KT) if m < NR7 else (w_v7, m - NR7)
                            gemm(pe, PS[:, 1 + m % 4, 0:CT], lambda k: w[:, k, i * P:i * P + P], range(KT)
                                 ).then_inc(PE.done(f"qkv{m}"), 1)
                        if m == 3:
                            ln_p1(pe, n)
                        if m == 10:
                            ln_p2(pe, n)
                        if 2 <= m < NR7 + 2:
                            rope_p(pe, c, m - 2, (qT if m - 2 < KT else kT)[:, (m - 2) % KT, :])
                    pe.wait_ge(V.sem, V.at("rr9", c))
                    pe.wait_ge(AC.sem, AC.at("ev11", c))
                    for b in range(CB):
                        for f in range(2):
                            o = (b % 2) * 256 + f * P
                            mm = pe.transpose(PS[0:S, 5 + b // 2, o:o + P], vT[:, f, b * S:(b + 1) * S], ident)
                    mm.then_inc(PE.done("Vt0"), 1)
                    for g in range(GROUPS + LAG):
                        if g < GROUPS:
                            scores_p(pe, c, g, True)
                        if g >= LAG:
                            values_p(pe, c, g - LAG,
                                     lambda u, j, q=g - LAG: v7[:, q // 2, (q % 2 * 4 + j) * HD:(q % 2 * 4 + j) * HD + HD],
                                     lambda u, j: PS[32 * u:32 * u + 32, 7, j * S:(j + 1) * S],
                                     V.sem, V.at(f"ctx{g - LAG - 1}", c) if g > LAG else V.prev("ctx7", c),
                                     lambda u, q=g: [(AC.sem, AC.at(f"pt{q - LAG - 1}_{2 + u}", c))] if q > LAG else
                                     [(AC.sem, AC.at("vt0", c))])

        for t in (V, AC, G, PE):
            t.close()
        if STOP_AFTER == 7:
            return finish()

        NJ = EXPERTS * MIXR // P
        o = W_AT
        w_base = words(o, KT, D)
        w_down = words(o + KT * D, KT, EXPERTS * MIXR)
        o += KT * D + KT * EXPERTS * MIXR
        w_up = words(o, NJ, D)
        w_key = words(o + NJ * D, KT, KEYS)
        keys = words(o + NJ * D + KT * KEYS, EXPERTS)
        o += NJ * D + KT * KEYS + EXPERTS
        x_sum = words(o, KT, CB)
        query = words(o + 32, CB)
        score = words(o + 36, EXPERTS, rows=CB)
        s_top, s_den = words(o + 44, 1, rows=CB), words(o + 45, 1, rows=CB)
        score_t = words(o + 46, CB, rows=EXPERTS)
        mix = words(o + 50, NJ, CB)
        wh = words(o + 66, NJ, CT)
        assert o + 66 + NJ * CT <= FREE_END
        V.layer(["xsum", "top", "off", "den", "rden", "coef"] + [f"wh{j}" for j in range(NJ)]
                + [f"res{m}" for m in range(KT)])
        AC.layer(["query", "exp", "turned", "mix"])
        order = [("query", 0), ("base", 0), ("score", 0), ("base", 1), ("down", 0), ("turn", 0), ("down", 1), ("mix", 0),
                 ("base", 2), ("down", 2), ("down", 3), ("base", 3)]
        for m in range(4, KT):
            order += [("up", m - 4), ("base", m)]
        order += [("up", m) for m in range(4, KT)]
        PE.layer([f"{x}{m}" for x, m in order])
        with nc.Block() as block:
            @block.sync
            def _(sp):
                for ap, name, k in ((w_key, "wq", KT), (w_base, "base3_w", KT), (w_down, "down", KT), (w_up, "up", NJ)):
                    sp.dma_start(ap, T[name].rearrange("p (k n) -> p k n", k=k)).then_inc(w_in[7], 16)
                sp.dma_start(keys, T["keys"]).then_inc(w_in[7], 16)
                with sp.Fori(0, NC) as c:
                    sp.wait_ge(V.sem, V.at("res7", c))
                    sp.dma_start(T["out"][bass.ds(c, 1)].rearrange("c p w -> p (c w)"),
                                 A[:, bass.ds(c * CW, CW)]).then_inc(out_done, 16)
                sp.wait_ge(out_done, 16 * NC)

            @block.vector
            def _(v):
                with v.Fori(0, NC) as c:
                    V.here = 0
                    n = c + (7 * NC + 1)
                    c1 = following(v, c)
                    v.wait_ge(LV.sem, LV.at("out", n - 1))
                    v.tensor_reduce(x_sum, xn.rearrange("p k (b s) -> p k b s", b=CB), AX.X, ALU.add
                                    ).then_inc(V.done("xsum"), 1)
                    ln_v1(v, n, h_chunk(c1))
                    v.wait_ge(PE.sem, PE.at("score0", c))
                    v.tensor_reduce(s_top, PS[0:CB, 1, 8:8 + EXPERTS], AX.X, ALU.max).then_inc(V.done("top"), 1)
                    own(v, V, c)
                    v.tensor_scalar(score, PS[0:CB, 1, 8:8 + EXPERTS], s_top, None, ALU.subtract).then_inc(V.done("off"), 1)
                    v.wait_ge(AC.sem, AC.at("exp", c))
                    v.tensor_reduce(s_den, score, AX.X, ALU.add).then_inc(V.done("den"), 1)
                    own(v, V, c)
                    v.reciprocal(s_den, s_den).then_inc(V.done("rden"), 1)
                    own(v, V, c)
                    v.tensor_scalar(score, score, s_den, None, ALU.mult).then_inc(V.done("coef"), 1)
                    ln_v2(v, n, h_chunk(c1))
                    v.wait_ge(AC.sem, AC.at("mix", c))
                    for j in range(NJ):
                        v.wait_ge(PE.sem, PE.at(f"down{j}", c))
                        v.tensor_tensor(wh[:, j, :].rearrange("p (b s) -> p b s", b=CB),
                                        PS[:, (2, 7)[j % 2], 0:CT].rearrange("p (b s) -> p b s", b=CB),
                                        mix[:, j, :].unsqueeze(2).broadcast_to([P, CB, S]), ALU.mult
                                        ).then_inc(V.done(f"wh{j}"), 1)
                    ln_v3(v, n, sq2)
                    for m in range(KT):
                        v.wait_ge(PE.sem, PE.at(f"up{m}", c))
                        v.tensor_tensor(h_tile(c, m), PS[:, 3 + m % 4, 0:CT], h_tile(c, m), ALU.add
                                        ).then_inc(V.done(f"res{m}"), 1)
                        if m == 3:
                            ln_v4(v, n)
                            ln_v5(v, n, [(PE.sem, PE.at("base7", c))])

            @block.scalar
            def _(a):
                with a.Fori(0, NC) as c:
                    AC.here = 0
                    n = c + (7 * NC + 1)
                    a.wait_ge(PE.sem, PE.at("query0", c))
                    a.activation(query, PS[:, 1, 0:CB], ACT.Copy, scale=1.0 / S).then_inc(AC.done("query"), 1)
                    a.wait_ge(V.sem, V.at("off", c))
                    a.activation(score, score, ACT.Exp, scale=float(KEYS) ** -0.5).then_inc(AC.done("exp"), 1)
                    a.wait_ge(PE.sem, PE.at("turn0", c))
                    a.activation(score_t, PS[0:EXPERTS, 1, 32:32 + CB], ACT.Copy).then_inc(AC.done("turned"), 1)
                    a.wait_ge(PE.sem, PE.at("mix0", c))
                    a.activation(mix, PS[:, 1, 64:64 + NJ * CB].rearrange("p (j b) -> p j b", j=NJ), ACT.Copy
                                 ).then_inc(AC.done("mix"), 1)
                    ln_a1(a, n, sq2)
                    ln_a2(a, n)

            @block.tensor
            def _(pe):
                pe.wait_ge(w_in[7], 80)
                with pe.Fori(0, NC) as c:
                    PE.here = 0
                    n = c + (7 * NC + 1)
                    pe.wait_ge(V.sem, V.at("xsum", c))
                    for what, m in order:
                        bank = PS[:, 3 + m % 4, 0:CT]
                        if what == "query":
                            pe.wait_ge(AC.sem, AC.prev("mix", c))
                            for k in range(KT):
                                mm = pe.matmul(PS[:, 1, 0:CB], w_key[:, k, :], x_sum[:, k, :], start=k == 0,
                                               stop=k == KT - 1)
                        elif what == "score":
                            pe.wait_ge(AC.sem, AC.at("query", c))
                            mm = pe.matmul(PS[0:CB, 1, 8:8 + EXPERTS], query, keys, start=True, stop=True)
                        elif what == "turn":
                            mm = pe.transpose(PS[0:EXPERTS, 1, 32:32 + CB], score, const("ident", CB)[:, 0:CB])
                        elif what == "mix":
                            pe.wait_ge(AC.sem, AC.at("turned", c))
                            for j in range(NJ):
                                mm = pe.matmul(PS[:, 1, 64 + CB * j:64 + CB * j + CB], const(f"mix{j}", EXPERTS), score_t,
                                               start=True, stop=True)
                        elif what == "down":
                            if m >= 2:
                                pe.wait_ge(V.sem, V.at(f"wh{m - 2}", c))
                            elif m == 1:
                                pe.wait_ge(V.sem, V.prev("wh3", c))
                            else:
                                pe.wait_ge(V.sem, V.at("coef", c))
                            mm = gemm(pe, PS[:, (2, 7)[m % 2], 0:CT], lambda k: w_down[:, k, m * P:m * P + P], range(KT))
                        elif what == "base":
                            if m >= 4:
                                pe.wait_ge(V.sem, V.at(f"res{m - 4}", c))
                            else:
                                pe.wait_ge(V.sem, V.prev(f"res{m + 4}", c))
                            mm = gemm(pe, bank, lambda k: w_base[:, k, m * P:m * P + P], range(KT), last=False)
                        else:
                            if m == 0:
                                pe.wait_ge(V.sem, V.at("wh3", c))
                            mm = gemm(pe, bank, lambda j: w_up[:, j, m * P:m * P + P], range(NJ), first=False, x=wh)
                        mm.then_inc(PE.done(f"{what}{m}"), 1)
                        if (what, m) == ("base", 1):
                            ln_p1(pe, n)
                        if (what, m) == ("up", 0):
                            ln_p2(pe, n)


def rows_first(w):
    k, n = w.shape
    return np.ascontiguousarray(w.reshape(k // P, P, n).transpose(1, 0, 2).reshape(P, -1))


def columns(b):
    return np.ascontiguousarray(b.reshape(-1, P).T)


def lay_out(i):
    x = i["x"]
    t = dict(const=CONST)
    t["x_re"] = np.tile(x[..., 0].transpose(2, 1, 0).reshape(STATES, -1), (2, 1))
    t["x_im"] = np.tile(x[..., 1].transpose(2, 1, 0).reshape(STATES, -1), (2, 1))
    t["abslog"] = np.tile(i["L0_tok_A_abslog"].T, (2, 1))
    t["phase"] = np.tile(i["L0_tok_A_phase"].T, (2, 1))
    t["cls"] = columns(i["cls_tok"].reshape(-1))
    t["qkv_w"] = rows_first(i["L0_attn_qkv_w"])
    t["qkv_b"] = columns(i["L0_attn_qkv_b"])
    t["out_w"] = rows_first(i["L0_attn_out_w"])
    t["out_b"] = columns(i["L0_attn_out_b"])
    t["base0_w"] = rows_first(i["L0_ffn_W_base"].T)
    t["base0_b"] = columns(i["L0_ffn_b_base"])
    t["router0"] = rows_first(i["L0_ffn_W_router"].T)
    t["a0"] = rows_first(i["L0_ffn_A_stack"].reshape(P, D).T)
    t["b0"] = i["L0_ffn_B_stack"].transpose(0, 2, 1).reshape(P, D)
    for n, k in (("q", "bv_q"), ("k", "bv_k"), ("v", "bv_v")):
        t[f"bind_{n}"] = i[f"L1_attn_{k}"]
    t["router1"] = rows_first(i["L1_ffn_route_w"].T)
    t["a1"] = rows_first(i["L1_ffn_A"].reshape(P, D).T)
    t["b1"] = i["L1_ffn_Bw"].transpose(0, 2, 1).reshape(P, D)
    t["a_log"] = rows_first(i["L2_attn_A_log"])
    t["skip"] = columns(i["L2_attn_D"])
    t["xproj"] = rows_first(i["L2_attn_x_proj_w"].T)
    t["dtw"] = i["L2_attn_dt_proj_w"].T
    t["dt_b"] = columns(i["L2_attn_dt_proj_b"])
    t["base2_w"] = rows_first(i["L2_ffn_W_base"].T)
    t["base2_b"] = columns(i["L2_ffn_b_base"])
    enc = np.concatenate([i["L2_ffn_enc0"], i["L2_ffn_enc1"]], 0)
    t["enc"] = rows_first(enc.T)
    coef = np.concatenate([i["L2_ffn_coefs0"], i["L2_ffn_coefs1"]], 2).transpose(1, 0, 2)
    mask = np.concatenate([i["L2_ffn_mask0"], i["L2_ffn_mask1"]], 2).transpose(1, 0, 2)
    t["coef"] = rows_first(coef.reshape(D, -1))
    t["mask"] = rows_first(mask.reshape(D, -1)).view(np.int32)
    t["fourier"] = rows_first(FOURIER)
    order = np.array([(4 * (4 * (t8 // 4) + j) + t8 % 4) * HD + d
                      for t8 in range(8) for j in range(4) for d in range(HD)])
    t["q_w"] = rows_first(i["L3_attn_wq"][:, order])
    t["q_b"] = columns(i["L3_attn_bq"][order])
    t["k_w"] = rows_first(i["L3_attn_wk"])
    t["k_b"] = columns(i["L3_attn_bk"])
    t["v_w"] = rows_first(i["L3_attn_wv"])
    t["v_b"] = columns(i["L3_attn_bv"])
    t["base3_w"] = rows_first(i["L3_ffn_W_org"].T)
    t["down"] = rows_first(i["L3_ffn_lora_down"].transpose(1, 0, 2).reshape(D, EXPERTS * MIXR))
    t["up"] = rows_first(i["L3_ffn_lora_up"].reshape(EXPERTS * MIXR, D))
    t["keys"] = i["L3_ffn_lora_keys"].T
    t["wq"] = rows_first(i["L3_ffn_Wq"].T)
    return {k: np.ascontiguousarray(v) for k, v in t.items()}


def fourier_matrix():
    t, n = np.arange(D, dtype=np.float64), D
    f = np.zeros((D, D))
    f[0] = 1.0 / np.sqrt(n)
    pair = np.sqrt(n / 2.0) * 2.0 / n
    for k in range(1, (n - 1) // 2 + 1):
        f[2 * k - 1] = pair * np.cos(2 * np.pi * k * t / n)
        f[2 * k] = pair * np.sin(2 * np.pi * k * t / n)
    f[n - 1] = np.sqrt(n) / n * (-1.0) ** t
    return f.astype(np.float32)


FOURIER = fourier_matrix()


def kernel(**inputs):
    import concourse.bacc as _bacc
    from concourse.bass_utils import run_bass_kernel_spmd as _run

    nc = _bacc.Bacc("TRN2", target_bir_lowering=False, num_devices=1, dynamic_dma_scratch_size=1024)
    arrays = {f"in_{k}": v for k, v in lay_out({k: np.asarray(v) for k, v in inputs.items()}).items()}
    tensors = {k[3:]: nc.dram_tensor(k, a.shape, mybir.dt.from_np(a.dtype), kind="ExternalInput").ap()
               for k, a in arrays.items()}
    tensors["out"] = nc.dram_tensor("out_h", (NC, P, CW), F32, kind="ExternalOutput").ap()
    build(nc, tensors)
    r = _run(nc, [arrays], core_ids=[0])
    h = r.results[0]["out_h"].reshape(NC, P, KT, CB, S)
    return np.ascontiguousarray(h.transpose(0, 3, 4, 2, 1).reshape(IMAGES, S, D))
```

```python
from contextlib import ExitStack

import numpy as np

import concourse.bass as bass
from concourse import mybir

F32 = mybir.dt.float32
U8 = mybir.dt.uint8
BF16 = mybir.dt.bfloat16
ALU = mybir.AluOpType
ACT = mybir.ActivationFunctionType
AX = mybir.AxisListType

P = 128
IMAGES, GRID, STATES = 32, 64, 64
S = GRID + 1
D = 1024
KT = D // P
CB = 4
CT = CB * S
NC = IMAGES // CB
CW = KT * CT
HEADS, HD = 32, 32
EPS = 1e-5
EXPERTS, RANK = 8, 16
SSM, DTR = 16, 32
ENC = 40
MIXR = 64
KEYS = 128
HDH = 4
LAYERS = 8

MAGIC = 12582912.0
TWO_PI = 6.283185307179586
PI_HEAD = 6.28125
PI_MID = 0.0019350051879882812
PI_TAIL = TWO_PI - PI_HEAD - PI_MID
SIN_MAX = 3.1415925
TOK_ANG1, TOK_ANG2, N_TOK_V = 7, 46, 76


class Steps:

    def __init__(self, sem):
        self.sem, self.base, self.names, self.here = sem, 0, [], 0

    def layer(self, names, rounds=NC):
        self.names, self.rounds, self.here = list(names), rounds, 0
        assert len(set(self.names)) == len(self.names)

    def at(self, name, c=0):
        return c * len(self.names) + (self.base + self.names.index(name) + 1)

    def prev(self, name, c):
        return c * len(self.names) + (self.base + self.names.index(name) + 1 - len(self.names))

    def own(self, c=0):
        return c * len(self.names) + (self.base + self.here)

    def done(self, name):
        assert self.names[self.here] == name, (self.names[self.here], name)
        self.here += 1
        return self.sem

    def close(self):
        assert self.here == len(self.names), (self.here, self.names)
        self.base += self.rounds * len(self.names)
        self.names, self.here = [], 0


def constant_table():
    parts, at = [], {}

    def put(name, a):
        a = np.asarray(a, np.float32)
        full = np.zeros((P, a.shape[1]), np.float32)
        full[:a.shape[0]] = a
        at[name] = (sum(p.shape[1] for p in parts), a.shape[1])
        parts.append(full)

    p = np.arange(P)
    put("ident", np.eye(P))
    put("mean", np.full((P, P), 1.0 / D))
    rot = np.zeros((P, P))
    for i in range(P):
        if i % HD < HD // 2:
            rot[i + HD // 2, i] = -1.0
        else:
            rot[i - HD // 2, i] = 1.0
    put("rotate", rot)
    half = HD // 2
    freq = (1.0 / np.float32(10000.0) ** (np.arange(half, dtype=np.float32) / half)).astype(np.float32)
    angle = (np.arange(S, dtype=np.float32)[None, :] * freq[p % half][:, None]).astype(np.float64)
    scale = 1.0 / np.sqrt(HD)
    put("cos_k", np.cos(angle))
    put("sin_k", np.sin(angle))
    put("cos_q", np.cos(angle) * scale)
    put("sin_q", np.sin(angle) * scale)
    s = np.arange(S)
    put("causal", np.where(s[None, :] > s[:, None], -66504.0, 0.0))
    put("causal_t", s[:, None] <= s[None, :])
    e = np.arange(EXPERTS)
    put("earlier", np.tile((e[None, :] < e[:, None]).reshape(1, -1), (P, 1)))
    put("spread2", (e[:, None] == (p // RANK)[None, :]) * 2.0)
    put("spread1", e[:, None] == (p // RANK)[None, :])
    for j in range(EXPERTS * MIXR // P):
        put(f"mix{j}", e[:, None] == (p // MIXR + j * (P // MIXR))[None, :])
    put("upper", (p < STATES)[:, None])
    put("lower", (p >= STATES)[:, None])
    put("shift", np.where(p < STATES, np.pi / 2, 0.0)[:, None])
    put("turn", np.where(p < STATES, 0.25, 0.0)[:, None])
    put("eps", np.full((P, 1), EPS))
    put("count", np.tile(np.arange(P), (P, 1)))
    return np.concatenate(parts, 1), at


CONST, CONST_AT = constant_table()

H_AT = 0
C_AT = H_AT + NC * CW
B_AT = C_AT + CONST.shape[1]
BIAS_NAMES = dict(qkv_b=24, out_b=8, base0_b=8, dt_b=8, skip=8, base2_b=8, q_b=8, k_b=2, v_b=2, cls=8)
BIAS_AT, _n = {}, 0
for _k, _v in BIAS_NAMES.items():
    BIAS_AT[_k] = (_n, _v)
    _n += _v
BIAS_W = _n
BIND_AT = B_AT + BIAS_W
LN_AT = BIND_AT + 24
XS_AT = LN_AT + 5 * CT + 2 * CW
W_AT = XS_AT + CW
WORDS = 57040
STOP_AFTER = LAYERS


def build(nc, T):
    ctx = ExitStack()
    with ctx:
        A = ctx.enter_context(nc.sbuf_tensor("arena", [P, WORDS], F32))
        PS = ctx.enter_context(nc.psum_tensor("banks", [P, 8, 512], F32))
        hD = nc.dram_tensor("h_scratch", (NC, P, CW), F32, kind="Internal").ap()
        bcD = nc.dram_tensor("bc_scratch", (2 * SSM, CT), F32, kind="Internal").ap()

        def sem(name):
            return ctx.enter_context(nc.semaphore(name))

        V = Steps(sem("vector_steps"))
        AC = Steps(sem("scalar_steps"))
        G = Steps(sem("gpsimd_steps"))
        PE = Steps(sem("tensor_steps"))
        LV = Steps(sem("layernorm_vector_steps"))
        LA = Steps(sem("layernorm_scalar_steps"))
        LP = Steps(sem("layernorm_tensor_steps"))
        ln_rounds = 1 + LAYERS * NC
        LV.layer(["sum", "center", "sumsq", "n1", "n2", "n3", "out"], ln_rounds)
        LA.layer(["square", "log", "seed"], ln_rounds)
        LP.layer(["mean", "var"], ln_rounds)
        consts_in = sem("constants_loaded")
        tok_in = sem("token_inputs_loaded")
        h_out = sem("h_stored")
        h_in = sem("h_loaded")
        w_in = [sem(f"weights_loaded_{i}") for i in range(LAYERS)]
        lora_in = sem("lora_weights_loaded")
        h_back = sem("h_back_loaded")
        h_last = sem("h_last_chunk_moved")
        bc_out = sem("bc_stored")
        bc_in = sem("bc_loaded")
        out_done = sem("output_stored")

        def const(name, rows=P):
            o, w = CONST_AT[name]
            return A[0:rows, C_AT + o:C_AT + o + w]

        def bias(name, i):
            o = B_AT + BIAS_AT[name][0] + i
            return A[:, o:o + 1]

        def words(at, *shape, rows=P):
            n = int(np.prod(shape))
            v = A[0:rows, at:at + n]
            if len(shape) == 2:
                return v.rearrange("p (a b) -> p a b", a=shape[0])
            if len(shape) == 3:
                return v.rearrange("p (a b c) -> p a b c", a=shape[0], b=shape[1])
            return v

        ident, mean_w = const("ident"), const("mean")

        s1 = words(LN_AT, CT)
        s2 = words(LN_AT + CT, CT)
        lv = words(LN_AT + 2 * CT, CT)
        rs = words(LN_AT + 3 * CT, CT)
        nt = words(LN_AT + 4 * CT, CT)
        xc_at = LN_AT + 5 * CT
        xn_at = xc_at + CW
        xc = words(xc_at, KT, CT)
        xn = words(xn_at, KT, CT)
        mean_ps = PS[:, 0, 0:CT]

        def parts(at, k, n):
            return A[:, at:at + k * n].bitcast(BF16).rearrange("p (k two n) -> p k two n", k=k, two=2)

        XS1_AT = WORDS - 2 * CW
        xs = [A[:, at:at + CW].bitcast(BF16).rearrange("p (two k t) -> p two k t", two=2, k=KT)
              for at in (XS_AT, XS1_AT)]

        def over_tiles(ap2):
            return ap2.unsqueeze(1).broadcast_to([P, KT, CT])

        def h_chunk(c):
            return A[:, bass.ds(c * CW, CW)].rearrange("p (k t) -> p k t", k=KT)

        def h_tile(c, m):
            return A[:, bass.ds(c * CW + m * CT, CT)]

        def ln_v1(v, n, src):
            LV.here = 0
            if not (isinstance(n, int) and n == 0):
                v.wait_ge(LP.sem, LP.at("var", n) - 2)
            v.tensor_reduce(s1, src.rearrange("p k t -> p t k"), AX.X, ALU.add).then_inc(LV.done("sum"), 1)

        def ln_v2(v, n, src):
            v.wait_ge(LP.sem, LP.at("mean", n))
            v.tensor_tensor(xc, src, over_tiles(mean_ps), ALU.subtract).then_inc(LV.done("center"), 1)

        def ln_v3(v, n, sq):
            v.wait_ge(LA.sem, LA.at("square", n))
            v.tensor_reduce(s2, sq.rearrange("p k t -> p t k"), AX.X, ALU.add).then_inc(LV.done("sumsq"), 1)

        def ln_v4(v, n):
            v.wait_ge(LA.sem, LA.at("seed", n))
            v.scalar_tensor_tensor(out=nt, in0=mean_ps, scalar=EPS, in1=rs, op0=ALU.add, op1=ALU.mult
                                   ).then_inc(LV.done("n1"), 1)
            v.wait_ge(LV.sem, LV.own(n))
            v.scalar_tensor_tensor(out=nt, in0=nt, scalar=-0.5, in1=rs, op0=ALU.mult, op1=ALU.mult
                                   ).then_inc(LV.done("n2"), 1)
            v.wait_ge(LV.sem, LV.own(n))
            v.scalar_tensor_tensor(out=rs, in0=nt, scalar=1.5, in1=rs, op0=ALU.add, op1=ALU.mult
                                   ).then_inc(LV.done("n3"), 1)

        def ln_v5(v, n, read=()):
            for s, at in read:
                v.wait_ge(s, at)
            v.wait_ge(LV.sem, LV.own(n))
            v.tensor_tensor(xn, xc, over_tiles(rs), ALU.mult).then_inc(LV.done("out"), 1)

        def ln_a1(a, n, sq):
            LA.here = 0
            a.wait_ge(LV.sem, LV.at("center", n))
            a.activation(sq, xc, ACT.Square).then_inc(LA.done("square"), 1)

        def ln_a2(a, n):
            a.wait_ge(LP.sem, LP.at("var", n))
            a.activation(lv, mean_ps, ACT.Ln, bias=const("eps")).then_inc(LA.done("log"), 1)
            a.wait_ge(LA.sem, LA.own(n))
            a.wait_ge(LV.sem, LV.at("center", n))
            a.activation(rs, lv, ACT.Exp, scale=-0.5).then_inc(LA.done("seed"), 1)

        def ln_p1(pe, n):
            LP.here = 0
            pe.wait_ge(LV.sem, LV.at("sum", n))
            pe.matmul(mean_ps, mean_w, s1, start=True, stop=True).then_inc(LP.done("mean"), 1)

        def ln_p2(pe, n):
            pe.wait_ge(LV.sem, LV.at("sumsq", n))
            pe.matmul(mean_ps, mean_w, s2, start=True, stop=True).then_inc(LP.done("var"), 1)

        def gemm(pe, out, w_of, kts, first=True, last=True, x=xn):
            for i, k in enumerate(kts):
                mm = pe.matmul(out, w_of(k), x[:, k, :], start=first and i == 0,
                               stop=last and i == len(kts) - 1)
            return mm


        def gemm3(pe, out, w_of, x_of, kts=KT, first=True, last=True):
            for k in range(kts):
                pe.matmul(out, w_of(k, 0), x_of(k, 0), start=first and k == 0, stop=False)
                pe.matmul(out, w_of(k, 0), x_of(k, 1), start=False, stop=False)
                mm = pe.matmul(out, w_of(k, 1), x_of(k, 0), start=False, stop=last and k == kts - 1)
            return mm

        def of_xs(slot):
            return lambda k, part: xs[slot][:, part, k, :]

        SX = Steps(sem("split_steps"))

        def split_xn(v, n, n_ln, slot=0):
            SX.here = 0
            v.wait_ge(LV.sem, LV.at("out", n_ln))
            v.tensor_copy(xs[slot][:, 0], xn).then_inc(SX.done("hi"), 1)
            v.wait_ge(SX.sem, SX.own(n))
            v.tensor_tensor(xs[slot][:, 1], xn, xs[slot][:, 0], ALU.subtract).then_inc(SX.done("lo"), 1)

        WA = Steps(sem("weight_high_steps"))
        WV = Steps(sem("weight_rest_steps"))
        SLOTS = 3
        stage_in = [sem(f"weights_staged_{i}") for i in range(SLOTS)]
        STAGE_AT = W_AT + 2 * KT * D
        STAGE_W = 2 * D
        staged = [0] * SLOTS

        def stage(u, nk, n, at):
            return words(at + u % SLOTS * STAGE_W, nk, n)

        def units_of(dst, src, n, per, at=STAGE_AT):
            out, kts = [], dst.shape[1]
            for k in range(0, kts, per):
                nk = min(per, kts - k)
                out.append((dst[:, k:k + nk], src[:, k:k + nk], nk, n, at))
            return out

        def stage_sp(sp, u, unit):
            dst, src, *where = unit
            if u >= SLOTS:
                sp.wait_ge(WV.sem, WV.at(f"lo{u - SLOTS}"))
            sp.dma_start(stage(u, *where), src).then_inc(stage_in[u % SLOTS], 16)

        def split_a(a, u, unit):
            dst, src, *where = unit
            a.wait_ge(stage_in[u % SLOTS], 16 * (staged[u % SLOTS] + u // SLOTS + 1))
            a.activation(dst[:, :, 0, :], stage(u, *where), ACT.Copy).then_inc(WA.done(f"hi{u}"), 1)

        def split_v(v, u, unit):
            dst, src, *where = unit
            v.wait_ge(WA.sem, WA.at(f"hi{u}"))
            v.tensor_tensor(dst[:, :, 1, :], stage(u, *where), dst[:, :, 0, :], ALU.subtract
                            ).then_inc(WV.done(f"lo{u}"), 1)

        def own(e, steps, c=0):
            e.wait_ge(steps.sem, steps.own(c))

        TOK = xc_at
        NA = D // P
        e1 = words(TOK, GRID, P)
        ang = words(TOK + 8192, GRID, P)
        kk = words(TOK + 16384, GRID, P)
        al, th = words(TOK + 24576, GRID), words(TOK + 24640, GRID)
        cr = words(TOK + 24704, GRID, IMAGES)
        ci = words(TOK + 26752, GRID, IMAGES)
        small = [words(TOK + 28800 + 512 * i, GRID, NA) for i in range(10)]
        col = [words(TOK + 33920 + GRID * i, GRID) for i in range(9)]
        assert TOK + 33920 + 9 * GRID <= WORDS
        HG = 8
        g_re = [words(TOK + 8192 + i * 2048, HG, IMAGES, NA) for i in range(2)]
        g_im = [words(TOK + 8192 + (2 + i) * 2048, HG, IMAGES, NA) for i in range(2)]
        hT = words(H_AT, NC, KT, CT)
        zero = words(LN_AT, 8)

        V.layer([f"v{i}" for i in range(N_TOK_V)] + [f"{x}{i}" for i in range(GRID // HG) for x in ("gre", "g")]
                + ["cls"], 1)
        AC.layer(["sin1", "exp1", "sin2r", "sin2i", "sinA", "cosA", "exp2", "expA"]
                 + [f"put{i}" for i in range(GRID)], 1)
        G.layer(["scaled", "e1"] + [f"gim{i}" for i in range(GRID // HG)], 1)
        PE.layer([f"tok{i}" for i in range(GRID)], 1)

        with nc.Block() as block:
            @block.sync
            def _(sp):
                sp.dma_start(A[:, C_AT:C_AT + CONST.shape[1]], T["const"]).then_inc(consts_in, 16)
                for name, (o, w) in BIAS_AT.items():
                    sp.dma_start(A[:, B_AT + o:B_AT + o + w], T[name]).then_inc(consts_in, 16)
                for ap, name in ((al, "abslog"), (th, "phase")):
                    sp.dma_start(ap, T[name]).then_inc(tok_in, 16)
                for ap, name in ((cr, "x_re"), (ci, "x_im")):
                    sp.dma_start(ap, T[name].rearrange("p (a b) -> p a b", a=GRID)).then_inc(tok_in, 16)

            @block.vector
            def _(v):
                n = [0]

                def step(make):
                    own(v, V)
                    make().then_inc(V.done(f"v{n[0]}"), 1)
                    n[0] += 1

                def reduce_angle(x, k, turn, shift):
                    step(lambda: v.tensor_scalar(k, x, 1.0 / TWO_PI, turn, ALU.mult, ALU.add))
                    step(lambda: v.tensor_scalar(k, k, MAGIC, MAGIC, ALU.add, ALU.subtract))
                    for part in (PI_HEAD, PI_MID, PI_TAIL):
                        step(lambda: v.scalar_tensor_tensor(out=x, in0=k, scalar=-part, in1=x,
                                                            op0=ALU.mult, op1=ALU.add))
                    step(lambda: v.tensor_scalar(x, x, shift, SIN_MAX, ALU.add, ALU.min))
                    step(lambda: v.tensor_scalar(x, x, -SIN_MAX, None, ALU.max))

                v.wait_ge(consts_in, 16 * (1 + len(BIAS_AT)))
                v.wait_ge(tok_in, 16 * 4)
                parts = const("count").unsqueeze(1).broadcast_to([P, GRID, P])
                blocks = const("count")[:, 0:NA].unsqueeze(1).broadcast_to([P, GRID, NA])
                wide = lambda x, w: x.unsqueeze(2).broadcast_to([P, GRID, w])
                v.tensor_tensor(ang, wide(th, P), parts, ALU.mult).then_inc(V.done("v0"), 1)
                n[0] = 1
                reduce_angle(ang, kk, const("turn"), const("shift"))
                i_ang = n[0]
                t128, k128, a2, k2, a2c, m2, cosA, sinA, x2, y2 = small
                step(lambda: v.tensor_scalar(col[0], th, 128.0, None, ALU.mult))
                step(lambda: v.tensor_scalar(col[1], col[0], 1.0 / TWO_PI, None, ALU.mult))
                step(lambda: v.tensor_scalar(col[1], col[1], MAGIC, MAGIC, ALU.add, ALU.subtract))
                for part in (PI_HEAD, PI_MID, PI_TAIL):
                    step(lambda: v.scalar_tensor_tensor(out=col[0], in0=col[1], scalar=-part, in1=col[0],
                                                        op0=ALU.mult, op1=ALU.add))
                step(lambda: v.tensor_tensor(a2, wide(col[0], NA), blocks, ALU.mult))
                step(lambda: v.tensor_copy(a2c, a2))
                reduce_angle(a2, k2, 0.0, 0.0)
                reduce_angle(a2c, k2, 0.25, np.pi / 2)
                step(lambda: v.tensor_tensor(m2, wide(al, NA), blocks, ALU.mult))
                step(lambda: v.tensor_copy(col[2], th))
                step(lambda: v.tensor_copy(col[3], th))
                sub = [x.unsqueeze(2) for x in (col[2], col[3], col[4])]
                reduce_angle(sub[0], sub[2], 0.0, 0.0)
                reduce_angle(sub[1], sub[2], 0.25, np.pi / 2)
                assert (i_ang - 1, n[0] - 1) == (TOK_ANG1, TOK_ANG2), (i_ang, n[0])
                v.wait_ge(AC.sem, AC.at("expA"))
                sA, cA, eA = col[5], col[6], col[7]
                step(lambda: v.tensor_tensor(sA, sA, eA, ALU.mult))
                step(lambda: v.tensor_tensor(cA, cA, eA, ALU.mult))
                step(lambda: v.tensor_scalar(cA, cA, 1.0, None, ALU.subtract))
                step(lambda: v.tensor_tensor(col[0], al, al, ALU.mult))
                step(lambda: v.tensor_tensor(col[1], th, th, ALU.mult))
                step(lambda: v.tensor_tensor(col[0], col[0], col[1], ALU.add))
                step(lambda: v.reciprocal(col[0], col[0]))
                fr, fi = col[2], col[3]
                step(lambda: v.tensor_tensor(fr, cA, al, ALU.mult))
                step(lambda: v.tensor_tensor(col[1], sA, th, ALU.mult))
                step(lambda: v.tensor_tensor(fr, fr, col[1], ALU.add))
                step(lambda: v.tensor_tensor(fr, fr, col[0], ALU.mult))
                step(lambda: v.tensor_tensor(fi, sA, al, ALU.mult))
                step(lambda: v.tensor_tensor(col[1], cA, th, ALU.mult))
                step(lambda: v.tensor_tensor(fi, fi, col[1], ALU.subtract))
                step(lambda: v.tensor_tensor(fi, fi, col[0], ALU.mult))
                step(lambda: v.tensor_tensor(cosA, cosA, m2, ALU.mult))
                step(lambda: v.tensor_tensor(sinA, sinA, m2, ALU.mult))
                step(lambda: v.tensor_tensor(x2, cosA, wide(fr, NA), ALU.mult))
                step(lambda: v.tensor_tensor(k2, sinA, wide(fi, NA), ALU.mult))
                step(lambda: v.tensor_tensor(x2, x2, k2, ALU.subtract))
                step(lambda: v.tensor_tensor(y2, sinA, wide(fr, NA), ALU.mult))
                step(lambda: v.tensor_tensor(k2, cosA, wide(fi, NA), ALU.mult))
                step(lambda: v.tensor_tensor(y2, y2, k2, ALU.add))
                u_re, u_im = a2, a2c
                step(lambda: v.tensor_scalar(u_re, x2, const("upper"), 2.0, ALU.mult, ALU.mult))
                step(lambda: v.tensor_scalar(k2, y2, const("lower"), -2.0, ALU.mult, ALU.mult))
                step(lambda: v.tensor_tensor(u_re, u_re, k2, ALU.add))
                step(lambda: v.tensor_scalar(u_im, y2, const("upper"), -2.0, ALU.mult, ALU.mult))
                step(lambda: v.tensor_scalar(k2, x2, const("lower"), -2.0, ALU.mult, ALU.mult))
                step(lambda: v.tensor_tensor(u_im, u_im, k2, ALU.add))
                assert n[0] == N_TOK_V, n[0]
                for i in range(GRID // HG):
                    if i == 0:
                        v.wait_ge(G.sem, G.at("e1"))
                    else:
                        own(v, V)
                    if i >= 2:
                        v.wait_ge(PE.sem, PE.at(f"tok{HG * (i - 1) - 1}"))
                    v.tensor_tensor(g_re[i % 2], cr[:, HG * i:HG * i + HG, :].unsqueeze(3).broadcast_to([P, HG, IMAGES, NA]),
                                    u_re[:, HG * i:HG * i + HG, :].unsqueeze(2).broadcast_to([P, HG, IMAGES, NA]),
                                    ALU.mult).then_inc(V.done(f"gre{i}"), 1)
                    own(v, V)
                    v.wait_ge(G.sem, G.at(f"gim{i}"))
                    v.tensor_tensor(g_re[i % 2], g_re[i % 2], g_im[i % 2], ALU.add).then_inc(V.done(f"g{i}"), 1)
                first = hT.rearrange("p c k (b s) -> p c k b s", b=CB)[:, :, :, :, 0]
                own(v, V)
                v.tensor_copy(first.rearrange("p c k b -> p k c b"),
                              A[:, B_AT + BIAS_AT["cls"][0]:B_AT + BIAS_AT["cls"][0] + KT].unsqueeze(2).unsqueeze(3)
                              .broadcast_to([P, KT, NC, CB])).then_inc(V.done("cls"), 1)

            @block.gpsimd
            def _(g):
                g.wait_ge(consts_in, 16 * (1 + len(BIAS_AT)))
                g.wait_ge(tok_in, 16 * 4)
                g.wait_ge(V.sem, V.at(f"v{TOK_ANG1}"))
                g.tensor_tensor(kk, al.unsqueeze(2).broadcast_to([P, GRID, P]),
                                const("count").unsqueeze(1).broadcast_to([P, GRID, P]),
                                ALU.mult).then_inc(G.done("scaled"), 1)
                g.wait_ge(AC.sem, AC.at("exp1"))
                g.tensor_tensor(e1, kk, ang, ALU.mult).then_inc(G.done("e1"), 1)
                g.wait_ge(G.sem, G.own())
                for i in range(GRID // HG):
                    if i == 0:
                        g.wait_ge(V.sem, V.at(f"v{N_TOK_V - 1}"))
                    if i >= 2:
                        g.wait_ge(V.sem, V.at(f"g{i - 2}"))
                    g.tensor_tensor(g_im[i % 2], ci[:, HG * i:HG * i + HG, :].unsqueeze(3).broadcast_to([P, HG, IMAGES, NA]),
                                    small[4][:, HG * i:HG * i + HG, :].unsqueeze(2).broadcast_to([P, HG, IMAGES, NA]),
                                    ALU.mult).then_inc(G.done(f"gim{i}"), 1)

            @block.scalar
            def _(a):
                t128, k128, a2, k2, a2c, m2, cosA, sinA, x2, y2 = small
                a.wait_ge(V.sem, V.at(f"v{TOK_ANG1}"))
                a.activation(ang, ang, ACT.Sin).then_inc(AC.done("sin1"), 1)
                a.wait_ge(G.sem, G.at("scaled"))
                a.activation(kk, kk, ACT.Exp).then_inc(AC.done("exp1"), 1)
                a.wait_ge(V.sem, V.at(f"v{TOK_ANG2}"))
                a.activation(sinA, a2, ACT.Sin).then_inc(AC.done("sin2r"), 1)
                a.activation(cosA, a2c, ACT.Sin).then_inc(AC.done("sin2i"), 1)
                a.activation(col[5], col[2], ACT.Sin).then_inc(AC.done("sinA"), 1)
                a.activation(col[6], col[3], ACT.Sin).then_inc(AC.done("cosA"), 1)
                a.activation(m2, m2, ACT.Exp, scale=128.0).then_inc(AC.done("exp2"), 1)
                a.activation(col[7], al, ACT.Exp).then_inc(AC.done("expA"), 1)
                for hh in range(GRID):
                    a.wait_ge(PE.sem, PE.at(f"tok{hh}"))
                    dst = hT.rearrange("p c k (b s) -> p c k b s", b=CB)[:, :, :, :, 1 + hh]
                    a.activation(dst.rearrange("p c k b -> p c b k"),
                                 PS[:, hh % 8, 0:IMAGES * NA].rearrange("p (c b k) -> p c b k", c=NC, b=CB),
                                 ACT.Copy).then_inc(AC.done(f"put{hh}"), 1)

            @block.tensor
            def _(pe):
                pe.wait_ge(G.sem, G.at("e1"))
                for hh in range(GRID):
                    if hh % HG == 0:
                        pe.wait_ge(V.sem, V.at(f"g{hh // HG}"))
                    if hh >= 8:
                        pe.wait_ge(AC.sem, AC.at(f"put{hh - 8}"))
                    pe.matmul(PS[:, hh % 8, 0:IMAGES * NA], e1[:, hh, :],
                              g_re[hh // HG % 2][:, hh % HG].rearrange("p b k -> p (b k)"), start=True, stop=True
                              ).then_inc(PE.done(f"tok{hh}"), 1)

        for t in (V, AC, G, PE):
            t.close()

        def finish(extra=()):
            with nc.Block() as block:
                @block.sync
                def _(sp):
                    for s, at in extra:
                        sp.wait_ge(s, at)
                    sp.dma_start(T["out"].rearrange("c p w -> p c w"),
                                 A[:, 0:NC * CW].rearrange("p (c w) -> p c w", c=NC)).then_inc(out_done, 16)
                    sp.wait_ge(out_done, 16)

        if STOP_AFTER == 0:
            return finish()

        GROUPS = 2 * CB
        GH, QT = HEADS // 2, 4
        qT = words(W_AT + 2 * KT * D, KT, CT)
        kT = words(W_AT + 2 * KT * D + CW, KT, CT)
        q_s = parts(W_AT + 2 * KT * D, KT, CT)
        k_s = parts(W_AT + 2 * KT * D + CW, KT, CT)
        vT_at = W_AT + 2 * KT * D + 2 * CW
        vT = words(vT_at, KT, CT)
        hbuf_at = vT_at + CW
        hbuf = words(hbuf_at, KT, CT)
        vb_at = hbuf_at + CW
        s_at = vb_at + 2 * D
        assert 2 * GH * S >= CW and SLOTS * STAGE_W <= 3 * CW
        sq = words(s_at, KT, CT)
        pt_at = s_at + 2 * GH * S
        pt_buf = [words(pt_at + i * QT * S, QT * S, rows=S) for i in range(2)]
        rt_at = pt_at + 2 * QT * S
        turned = [words(rt_at + i * CT, CT) for i in range(4)]
        SB = 3
        s_buf = [words((s_at, s_at + GH * S, rt_at)[i], QT, QT, S, rows=S) for i in range(SB)]
        mx = [words(rt_at + 4 * CT + 16 * i, GH, rows=S) for i in range(SB)]
        rsum = [words(rt_at + 4 * CT + 16 * (SB + i), GH, rows=S) for i in range(SB)]
        assert GH * S <= 4 * CT and rt_at + 4 * CT + 32 * SB <= WORDS
        s_ps = PS[0:S, 1:5, 0:QT * S].rearrange("p j (m k) -> p j m k", m=QT)

        def heads16(x):
            return x.rearrange("p (j m) -> p j m", j=QT).unsqueeze(3).broadcast_to([S, QT, QT, S])

        def rope_v(v, c, m):
            v.wait_ge(PE.sem, PE.at(f"rot{m}", c))
            sin = const("sin_q" if m < KT else "sin_k")
            v.tensor_tensor(turned[2 + m % 2].rearrange("p (b s) -> p b s", b=CB),
                            PS[:, 5 + m % 2, 0:CT].rearrange("p (b s) -> p b s", b=CB),
                            sin.unsqueeze(1).broadcast_to([P, CB, S]), ALU.mult).then_inc(V.done(f"rs{m}"), 1)
            own(v, V, c)
            v.wait_ge(G.sem, G.at(f"rc{m}", c))
            v.tensor_tensor(turned[m % 2], turned[m % 2], turned[2 + m % 2], ALU.add).then_inc(V.done(f"rr{m}"), 1)
            dst = (q_s if m < KT else k_s)[:, m % KT]
            own(v, V, c)
            v.tensor_copy(dst[:, 0], turned[m % 2]).then_inc(V.done(f"rh{m}"), 1)
            own(v, V, c)
            v.tensor_tensor(dst[:, 1], turned[m % 2], dst[:, 0], ALU.subtract).then_inc(V.done(f"rl{m}"), 1)

        def rope_g(g, c, m, x):
            g.wait_ge(AC.sem, AC.at(f"ev{m}", c))
            if m >= 2:
                g.wait_ge(V.sem, V.at(f"rl{m - 2}", c))
            cos = const("cos_q" if m < KT else "cos_k")
            g.tensor_tensor(turned[m % 2].rearrange("p (b s) -> p b s", b=CB),
                            x.rearrange("p (b s) -> p b s", b=CB),
                            cos.unsqueeze(1).broadcast_to([P, CB, S]), ALU.mult).then_inc(G.done(f"rc{m}"), 1)

        def rope_p(pe, c, m, x):
            pe.wait_ge(AC.sem, AC.at(f"ev{m}", c))
            if m >= 2:
                pe.wait_ge(V.sem, V.at(f"rs{m - 2}", c))
            pe.matmul(PS[:, 5 + m % 2, 0:CT], const("rotate"), x, start=True, stop=True).then_inc(PE.done(f"rot{m}"), 1)

        def soft_top(v, c, g, causal):
            v.wait_ge(PE.sem, PE.at(f"S{g}", c))
            if g >= SB:
                v.wait_ge(PE.sem, PE.at(f"P{g - SB}_3", c))
            if causal:
                v.tensor_tensor(s_buf[g % SB], s_ps,
                                const("causal", S).unsqueeze(1).unsqueeze(1).broadcast_to([S, QT, QT, S]),
                                ALU.add).then_inc(V.done(f"mask{g}"), 1)
                own(v, V, c)
                v.tensor_reduce(mx[g % SB], s_buf[g % SB], AX.X, ALU.max).then_inc(V.done(f"max{g}"), 1)
            else:
                v.tensor_reduce(mx[g % SB], s_ps, AX.X, ALU.max).then_inc(V.done(f"max{g}"), 1)
                own(v, V, c)
                v.tensor_tensor(s_buf[g % SB], s_ps, heads16(mx[g % SB]), ALU.subtract).then_inc(V.done(f"mask{g}"), 1)

        def soft_sum(v, c, g):
            v.wait_ge(AC.sem, AC.at(f"exp{g}", c))
            v.tensor_reduce(rsum[g % SB], s_buf[g % SB], AX.X, ALU.add).then_inc(V.done(f"sum{g}"), 1)
            own(v, V, c)
            v.reciprocal(rsum[g % SB], rsum[g % SB]).then_inc(V.done(f"rcp{g}"), 1)

        def soft_shift(gp, c, g):
            gp.wait_ge(V.sem, V.at(f"max{g}", c))
            gp.tensor_tensor(s_buf[g % SB], s_buf[g % SB], heads16(mx[g % SB]), ALU.subtract
                             ).then_inc(G.done(f"shift{g}"), 1)

        def soft_norm(gp, c, g):
            gp.wait_ge(V.sem, V.at(f"rcp{g}", c))
            gp.tensor_tensor(s_buf[g % SB], s_buf[g % SB], heads16(rsum[g % SB]), ALU.mult
                             ).then_inc(G.done(f"norm{g}"), 1)

        def soft_exp(a, c, g, causal):
            if causal:
                a.wait_ge(G.sem, G.at(f"shift{g}", c))
            else:
                a.wait_ge(V.sem, V.at(f"mask{g}", c))
            a.activation(s_buf[g % SB], s_buf[g % SB], ACT.Exp).then_inc(AC.done(f"exp{g}"), 1)

        LAG = 2

        def probs_names(i):
            return ([f"pt{i - LAG}_{u}" for u in range(QT)] if i >= LAG else []) + ([f"exp{i}"] if i < GROUPS else [])

        def probs_a(a, c, i, causal):
            g = i - LAG
            for u in range(QT if g >= 0 else 0):
                a.wait_ge(PE.sem, PE.at(f"P{g}_{u}", c))
                if u < 2 and g > 0:
                    a.wait_ge(PE.sem, PE.at(f"O{g - 1}", c))
                if u >= 2:
                    a.wait_ge(PE.sem, PE.at(f"O{g}_{u - 2}", c))
                a.activation(pt_buf[u % 2], PS[0:S, 5 + u % 2, 0:QT * S], ACT.Copy).then_inc(AC.done(f"pt{g}_{u}"), 1)
            if i < GROUPS:
                soft_exp(a, c, i, causal)

        def scores_p(pe, c, g, half_k):
            b, half = g // 2, g % 2
            if g > 0:
                pe.wait_ge(V.sem, V.at(f"mask{g - 1}", c))
            for u in range(QT):
                for j in range(4):
                    t = half * QT + u
                    k = half if half_k else t
                    rows = slice(32 * j, 32 * j + 32)
                    for q_part, k_part in ((0, 0), (0, 1), (1, 0)):
                        mm = pe.matmul(PS[0:S, 1 + j, u * S:(u + 1) * S], q_s[rows, t, q_part, b * S:(b + 1) * S],
                                       k_s[rows, k, k_part, b * S:(b + 1) * S], start=q_part + k_part == 0,
                                       stop=q_part == 1)
            mm.then_inc(PE.done(f"S{g}"), 1)

        def values_p(pe, c, g, v_of, out_of, free_sem, free_at, bank_waits):
            pe.wait_ge(G.sem, G.at(f"norm{g}", c))

            def product(u):
                pe.wait_ge(AC.sem, AC.at(f"pt{g}_{u}", c))
                if u == 0 and free_at is not None:
                    pe.wait_ge(free_sem, free_at)
                for j in range(4):
                    mm = pe.matmul(out_of(u, j), v_of(u, j), pt_buf[u % 2][:, j * S:(j + 1) * S],
                                   start=True, stop=True)
                mm.then_inc(PE.done(f"O{g}_{u}" if u < 3 else f"O{g}"), 1)

            for u in range(QT):
                if u < 2:
                    for s, at in bank_waits(u):
                        pe.wait_ge(s, at)
                else:
                    pe.wait_ge(AC.sem, AC.at(f"pt{g}_{u - 2}", c))
                for j in range(4):
                    mm = pe.transpose(PS[0:S, 5 + u % 2, j * S:(j + 1) * S], s_buf[g % SB][:, j, u, :],
                                      const("ident", S)[:, 0:S])
                mm.then_inc(PE.done(f"P{g}_{u}"), 1)
                if u > 0:
                    product(u - 1)
            product(3)

        def value_names(g):
            return [f"P{g}_0", f"P{g}_1", f"O{g}_0", f"P{g}_2", f"O{g}_1", f"P{g}_3", f"O{g}_2", f"O{g}"]

        raw0 = words(W_AT, KT, D)
        w_qk = parts(H_AT, KT, 2 * D)
        w_v = parts(W_AT, KT, D)
        w_out = parts(W_AT + KT * D, KT, D)
        ctxT = A[:, vT_at:vT_at + CW].bitcast(BF16).rearrange("p (k b two s) -> p k b two s", k=KT, b=CB, two=2)
        w3 = T["qkv_w"].rearrange("p (k n) -> p k n", k=KT)
        early = units_of(w_out, T["out_w"].rearrange("p (k n) -> p k n", k=KT), D, 2) + units_of(w_v, w3[:, :, 2 * D:], D, 2)
        late = units_of(w_qk, w3[:, :, 0:2 * D], 2 * D, 1)
        units = list(enumerate(early + late))
        SX.layer(["hi", "lo"], 1 + NC)
        WA.layer([f"hi{u}" for u, _ in units], 1)
        WV.layer([f"lo{u}" for u, _ in units], 1)
        v_tok = [words(vb_at + i * D, D, rows=S) for i in range(2)]
        NQ = 3 * KT

        V.layer([f"{x}{m}" for m in range(2 * KT) for x in ("rs", "rr", "rh", "rl")]
                + [x for g in range(GROUPS + LAG + 1) for x in
                   ([f"rest{g - LAG - 1}"] if g > LAG else []) + ([f"mask{g}", f"max{g}"] if g < GROUPS else [])
                   + ([f"sum{g - 1}", f"rcp{g - 1}"] if 0 < g <= GROUPS else [])]
                + [f"res{m}" for m in range(KT)])
        AC.layer([f"ev{m}" for m in range(NQ)] + [x for g in range(GROUPS + LAG) for x in
                 ([f"vt{g // 2}"] if g % 2 == 0 and g < GROUPS else []) + probs_names(g)
                 + ([f"ctx{g - LAG}"] if g >= LAG else [])])
        G.layer([f"rc{m}" for m in range(2 * KT)] + [x for g in range(GROUPS + 1) for x in
                ([f"shift{g}"] if g < GROUPS else []) + ([f"norm{g - 1}"] if g else [])])
        pe_names = []
        for m in range(NQ + 2):
            pe_names += ([f"qkv{m}"] if m < NQ else []) + ([f"rot{m - 2}"] if 2 <= m < 2 * KT + 2 else [])
        for g in range(GROUPS + LAG):
            pe_names += [f"Vt{g // 2}"] if g % 2 == 0 and g < GROUPS else []
            pe_names += [f"S{g}"] if g < GROUPS else []
            pe_names += value_names(g - LAG) if g >= LAG else []
        PE.layer(pe_names + [f"proj{m}" for m in range(KT)])

        with nc.Block() as block:
            @block.sync
            def _(sp):
                sp.dma_start(hD.rearrange("c p w -> p c w"),
                             A[:, 0:NC * CW].rearrange("p (c w) -> p c w", c=NC)).then_inc(h_out, 16)
                for u, unit in units:
                    stage_sp(sp, u, unit)
                sp.wait_ge(h_out, 16)
                sp.dma_start(hbuf, hD[1].rearrange("p (k t) -> p k t", k=KT)).then_inc(h_in, 16)

                def turn(c, after_next):
                    sp.wait_ge(LV.sem, LV.at("center", c + 1))
                    sp.wait_ge(h_in, c * 32 + 16)
                    sp.dma_start(hbuf, hD[bass.ds(c, 1)].rearrange("c p (k t) -> p (c k) t", k=KT)
                                 ).then_inc(h_in, 16)
                    sp.wait_ge(V.sem, V.at("res7", c))
                    sp.dma_start(hD[bass.ds(c, 1)].rearrange("c p (k t) -> p (c k) t", k=KT), hbuf
                                 ).then_inc(h_out, 16)
                    sp.wait_ge(h_out, c * 16 + 32)
                    if after_next is not None:
                        sp.dma_start(hbuf, hD[bass.ds(after_next, 1)].rearrange("c p (k t) -> p (c k) t", k=KT)
                                     ).then_inc(h_in, 16)

                with sp.Fori(0, NC - 2) as c:
                    turn(c, c + 2)
                turn(NC - 2, 0)
                sp.wait_ge(LV.sem, LV.at("center", NC))
                sp.wait_ge(h_in, (NC - 1) * 32 + 16)
                sp.dma_start(hbuf, hD[NC - 1].rearrange("p (k t) -> p k t", k=KT)).then_inc(h_in, 16)
                sp.wait_ge(PE.sem, PE.at("qkv23", NC - 1))
                sp.dma_start(A[:, 0:(NC - 1) * CW].rearrange("p (c w) -> p c w", c=NC - 1),
                             hD[0:NC - 1].rearrange("c p w -> p c w")).then_inc(h_back, 16)
                sp.dma_start(raw0, T["base0_w"].rearrange("p (k n) -> p k n", k=KT)).then_inc(w_in[1], 16)
                sp.wait_ge(V.sem, V.at("res7", NC - 1))
                sp.dma_start(A[:, (NC - 1) * CW:NC * CW].rearrange("p (k t) -> p k t", k=KT), hbuf).then_inc(h_last, 16)
                sp.wait_ge(h_in, 16 * 2 * NC)
                sp.wait_ge(h_back, 16)
                sp.wait_ge(h_last, 16)

            @block.vector
            def _(v):
                ln_v1(v, 0, h_chunk(0))
                ln_v2(v, 0, h_chunk(0))
                ln_v3(v, 0, sq)
                ln_v4(v, 0)
                ln_v5(v, 0)
                split_xn(v, 0, 0)
                for u, unit in units:
                    if u == len(early):
                        v.wait_ge(h_out, 16)
                    split_v(v, u, unit)
                with v.Fori(0, NC) as c:
                    V.here = 0
                    for m in range(2 * KT):
                        rope_v(v, c, m)
                        if m == 3:
                            v.wait_ge(h_in, c * 32 + 16)
                            ln_v1(v, c + 1, hbuf)
                        if m == 7:
                            ln_v2(v, c + 1, hbuf)
                        if m == 11:
                            ln_v3(v, c + 1, sq)
                    for g in range(GROUPS + LAG + 1):
                        if g > LAG:
                            done = g - LAG - 1
                            b, half = done // 2, done % 2
                            v.wait_ge(AC.sem, AC.at(f"ctx{done}", c))
                            v.tensor_tensor(ctxT[:, half * QT:half * QT + QT, b, 1, :],
                                            PS[:, 7, 0:QT * S].rearrange("p (u t) -> p u t", u=QT),
                                            ctxT[:, half * QT:half * QT + QT, b, 0, :], ALU.subtract
                                            ).then_inc(V.done(f"rest{done}"), 1)
                        if g < GROUPS:
                            soft_top(v, c, g, True)
                        if 0 < g <= GROUPS:
                            soft_sum(v, c, g - 1)
                        if g == 2:
                            ln_v4(v, c + 1)
                        if g == 3:
                            ln_v5(v, c + 1, [(PE.sem, PE.at("qkv23", c))])
                        if g == 5:
                            split_xn(v, c + 1, c + 1)
                    v.wait_ge(h_in, c * 32 + 32)
                    for m in range(KT):
                        v.wait_ge(PE.sem, PE.at(f"proj{m}", c))
                        v.scalar_tensor_tensor(out=hbuf[:, m, :], in0=PS[:, 1 + m % 4, 0:CT], scalar=bias("out_b", m),
                                               in1=hbuf[:, m, :], op0=ALU.add, op1=ALU.add
                                               ).then_inc(V.done(f"res{m}"), 1)

            @block.gpsimd
            def _(g):
                with g.Fori(0, NC) as c:
                    G.here = 0
                    for m in range(2 * KT):
                        rope_g(g, c, m, (qT if m < KT else kT)[:, m % KT, :])
                    for i in range(GROUPS + 1):
                        if i < GROUPS:
                            soft_shift(g, c, i)
                        if i:
                            soft_norm(g, c, i - 1)

            @block.scalar
            def _(a):
                ln_a1(a, 0, sq)
                ln_a2(a, 0)
                for u, unit in units:
                    if u == len(early):
                        a.wait_ge(h_out, 16)
                        a.wait_ge(LV.sem, LV.at("center", 0))
                    split_a(a, u, unit)
                with a.Fori(0, NC) as c:
                    AC.here = 0
                    for m in range(NQ):
                        a.wait_ge(PE.sem, PE.at(f"qkv{m}", c))
                        x = (qT, kT, vT)[m // KT]
                        a.activation(x[:, m % KT, :], PS[:, 1 + m % 4, 0:CT], ACT.Identity, bias=bias("qkv_b", m)
                                     ).then_inc(AC.done(f"ev{m}"), 1)
                        if m == 13:
                            ln_a1(a, c + 1, sq)
                        if m == 20:
                            ln_a2(a, c + 1)
                    for g in range(GROUPS + LAG):
                        if g % 2 == 0 and g < GROUPS:
                            b = g // 2
                            a.wait_ge(PE.sem, PE.at(f"Vt{b}", c))
                            if b >= 2:
                                a.wait_ge(PE.sem, PE.at(f"O{2 * b - 3}", c))
                            a.activation(v_tok[b % 2].rearrange("p (n w) -> p n w", n=2), PS[0:S, 5:7, :], ACT.Copy
                                         ).then_inc(AC.done(f"vt{b}"), 1)
                        probs_a(a, c, g, True)
                        if g >= LAG:
                            b, half = (g - LAG) // 2, (g - LAG) % 2
                            a.wait_ge(PE.sem, PE.at(f"O{g - LAG}", c))
                            a.activation(ctxT[:, half * QT:half * QT + QT, b, 0, :],
                                         PS[:, 7, 0:QT * S].rearrange("p (u t) -> p u t", u=QT), ACT.Copy
                                         ).then_inc(AC.done(f"ctx{g - LAG}"), 1)

            @block.tensor
            def _(pe):
                ln_p1(pe, 0)
                ln_p2(pe, 0)
                pe.wait_ge(WV.sem, WV.at(f"lo{len(units) - 1}"))
                with pe.Fori(0, NC) as c:
                    PE.here = 0
                    pe.wait_ge(SX.sem, SX.at("lo", c))
                    for m in range(NQ + 2):
                        if m < NQ:
                            if m >= 4:
                                pe.wait_ge(AC.sem, AC.at(f"ev{m - 4}", c))
                            else:
                                pe.wait_ge(V.sem, V.prev(f"res{m + 4}", c))
                            w = w_qk if m < 2 * KT else w_v
                            o = (m % (2 * KT)) * P
                            gemm3(pe, PS[:, 1 + m % 4, 0:CT], lambda k, part: w[:, k, part, o:o + P], of_xs(0)
                                  ).then_inc(PE.done(f"qkv{m}"), 1)
                        if m == 8:
                            ln_p1(pe, c + 1)
                        if m == 18:
                            ln_p2(pe, c + 1)
                        if 2 <= m < 2 * KT + 2:
                            rope_p(pe, c, m - 2, (qT if m - 2 < KT else kT)[:, (m - 2) % KT, :])
                    pe.wait_ge(V.sem, V.at("rl15", c))
                    for g in range(GROUPS + LAG):
                        if g % 2 == 0 and g < GROUPS:
                            b = g // 2
                            if b == 0:
                                pe.wait_ge(AC.sem, AC.at("ev23", c))
                            elif 2 * b <= LAG:
                                pe.wait_ge(AC.sem, AC.at(f"vt{b - 1}", c))
                            else:
                                pe.wait_ge(AC.sem, AC.at(f"pt{2 * b - LAG - 1}_3", c))
                            for k in range(KT):
                                mm = pe.transpose(PS[0:S, 5 + k // 4, k % 4 * P:k % 4 * P + P],
                                                  vT[:, k, b * S:(b + 1) * S], ident)
                            mm.then_inc(PE.done(f"Vt{b}"), 1)
                        if g < GROUPS:
                            scores_p(pe, c, g, False)
                        if g >= LAG:
                            values_p(pe, c, g - LAG,
                                     lambda u, j, q=g - LAG: v_tok[q // 2 % 2][:, (q % 2 * 16 + 4 * u + j) * HD:
                                                                           (q % 2 * 16 + 4 * u + j) * HD + HD],
                                     lambda u, j: PS[32 * j:32 * j + 32, 7, u * S:(u + 1) * S],
                                     V.sem, V.at(f"rest{g - LAG - 1}", c) if g > LAG else None,
                                     lambda u, q=g: [(AC.sem, AC.at(f"vt{q // 2}", c))] if q % 2 == 0 and q < GROUPS
                                     else [(AC.sem, AC.at(f"pt{q - LAG - 1}_{2 + u}", c))])
                    pe.wait_ge(V.sem, V.at("rest7", c))
                    for m in range(KT):
                        if m >= 4:
                            pe.wait_ge(V.sem, V.at(f"res{m - 4}", c))
                        gemm3(pe, PS[:, 1 + m % 4, 0:CT].rearrange("p (b s) -> p b s", b=CB),
                              lambda k, part: w_out[:, k, part, m * P:m * P + P], lambda k, part: ctxT[:, k, :, part, :]
                              ).then_inc(PE.done(f"proj{m}"), 1)

        for t in (V, AC, G, PE, SX, WA, WV):
            t.close()
        staged = [staged[i] + len(units[i::SLOTS]) for i in range(SLOTS)]
        if STOP_AFTER == 1:
            return finish()

        sq2_at = WORDS - CW
        sq2 = words(sq2_at, KT, CT)
        FREE_END = sq2_at
        assert XS1_AT == sq2_at - CW

        def following(e, c):
            return e.snap((c + 1) & 7)

        def routed(layer, top, base_name, router_name, a_name, b_name, bias_name, spread):
            w_base = parts(W_AT + KT * D, KT, D)
            o = W_AT + 2 * KT * D
            w_a = words(o, KT, P)
            w_b = words(o + D, D)
            w_r = words(o + 2 * D, KT, EXPERTS)
            o += 2 * D + KT * EXPERTS
            h_a, comb_t, wh = words(o, CT), words(o + CT, CT, rows=EXPERTS), words(o + 2 * CT, CT)
            o += 3 * CT
            pair = [words(o + 256 * i, CB, EXPERTS, EXPERTS, rows=S) for i in range(2)]
            o += 512
            lg, rank, ex, comb = (words(o + 32 * i, CB, EXPERTS, rows=S) for i in range(4))
            top_l, den = (words(o + 128 + 4 * i, CB, rows=S) for i in range(2))
            assert o + 136 <= XS1_AT
            base = base_name is not None
            pieces = list(range(0, KT, 2)) if base else []
            if base:
                SX.layer(["hi", "lo"])
                WA.layer([f"hi{k}" for k in pieces], 1)
                WV.layer([f"lo{k}" for k in pieces], 1)
            LAG = 3

            V.layer(["lg", "gt", "eq", "tie", "both", "rank", "sel"]
                    + (["top", "off", "kept", "den", "rden"] if top == 2 else []) + ["comb", "wh"]
                    + [f"res{m}" for m in range(KT)])
            AC.layer(["ha"] + (["ex"] if top == 2 else []) + ["ct"])
            pe_names = ["router", "hA"]
            order = []
            for m in range(KT + LAG):
                if m < KT and base:
                    order.append(("base", m))
                if m == 1:
                    order.append(("comb", 0))
                if m == 2:
                    order.append(("spread", 0))
                if m >= LAG:
                    order.append(("lora", m - LAG))
            PE.layer(pe_names + [f"{x}{m}" for x, m in order])

            with nc.Block() as block:
                @block.sync
                def _(sp):
                    sp.dma_start(w_r, T[router_name].rearrange("p (k n) -> p k n", k=KT)).then_inc(lora_in, 16)
                    sp.dma_start(w_a, T[a_name].rearrange("p (k n) -> p k n", k=KT)).then_inc(lora_in, 16)
                    sp.dma_start(w_b, T[b_name]).then_inc(lora_in, 16)

                @block.vector
                def _(v):
                    for k in pieces:
                        v.wait_ge(WA.sem, WA.at(f"hi{k}"))
                        v.tensor_tensor(w_base[:, k:k + 2, 1, :], raw0[:, k:k + 2], w_base[:, k:k + 2, 0, :],
                                        ALU.subtract).then_inc(WV.done(f"lo{k}"), 1)
                    with v.Fori(0, NC, 2) as even:
                        for slot in range(2):
                            c = even + slot
                            V.here = 0
                            n = c + (layer * NC + 1)
                            c1 = following(v, c)
                            ln_v1(v, n, h_chunk(c1))
                            v.wait_ge(PE.sem, PE.at("router", c))
                            v.tensor_copy(lg, PS[0:S, 1, 0:CB * EXPERTS].rearrange("p (b e) -> p b e", b=CB)
                                          ).then_inc(V.done("lg"), 1)
                            other = lg.unsqueeze(2).broadcast_to([S, CB, EXPERTS, EXPERTS])
                            self_ = lg.unsqueeze(3).broadcast_to([S, CB, EXPERTS, EXPERTS])
                            own(v, V, c)
                            v.tensor_tensor(pair[0], other, self_, ALU.is_gt).then_inc(V.done("gt"), 1)
                            v.tensor_tensor(pair[1], other, self_, ALU.is_equal).then_inc(V.done("eq"), 1)
                            own(v, V, c)
                            v.tensor_tensor(pair[1], pair[1],
                                            const("earlier", S).rearrange("p (e j) -> p e j", e=EXPERTS).unsqueeze(1)
                                            .broadcast_to([S, CB, EXPERTS, EXPERTS]), ALU.mult).then_inc(V.done("tie"), 1)
                            own(v, V, c)
                            v.tensor_tensor(pair[0], pair[0], pair[1], ALU.add).then_inc(V.done("both"), 1)
                            own(v, V, c)
                            v.tensor_reduce(rank, pair[0], AX.X, ALU.add).then_inc(V.done("rank"), 1)
                            own(v, V, c)
                            v.tensor_scalar(rank, rank, float(top), None, ALU.is_lt).then_inc(V.done("sel"), 1)
                            if top == 2:
                                v.tensor_reduce(top_l, lg, AX.X, ALU.max).then_inc(V.done("top"), 1)
                                own(v, V, c)
                                v.tensor_tensor(ex, lg, top_l.unsqueeze(2).broadcast_to([S, CB, EXPERTS]), ALU.subtract
                                                ).then_inc(V.done("off"), 1)
                                v.wait_ge(AC.sem, AC.at("ex", c))
                                v.tensor_tensor(ex, ex, rank, ALU.mult).then_inc(V.done("kept"), 1)
                                own(v, V, c)
                                v.tensor_reduce(den, ex, AX.X, ALU.add).then_inc(V.done("den"), 1)
                                own(v, V, c)
                                v.reciprocal(den, den).then_inc(V.done("rden"), 1)
                                own(v, V, c)
                                v.tensor_tensor(comb, ex, den.unsqueeze(2).broadcast_to([S, CB, EXPERTS]), ALU.mult
                                                ).then_inc(V.done("comb"), 1)
                            else:
                                own(v, V, c)
                                v.tensor_tensor(comb, lg, rank, ALU.mult).then_inc(V.done("comb"), 1)
                            ln_v2(v, n, h_chunk(c1))
                            v.wait_ge(PE.sem, PE.at("spread0", c))
                            v.tensor_tensor(wh, h_a, PS[:, 2, 0:CT], ALU.mult).then_inc(V.done("wh"), 1)
                            ln_v3(v, n, sq2)
                            for m in range(KT):
                                v.wait_ge(PE.sem, PE.at(f"lora{m}", c))
                                hm, ps = h_tile(c, m), PS[:, 3 + m % 5, 0:CT]
                                if bias_name:
                                    v.scalar_tensor_tensor(out=hm, in0=ps, scalar=bias(bias_name, m), in1=hm, op0=ALU.add,
                                                           op1=ALU.add).then_inc(V.done(f"res{m}"), 1)
                                else:
                                    v.tensor_tensor(hm, ps, hm, ALU.add).then_inc(V.done(f"res{m}"), 1)
                                if m == 3:
                                    ln_v4(v, n)
                                    ln_v5(v, n, [(PE.sem, PE.at("hA", c))])
                                    if base:
                                        split_xn(v, c, n, 1 - slot)

                @block.scalar
                def _(a):
                    if base:
                        a.wait_ge(w_in[layer], 16)
                    for k in pieces:
                        a.activation(w_base[:, k:k + 2, 0, :], raw0[:, k:k + 2], ACT.Copy
                                     ).then_inc(WA.done(f"hi{k}"), 1)
                    with a.Fori(0, NC, 2) as even:
                        for slot in range(2):
                            c = even + slot
                            AC.here = 0
                            n = c + (layer * NC + 1)
                            a.wait_ge(PE.sem, PE.at("hA", c))
                            a.activation(h_a, PS[:, 2, 0:CT], ACT.Copy).then_inc(AC.done("ha"), 1)
                            if top == 2:
                                a.wait_ge(V.sem, V.at("off", c))
                                a.activation(ex, ex, ACT.Exp).then_inc(AC.done("ex"), 1)
                            a.wait_ge(PE.sem, PE.at("comb0", c))
                            a.activation(comb_t, PS[0:EXPERTS, 1, 0:CT], ACT.Copy).then_inc(AC.done("ct"), 1)
                            ln_a1(a, n, sq2)
                            ln_a2(a, n)

                @block.tensor
                def _(pe):
                    pe.wait_ge(lora_in, 48 if base else 96)
                    if base:
                        pe.wait_ge(WV.sem, WV.at(f"lo{pieces[-1]}"))
                    with pe.Fori(0, NC, 2) as even:
                        for slot in range(2):
                            c = even + slot
                            PE.here = 0
                            n = c + (layer * NC + 1)
                            pe.wait_ge(LV.sem, LV.at("out", n - 1))
                            pe.wait_ge(AC.sem, AC.prev("ct", c))
                            for b in range(CB):
                                for k in range(KT):
                                    mm = pe.matmul(PS[0:S, 1, b * EXPERTS:(b + 1) * EXPERTS], xn[:, k, b * S:(b + 1) * S],
                                                   w_r[:, k, :], start=k == 0, stop=k == KT - 1)
                            mm.then_inc(PE.done("router"), 1)
                            pe.wait_ge(V.sem, V.prev("wh", c))
                            gemm(pe, PS[:, 2, 0:CT], lambda k: w_a[:, k, :], range(KT)).then_inc(PE.done("hA"), 1)
                            for what, m in order:
                                bank = PS[:, 3 + m % 5, 0:CT]
                                first = what == "base" or (what == "lora" and not base)
                                if first:
                                    if m >= 5:
                                        pe.wait_ge(V.sem, V.at(f"res{m - 5}", c))
                                    else:
                                        pe.wait_ge(V.sem, V.prev(f"res{min(m + 5, 7)}", c))
                                if (what, m) == ("base", 0):
                                    pe.wait_ge(SX.sem, SX.prev("lo", c))
                                if what == "base":
                                    gemm3(pe, bank, lambda k, part: w_base[:, k, part, m * P:m * P + P], of_xs(slot),
                                          last=False).then_inc(PE.done(f"base{m}"), 1)
                                elif what == "comb":
                                    pe.wait_ge(V.sem, V.at("comb", c))
                                    for b in range(CB):
                                        mm = pe.transpose(PS[0:EXPERTS, 1, b * S:(b + 1) * S], comb[:, b, :],
                                                          const("ident", S)[:, 0:S])
                                    mm.then_inc(PE.done("comb0"), 1)
                                    ln_p1(pe, n)
                                elif what == "spread":
                                    pe.wait_ge(AC.sem, AC.at("ct", c))
                                    pe.matmul(PS[:, 2, 0:CT], const(spread, EXPERTS), comb_t, start=True, stop=True
                                              ).then_inc(PE.done("spread0"), 1)
                                else:
                                    if m == 0:
                                        pe.wait_ge(V.sem, V.at("wh", c))
                                    pe.matmul(bank, w_b[:, m * P:m * P + P], wh, start=not base, stop=True
                                              ).then_inc(PE.done(f"lora{m}"), 1)
                                    if m == 0:
                                        ln_p2(pe, n)

            for t in (V, AC, G, PE) + ((SX, WA, WV) if base else ()):
                t.close()

        G.layer([])
        routed(1, 2, "base0_w", "router0", "a0", "b0", "base0_b", "spread2")
        if STOP_AFTER == 2:
            return finish()

        rows = {x: words(W_AT + 256 * i, 256, rows=HDH) for i, x in enumerate("qkv")}
        t_abs, t_pos, t_neg = (words(W_AT + 768 + 256 * i, 256, rows=HDH) for i in range(3))
        alpha = words(W_AT + 1536, 1, rows=HDH)
        bind = {x: A[:, BIND_AT + 8 * i:BIND_AT + 8 * i + 8] for i, x in enumerate("qkv")}
        V.layer([f"{x}{s}" for x in "qkv" for s in ("pos", "neg", "al", "mean", "sign", "hard", "zero", "fill", "diff",
                                                     "sum", "col")], 1)
        PE.layer([f"{x}t" for x in "qkv"], 1)
        with nc.Block() as block:
            @block.sync
            def _(sp):
                for x in "qkv":
                    sp.dma_start(rows[x], T[f"bind_{x}"]).then_inc(w_in[2], 16)

            @block.vector
            def _(v):
                v.wait_ge(w_in[2], 48)
                for x in "qkv":
                    w = rows[x]
                    own(v, V)
                    v.tensor_scalar(t_pos, w, 0.0, None, ALU.is_gt).then_inc(V.done(f"{x}pos"), 1)
                    own(v, V)
                    v.tensor_scalar(t_neg, w, 0.0, None, ALU.is_lt).then_inc(V.done(f"{x}neg"), 1)
                    own(v, V)
                    v.tensor_reduce(alpha, w, AX.X, ALU.add, apply_absolute_value=True).then_inc(V.done(f"{x}al"), 1)
                    own(v, V)
                    v.tensor_scalar(alpha, alpha, 1.0 / 256, None, ALU.mult).then_inc(V.done(f"{x}mean"), 1)
                    own(v, V)
                    v.tensor_tensor(t_pos, t_pos, t_neg, ALU.subtract).then_inc(V.done(f"{x}sign"), 1)
                    own(v, V)
                    v.tensor_scalar(t_pos, t_pos, alpha, None, ALU.mult).then_inc(V.done(f"{x}hard"), 1)
                    own(v, V)
                    v.tensor_scalar(t_neg, t_pos, 0.0, alpha, ALU.is_equal, ALU.mult).then_inc(V.done(f"{x}zero"), 1)
                    own(v, V)
                    v.tensor_tensor(t_pos, t_pos, t_neg, ALU.add).then_inc(V.done(f"{x}fill"), 1)
                    own(v, V)
                    v.tensor_tensor(t_pos, t_pos, w, ALU.subtract).then_inc(V.done(f"{x}diff"), 1)
                    own(v, V)
                    v.tensor_tensor(w, t_pos, w, ALU.add).then_inc(V.done(f"{x}sum"), 1)
                    v.wait_ge(PE.sem, PE.at(f"{x}t"))
                    v.tensor_copy(bind[x].rearrange("p (h f) -> p f h", f=2),
                                  PS[:, 1, 0:2 * HDH].rearrange("p (f h) -> p f h", f=2)).then_inc(V.done(f"{x}col"), 1)

            @block.tensor
            def _(pe):
                for x in "qkv":
                    pe.wait_ge(V.sem, V.at(f"{x}sum"))
                    for f in range(2):
                        mm = pe.transpose(PS[:, 1, f * HDH:(f + 1) * HDH], rows[x][:, f * P:(f + 1) * P],
                                          const("ident", HDH)[:, 0:HDH])
                    mm.then_inc(PE.done(f"{x}t"), 1)

        for t in (V, PE):
            t.close()

        o = W_AT
        q3, k3, v3 = (words(o + i * CW, KT, CT) for i in range(3))
        v3_tok = [words(o + 3 * CW + i * D, D, rows=S) for i in range(CB)]
        att = words(o + 3 * CW + CB * D, CB, HDH, S, rows=S)
        V.layer(["Q", "K", "one", "rec", "keep"] + [f"res{m}" for m in range(KT)])
        G.layer(["V"])
        AC.layer(["ex"] + [f"vt{b}" for b in range(CB)])
        PE.layer(["S"] + [f"Vt{b}" for b in range(CB)] + [f"O{m}" for m in range(KT)])
        LAYER = 2
        with nc.Block() as block:
            @block.vector
            def _(v):
                with v.Fori(0, NC) as c:
                    V.here = 0
                    n = c + (LAYER * NC + 1)
                    c1 = following(v, c)
                    wide = lambda x: bind[x].unsqueeze(2).broadcast_to([P, KT, CT])
                    v.wait_ge(PE.sem, PE.prev("S", c))
                    v.tensor_tensor(q3, xn, wide("q"), ALU.mult).then_inc(V.done("Q"), 1)
                    v.tensor_tensor(k3, xn, wide("k"), ALU.mult).then_inc(V.done("K"), 1)
                    ln_v1(v, n, h_chunk(c1))
                    ln_v2(v, n, h_chunk(c1))
                    v.wait_ge(AC.sem, AC.at("ex", c))
                    v.tensor_scalar(att, att, 1.0, None, ALU.add).then_inc(V.done("one"), 1)
                    own(v, V, c)
                    v.reciprocal(att, att).then_inc(V.done("rec"), 1)
                    own(v, V, c)
                    v.tensor_tensor(att, att, const("causal_t", S).unsqueeze(1).unsqueeze(1)
                                    .broadcast_to([S, CB, HDH, S]), ALU.mult).then_inc(V.done("keep"), 1)
                    ln_v3(v, n, sq2)
                    ln_v4(v, n)
                    ln_v5(v, n, [(G.sem, G.at("V", c))])
                    for m in range(KT):
                        v.wait_ge(PE.sem, PE.at(f"O{m}", c))
                        v.tensor_tensor(h_tile(c, m), PS[:, 5 + m % 3, 0:CT], h_tile(c, m), ALU.add
                                        ).then_inc(V.done(f"res{m}"), 1)

            @block.gpsimd
            def _(g):
                with g.Fori(0, NC) as c:
                    G.here = 0
                    g.wait_ge(LV.sem, LV.at("out", c + LAYER * NC))
                    g.wait_ge(PE.sem, PE.prev("Vt3", c))
                    g.tensor_tensor(v3, xn, bind["v"].unsqueeze(2).broadcast_to([P, KT, CT]), ALU.mult
                                    ).then_inc(G.done("V"), 1)

            @block.scalar
            def _(a):
                with a.Fori(0, NC) as c:
                    AC.here = 0
                    n = c + (LAYER * NC + 1)
                    a.wait_ge(PE.sem, PE.at("S", c))
                    a.wait_ge(PE.sem, PE.prev("O7", c))
                    a.activation(att.rearrange("p b h s -> p b (h s)"), PS[0:S, 1:5, 0:HDH * S], ACT.Exp, scale=-0.25
                                 ).then_inc(AC.done("ex"), 1)
                    ln_a1(a, n, sq2)
                    for b in range(CB):
                        a.wait_ge(PE.sem, PE.at(f"Vt{b}", c))
                        a.activation(v3_tok[b].rearrange("p (n w) -> p n w", n=2), PS[0:S, 5:7, :], ACT.Copy
                                     ).then_inc(AC.done(f"vt{b}"), 1)
                    ln_a2(a, n)

            @block.tensor
            def _(pe):
                with pe.Fori(0, NC) as c:
                    PE.here = 0
                    n = c + (LAYER * NC + 1)
                    pe.wait_ge(V.sem, V.at("K", c))
                    for b in range(CB):
                        for hd in range(HDH):
                            for f in range(2):
                                k = 2 * hd + f
                                mm = pe.matmul(PS[0:S, 1 + b, hd * S:(hd + 1) * S], k3[:, k, b * S:(b + 1) * S],
                                               q3[:, k, b * S:(b + 1) * S], start=f == 0, stop=f == 1)
                    mm.then_inc(PE.done("S"), 1)
                    ln_p1(pe, n)
                    pe.wait_ge(G.sem, G.at("V", c))
                    for b in range(CB):
                        if b:
                            pe.wait_ge(AC.sem, AC.at(f"vt{b - 1}", c))
                        else:
                            pe.wait_ge(V.sem, V.prev("res7", c))
                        for k in range(KT):
                            mm = pe.transpose(PS[0:S, 5 + k // 4, k % 4 * P:k % 4 * P + P], v3[:, k, b * S:(b + 1) * S],
                                              ident)
                        mm.then_inc(PE.done(f"Vt{b}"), 1)
                    ln_p2(pe, n)
                    pe.wait_ge(V.sem, V.at("keep", c))
                    pe.wait_ge(AC.sem, AC.at("vt3", c))
                    for m in range(KT):
                        if m >= 3:
                            pe.wait_ge(V.sem, V.at(f"res{m - 3}", c))
                        for b in range(CB):
                            mm = pe.matmul(PS[:, 5 + m % 3, b * S:(b + 1) * S], v3_tok[b][:, m * P:m * P + P],
                                           att[:, b, m // 2, :], start=True, stop=True)
                        mm.then_inc(PE.done(f"O{m}"), 1)

        for t in (V, AC, G, PE):
            t.close()
        if STOP_AFTER == 3:
            return finish()

        G.layer([])
        routed(3, 1, None, "router1", "a1", "b1", None, "spread1")
        if STOP_AFTER == 4:
            return finish()

        o = W_AT
        w_xp = words(o, KT, DTR + 2 * SSM)
        w_dt = words(o + 512, D, rows=DTR)
        neg_a = words(C_AT + CONST_AT["count"][0], KT, SSM)
        xp = words(o + 1536, CT, rows=DTR + 2 * SSM)
        BC_AT = o + 1536 + CT
        BC_W = 2 * SSM * CT
        o = BC_AT + 2 * BC_W
        dt = [words(at, KT, CT) for at in (XS_AT, o)]
        ux = words(o + CW, KT, CT)
        o += 2 * CW
        UN = 4
        UW = UN * CT
        NU = SSM // UN
        ST = 4
        da = [words(o + i * UW, UN, CB, S) for i in range(2)]
        st_at = o + 2 * UW
        st = [words(st_at + i * UW, UN, CT) for i in range(ST)]
        st_flat = [words(st_at + i * UW, UW) for i in range(ST)]
        da_flat = [words(o + i * UW, UW) for i in range(2)]
        soft = sq2
        assert st_at + ST * UW <= FREE_END
        LAYER5 = 4
        XP, XA = Steps(sem("scan_input_tensor_steps")), Steps(sem("scan_input_scalar_steps"))
        XV = Steps(sem("scan_input_vector_steps"))
        XP.layer(["xp"] + [f"dt{m}" for m in range(KT)], NC + 1)
        XA.layer(["xp"] + [f"z{m}" for m in range(KT)] + ["abs", "exp", "log"], NC + 1)
        XV.layer(["dt"], NC + 1)

        def xp_p(pe, c):
            pe.wait_ge(LV.sem, LV.at("out", c + LAYER5 * NC))
            XP.here = 0
            gemm(pe, PS[0:DTR + 2 * SSM, 7, 0:CT], lambda k: w_xp[:, k, :], range(KT)).then_inc(XP.done("xp"), 1)

        def xp_a(a, c):
            XA.here = 0
            a.wait_ge(XP.sem, XP.at("xp", c))
            a.activation(xp, PS[0:DTR + 2 * SSM, 7, 0:CT], ACT.Copy).then_inc(XA.done("xp"), 1)

        def dt_p(pe, c, tiles):
            pe.wait_ge(XA.sem, XA.at("xp", c))
            for m in tiles:
                if m >= 3:
                    pe.wait_ge(XA.sem, XA.at(f"z{m - 3}", c))
                pe.matmul(PS[:, 1 + m % 3, 0:CT], w_dt[:, m * P:m * P + P], xp[0:DTR, :], start=True, stop=True
                          ).then_inc(XP.done(f"dt{m}"), 1)

        def z_a(a, c, slot, tiles):
            for m in tiles:
                a.wait_ge(XP.sem, XP.at(f"dt{m}", c))
                a.activation(dt[slot][:, m, :], PS[:, 1 + m % 3, 0:CT], ACT.Identity, bias=bias("dt_b", m)
                             ).then_inc(XA.done(f"z{m}"), 1)

        def abs_a(a, c, slot):
            own(a, XA, c)
            a.activation(soft, dt[slot], ACT.Abs).then_inc(XA.done("abs"), 1)

        def exp_a(a, c):
            own(a, XA, c)
            a.activation(soft, soft, ACT.Exp, scale=-1.0).then_inc(XA.done("exp"), 1)

        def log_a(a, c):
            own(a, XA, c)
            a.activation(soft, soft, ACT.Ln, bias=1.0).then_inc(XA.done("log"), 1)

        def dt_v(v, c, slot):
            XV.here = 0
            v.wait_ge(XA.sem, XA.at("log", c))
            v.scalar_tensor_tensor(out=dt[slot], in0=dt[slot], scalar=0.0, in1=soft, op0=ALU.max, op1=ALU.add
                                   ).then_inc(XV.done("dt"), 1)

        def spread(sp, r, slot):
            sp.wait_ge(XA.sem, XA.at("xp", r))
            sp.dma_start(bcD, xp[DTR:, :]).then_inc(bc_out, 16)
            sp.wait_ge(bc_out, r * 16 + 16)
            sp.dma_start(A[:, BC_AT + slot * BC_W:BC_AT + (slot + 1) * BC_W],
                         bcD.rearrange("n t -> (n t)").unsqueeze(0).broadcast_to([P, BC_W])
                         ).then_inc(bc_in, 16)

        V.layer(["neg", "zero0", "zero1"], 1)
        AC.layer(["a"], 1)
        with nc.Block() as block:
            @block.sync
            def _(sp):
                sp.dma_start(w_xp, T["xproj"].rearrange("p (k n) -> p k n", k=KT)).then_inc(w_in[4], 16)
                sp.dma_start(w_dt, T["dtw"]).then_inc(w_in[4], 16)
                sp.dma_start(neg_a, T["a_log"].rearrange("p (k n) -> p k n", k=KT)).then_inc(w_in[4], 16)
                spread(sp, 0, 0)

            @block.scalar
            def _(a):
                a.wait_ge(w_in[4], 48)
                a.activation(neg_a, neg_a, ACT.Exp).then_inc(AC.done("a"), 1)
                xp_a(a, 0)
                z_a(a, 0, 0, range(KT))
                abs_a(a, 0, 0)
                exp_a(a, 0)
                log_a(a, 0)

            @block.vector
            def _(v):
                v.wait_ge(AC.sem, AC.at("a"))
                v.tensor_scalar(neg_a, neg_a, -1.0, None, ALU.mult).then_inc(V.done("neg"), 1)
                for i in range(2):
                    v.memset(da[i][:, :, :, 0], 0.0).then_inc(V.done(f"zero{i}"), 1)
                dt_v(v, 0, 0)

            @block.tensor
            def _(pe):
                pe.wait_ge(w_in[4], 48)
                xp_p(pe, 0)
                dt_p(pe, 0, range(KT))

        for t in (V, AC):
            t.close()

        units = [(m, q) for m in range(KT) for q in range(NU)]
        V.layer(["u"] + [f"skip{m}" for m in range(KT)]
                + [x for i, (m, q) in enumerate(units) for x in
                   ([f"scan{m}_{q}", f"hc{m}_{q}"] + ([f"res{m - 1}"] if q == 1 and m else []))]
                + ["res7"])
        AC.layer([f"da{m}_{q}" for m, q in units])
        G.layer([f"bx{m}_{q}" for m, q in units])
        PE.layer([f"y{m}_{q}" for m, q in units])

        with nc.Block() as block:
            @block.sync
            def _(sp):
                with sp.Fori(1, NC - 1, 2) as r:
                    spread(sp, r, 1)
                    spread(sp, r + 1, 0)
                spread(sp, NC - 1, 1)

            @block.gpsimd
            def _(g):
                def chunk(c, slot):
                    G.here = 0
                    g.wait_ge(bc_in, c * 16 + 16)
                    g.wait_ge(V.sem, V.at("u", c))
                    for i, (m, q) in enumerate(units):
                        if i >= ST:
                            mm_, qq_ = units[i - ST]
                            g.wait_ge(PE.sem, PE.at(f"y{mm_}_{qq_}", c))
                        g.tensor_tensor(st[i % ST], ux[:, m, :].unsqueeze(1).broadcast_to([P, UN, CT]),
                                        words(BC_AT + slot * BC_W + q * UW, UN, CT), ALU.mult
                                        ).then_inc(G.done(f"bx{m}_{q}"), 1)

                with g.Fori(0, NC, 2) as c:
                    chunk(c, 0)
                    chunk(c + 1, 1)

            @block.vector
            def _(v):
                with v.Fori(0, NC, 2) as even:
                    for slot in range(2):
                        c = even + slot
                        V.here = 0
                        n = c + (LAYER5 * NC + 1)
                        c1 = following(v, c)
                        v.wait_ge(XV.sem, XV.at("dt", c))
                        v.tensor_tensor(ux, dt[slot], xn, ALU.mult).then_inc(V.done("u"), 1)
                        for m in range(KT):
                            v.scalar_tensor_tensor(out=h_tile(c, m), in0=xn[:, m, :], scalar=bias("skip", m),
                                                   in1=h_tile(c, m), op0=ALU.mult, op1=ALU.add
                                                   ).then_inc(V.done(f"skip{m}"), 1)
                        for i, (m, q) in enumerate(units):
                            v.wait_ge(AC.sem, AC.at(f"da{m}_{q}", c))
                            v.wait_ge(G.sem, G.at(f"bx{m}_{q}", c))
                            v.tensor_tensor_scan(st_flat[i % ST], da_flat[i % 2], st_flat[i % ST], 0.0, ALU.mult, ALU.add
                                                 ).then_inc(V.done(f"scan{m}_{q}"), 1)
                            own(v, V, c)
                            v.tensor_tensor(st_flat[i % ST], st_flat[i % ST],
                                            words(BC_AT + slot * BC_W + SSM * CT + q * UW, UW), ALU.mult
                                            ).then_inc(V.done(f"hc{m}_{q}"), 1)
                            if q == 1 and m:
                                v.wait_ge(PE.sem, PE.at(f"y{m - 1}_{NU - 1}", c))
                                v.tensor_tensor(h_tile(c, m - 1), PS[:, 4 + (m - 1) % 3, 0:CT], h_tile(c, m - 1), ALU.add
                                                ).then_inc(V.done(f"res{m - 1}"), 1)
                            if (m, q) == (0, 1):
                                ln_v1(v, n, h_chunk(c1))
                            if (m, q) == (0, 3):
                                ln_v2(v, n, h_chunk(c1))
                            if (m, q) == (1, 3):
                                ln_v3(v, n, sq2)
                            if (m, q) == (3, 1):
                                ln_v4(v, n)
                                ln_v5(v, n)
                            if (m, q) == (7, 3):
                                dt_v(v, c + 1, 1 - slot)
                        v.wait_ge(PE.sem, PE.at(f"y7_{NU - 1}", c))
                        v.tensor_tensor(h_tile(c, 7), PS[:, 4 + 7 % 3, 0:CT], h_tile(c, 7), ALU.add
                                        ).then_inc(V.done("res7"), 1)

            @block.scalar
            def _(a):
                with a.Fori(0, NC, 2) as even:
                    for slot in range(2):
                        c = even + slot
                        AC.here = 0
                        n = c + (LAYER5 * NC + 1)
                        a.wait_ge(XV.sem, XV.at("dt", c))
                        for i, (m, q) in enumerate(units):
                            mm_, qq_ = units[i - 2]
                            a.wait_ge(V.sem, (V.at if i >= 2 else V.prev)(f"scan{mm_}_{qq_}", c))
                            x = dt[slot][:, m, :].rearrange("p (b s) -> p b s", b=CB)[:, :, 1:]
                            for k in range(UN):
                                ins = a.activation(da[i % 2][:, k, :, 1:], x, ACT.Exp,
                                                   scale=neg_a[:, m, q * UN + k:q * UN + k + 1])
                            ins.then_inc(AC.done(f"da{m}_{q}"), 1)
                            if (m, q) == (1, 1):
                                ln_a1(a, n, sq2)
                            if (m, q) == (3, 0):
                                ln_a2(a, n)
                            if (m, q) == (4, 2):
                                a.wait_ge(bc_out, c * 16 + 16)
                                xp_a(a, c + 1)
                            if 0 <= i - 22 < KT // 2:
                                z_a(a, c + 1, 1 - slot, (2 * (i - 22), 2 * (i - 22) + 1))
                            if (m, q) == (6, 2):
                                abs_a(a, c + 1, 1 - slot)
                            if (m, q) == (7, 0):
                                exp_a(a, c + 1)
                            if (m, q) == (7, 1):
                                log_a(a, c + 1)

            @block.tensor
            def _(pe):
                with pe.Fori(0, NC) as c:
                    PE.here = 0
                    n = c + (LAYER5 * NC + 1)
                    for i, (m, q) in enumerate(units):
                        if q == 0 and m >= 3:
                            pe.wait_ge(V.sem, V.at(f"res{m - 3}", c))
                        pe.wait_ge(V.sem, V.at(f"hc{m}_{q}", c))
                        for k in range(UN):
                            mm = pe.matmul(PS[:, 4 + m % 3, 0:CT], ident, st[i % ST][:, k, :], start=q == 0 and k == 0,
                                           stop=q == NU - 1 and k == UN - 1)
                        mm.then_inc(PE.done(f"y{m}_{q}"), 1)
                        if (m, q) == (0, 2):
                            ln_p1(pe, n)
                        if (m, q) == (2, 2):
                            ln_p2(pe, n)
                        if (m, q) == (4, 0):
                            xp_p(pe, c + 1)
                        if 0 <= i - 20 < KT // 2:
                            dt_p(pe, c + 1, (2 * (i - 20), 2 * (i - 20) + 1))

        for t in (V, AC, G, PE, XP, XA, XV):
            t.close()
        if STOP_AFTER == 5:
            return finish()

        o = W_AT
        w_base = parts(o, KT, D)
        w_enc = words(o + KT * D, KT, ENC)
        w_wave = words(o + KT * D + KT * ENC, D, rows=ENC)
        enc_s = words(o + KT * D + KT * ENC + D, CT, rows=ENC)
        o += KT * D + KT * ENC + D + CT
        fourier = words(o, KT, D)
        coef = words(o + KT * D, KT, 3, ENC)
        mask_f = words(o + KT * D + KT * 3 * ENC, KT, 3, ENC)
        mask_u = A[:, o + KT * D + 2 * KT * 3 * ENC:o + KT * D + 2 * KT * 3 * ENC + KT * 3 * ENC // 4].bitcast(U8)
        w_sum = words(o + KT * D + 2 * KT * 3 * ENC + KT * 3 * ENC // 4, KT, ENC)
        o += KT * D + 2 * KT * 3 * ENC + KT * 3 * ENC // 4 + KT * ENC
        assert o + SLOTS * STAGE_W <= XS1_AT
        units = list(enumerate(units_of(w_base, T["base2_w"].rearrange("p (k n) -> p k n", k=KT), D, 2, o)))
        SX.layer(["hi", "lo"], 1 + NC)
        WA.layer([f"hi{u}" for u, _ in units], 1)
        WV.layer([f"lo{u}" for u, _ in units], 1)
        V.layer(["mask", "kept", "sum"], 1)
        PE.layer(["wave"], 1)
        AC.layer(["wave"], 1)
        with nc.Block() as block:
            @block.sync
            def _(sp):
                sp.dma_start(coef.rearrange("p k e r -> p (k e r)"), T["coef"]).then_inc(w_in[5], 16)
                sp.dma_start(mask_u.bitcast(mybir.dt.int32), T["mask"]).then_inc(w_in[5], 16)
                sp.dma_start(fourier, T["fourier"].rearrange("p (k n) -> p k n", k=KT)).then_inc(w_in[5], 16)
                sp.dma_start(w_enc, T["enc"].rearrange("p (k n) -> p k n", k=KT)).then_inc(w_in[5], 16)
                for u, unit in units:
                    stage_sp(sp, u, unit)

            @block.vector
            def _(v):
                split_xn(v, 0, 5 * NC)
                v.wait_ge(w_in[5], 64)
                v.tensor_copy(mask_f.rearrange("p k e r -> p (k e r)"), mask_u).then_inc(V.done("mask"), 1)
                own(v, V)
                v.tensor_tensor(coef, coef, mask_f, ALU.mult).then_inc(V.done("kept"), 1)
                own(v, V)
                v.tensor_reduce(w_sum, coef.rearrange("p k e r -> p k r e"), AX.X, ALU.add).then_inc(V.done("sum"), 1)
                for u, unit in units:
                    split_v(v, u, unit)

            @block.tensor
            def _(pe):
                pe.wait_ge(V.sem, V.at("sum"))
                for n in range(2):
                    for k in range(KT):
                        mm = pe.matmul(PS[0:ENC, 1 + n, :], w_sum[:, k, :], fourier[:, k, 512 * n:512 * n + 512],
                                       start=k == 0, stop=k == KT - 1)
                mm.then_inc(PE.done("wave"), 1)

            @block.scalar
            def _(a):
                for u, unit in units:
                    split_a(a, u, unit)
                a.wait_ge(PE.sem, PE.at("wave"))
                a.activation(w_wave.rearrange("p (n w) -> p n w", n=2), PS[0:ENC, 1:3, :], ACT.Copy, scale=0.5
                             ).then_inc(AC.done("wave"), 1)

        for t in (V, AC, PE):
            t.close()
        V.layer([f"res{m}" for m in range(KT)])
        AC.layer(["enc"])
        PE.layer(["enc"] + [f"out{m}" for m in range(KT)])
        with nc.Block() as block:
            @block.vector
            def _(v):
                with v.Fori(0, NC, 2) as even:
                    for slot in range(2):
                        c = even + slot
                        V.here = 0
                        n = c + (5 * NC + 1)
                        c1 = following(v, c)
                        ln_v1(v, n, h_chunk(c1))
                        ln_v2(v, n, h_chunk(c1))
                        for m in range(KT):
                            v.wait_ge(PE.sem, PE.at(f"out{m}", c))
                            v.scalar_tensor_tensor(out=h_tile(c, m), in0=PS[:, 2 + m % 4, 0:CT], scalar=bias("base2_b", m),
                                                   in1=h_tile(c, m), op0=ALU.add, op1=ALU.add).then_inc(V.done(f"res{m}"), 1)
                            if m == 2:
                                ln_v3(v, n, sq2)
                            if m == 4:
                                ln_v4(v, n)
                                ln_v5(v, n, [(PE.sem, PE.at("enc", c))])
                                split_xn(v, c + 1, n, 1 - slot)

            @block.scalar
            def _(a):
                with a.Fori(0, NC, 2) as even:
                    for slot in range(2):
                        c = even + slot
                        AC.here = 0
                        n = c + (5 * NC + 1)
                        a.wait_ge(PE.sem, PE.at("enc", c))
                        a.wait_ge(PE.sem, PE.prev("out7", c))
                        a.activation(enc_s, PS[0:ENC, 1, 0:CT], ACT.Copy).then_inc(AC.done("enc"), 1)
                        ln_a1(a, n, sq2)
                        ln_a2(a, n)

            @block.tensor
            def _(pe):
                with pe.Fori(0, NC, 2) as even:
                    for slot in range(2):
                        c = even + slot
                        PE.here = 0
                        n = c + (5 * NC + 1)
                        pe.wait_ge(LV.sem, LV.at("out", n - 1))
                        pe.wait_ge(AC.sem, AC.prev("enc", c))
                        gemm(pe, PS[0:ENC, 1, 0:CT], lambda k: w_enc[:, k, :], range(KT)).then_inc(PE.done("enc"), 1)
                        for m in range(KT):
                            bank = PS[:, 2 + m % 4, 0:CT]
                            if m >= 4:
                                pe.wait_ge(V.sem, V.at(f"res{m - 4}", c))
                            else:
                                pe.wait_ge(V.sem, V.prev(f"res{m + 4}", c))
                            if m == 0:
                                pe.wait_ge(SX.sem, SX.at("lo", c))
                            gemm3(pe, bank, lambda k, part: w_base[:, k, part, m * P:m * P + P], of_xs(slot), last=False)
                            if m == 0:
                                pe.wait_ge(AC.sem, AC.at("enc", c))
                            pe.matmul(bank, w_wave[:, m * P:m * P + P], enc_s, start=False, stop=True
                                      ).then_inc(PE.done(f"out{m}"), 1)
                            if m == 1:
                                ln_p1(pe, n)
                            if m == 4:
                                ln_p2(pe, n)

        for t in (V, AC, PE, SX, WA, WV):
            t.close()
        staged = [staged[i] + len(units[i::SLOTS]) for i in range(SLOTS)]
        if STOP_AFTER == 6:
            return finish()

        w_q = parts(W_AT, KT, D)
        w_k = parts(W_AT + KT * D, KT, 256)
        w_v7 = parts(W_AT + KT * D + KT * 256, KT, 256)
        units = []
        for dst, name, n, per in ((w_q, "q_w", D, 2), (w_k, "k_w", 256, KT), (w_v7, "v_w", 256, KT)):
            units += units_of(dst, T[name].rearrange("p (k n) -> p k n", k=KT), n, per)
        units = list(enumerate(units))
        SX.layer(["hi", "lo"])
        WA.layer([f"hi{u}" for u, _ in units], 1)
        WV.layer([f"lo{u}" for u, _ in units], 1)
        v7 = words(vb_at, CB, 256, rows=S)
        NQ7, NR7 = 12, 10
        V.layer([f"{x}{m}" for m in range(NR7) for x in ("rs", "rr", "rh", "rl")]
                + [x for g in range(GROUPS + LAG + 1) for x in
                   ([f"sum{g - 1}", f"rcp{g - 1}"] if 0 < g <= GROUPS else [])
                   + ([f"ctx{g - LAG - 1}"] if g > LAG else []) + ([f"max{g}", f"mask{g}"] if g < GROUPS else [])])
        AC.layer([f"ev{m}" for m in range(NQ7)] + ["vt0"] + [x for g in range(GROUPS + LAG)
                                                                       for x in probs_names(g)])
        G.layer([f"rc{m}" for m in range(NR7)] + [f"norm{g}" for g in range(GROUPS)])
        pe_names = []
        for m in range(NQ7 + 2):
            pe_names += ([f"qkv{m}"] if m < NQ7 else []) + ([f"rot{m - 2}"] if 2 <= m < NR7 + 2 else [])
        pe_names.append("Vt0")
        for g in range(GROUPS + LAG):
            pe_names += ([f"S{g}"] if g < GROUPS else []) + (value_names(g - LAG) if g >= LAG else [])
        PE.layer(pe_names)
        with nc.Block() as block:
            @block.sync
            def _(sp):
                for u, unit in units:
                    stage_sp(sp, u, unit)

            @block.vector
            def _(v):
                for u, unit in units:
                    split_v(v, u, unit)
                with v.Fori(0, NC) as c:
                    V.here = 0
                    n = c + (6 * NC + 1)
                    c1 = following(v, c)
                    ln_v1(v, n, h_chunk(c1))
                    for m in range(NR7):
                        rope_v(v, c, m)
                        if m == 3:
                            ln_v2(v, n, h_chunk(c1))
                        if m == 6:
                            ln_v3(v, n, sq)
                    for g in range(GROUPS + LAG + 1):
                        if 0 < g <= GROUPS:
                            soft_sum(v, c, g - 1)
                        if g > LAG:
                            done = g - LAG - 1
                            b, half = done // 2, done % 2
                            dst = h_chunk(c)[:, half * 4:half * 4 + 4, b * S:(b + 1) * S]
                            v.wait_ge(PE.sem, PE.at(f"O{done}", c))
                            v.tensor_tensor(dst, PS[:, 7, 0:4 * S].rearrange("p (j t) -> p j t", j=4), dst, ALU.add
                                            ).then_inc(V.done(f"ctx{done}"), 1)
                        if g < GROUPS:
                            soft_top(v, c, g, False)
                        if g == 2:
                            ln_v4(v, n)
                        if g == 3:
                            ln_v5(v, n, [(PE.sem, PE.at("qkv11", c))])
                        if g == 5:
                            split_xn(v, c, n)

            @block.gpsimd
            def _(g):
                with g.Fori(0, NC) as c:
                    G.here = 0
                    for m in range(NR7):
                        rope_g(g, c, m, (qT if m < KT else kT)[:, m % KT, :])
                    for i in range(GROUPS):
                        soft_norm(g, c, i)

            @block.scalar
            def _(a):
                for u, unit in units:
                    split_a(a, u, unit)
                with a.Fori(0, NC) as c:
                    AC.here = 0
                    n = c + (6 * NC + 1)
                    for m in range(NQ7):
                        x, name, i = ((qT, "q_b", m) if m < KT else (kT, "k_b", m - KT) if m < NR7
                                      else (vT, "v_b", m - NR7))
                        a.wait_ge(PE.sem, PE.at(f"qkv{m}", c))
                        a.activation(x[:, i, :], PS[:, 1 + m % 4, 0:CT], ACT.Identity, bias=bias(name, i)
                                     ).then_inc(AC.done(f"ev{m}"), 1)
                        if m == 8:
                            ln_a1(a, n, sq)
                    a.wait_ge(PE.sem, PE.at("Vt0", c))
                    a.activation(v7.rearrange("p (n b) w -> p n (b w)", n=2), PS[0:S, 5:7, :], ACT.Copy
                                 ).then_inc(AC.done("vt0"), 1)
                    ln_a2(a, n)
                    for g in range(GROUPS + LAG):
                        probs_a(a, c, g, False)

            @block.tensor
            def _(pe):
                pe.wait_ge(WV.sem, WV.at(f"lo{KT // 2 - 1}"))
                with pe.Fori(0, NC) as c:
                    PE.here = 0
                    n = c + (6 * NC + 1)
                    pe.wait_ge(SX.sem, SX.prev("lo", c))
                    for m in range(NQ7 + 2):
                        if m < NQ7:
                            if m >= 4:
                                pe.wait_ge(AC.sem, AC.at(f"ev{m - 4}", c))
                            else:
                                pe.wait_ge(V.sem, V.prev("mask7", c))
                            w, i = (w_q, m) if m < KT else (w_k, m - KT) if m < NR7 else (w_v7, m - NR7)
                            if m == KT:
                                pe.wait_ge(WV.sem, WV.at(f"lo{len(units) - 1}"))
                            gemm3(pe, PS[:, 1 + m % 4, 0:CT], lambda k, part: w[:, k, part, i * P:i * P + P], of_xs(0)
                                  ).then_inc(PE.done(f"qkv{m}"), 1)
                        if m == 3:
                            ln_p1(pe, n)
                        if m == 10:
                            ln_p2(pe, n)
                        if 2 <= m < NR7 + 2:
                            rope_p(pe, c, m - 2, (qT if m - 2 < KT else kT)[:, (m - 2) % KT, :])
                    pe.wait_ge(V.sem, V.at("rl9", c))
                    pe.wait_ge(AC.sem, AC.at("ev11", c))
                    for b in range(CB):
                        for f in range(2):
                            o = (b % 2) * 256 + f * P
                            mm = pe.transpose(PS[0:S, 5 + b // 2, o:o + P], vT[:, f, b * S:(b + 1) * S], ident)
                    mm.then_inc(PE.done("Vt0"), 1)
                    for g in range(GROUPS + LAG):
                        if g < GROUPS:
                            scores_p(pe, c, g, True)
                        if g >= LAG:
                            values_p(pe, c, g - LAG,
                                     lambda u, j, q=g - LAG: v7[:, q // 2, (q % 2 * 4 + j) * HD:(q % 2 * 4 + j) * HD + HD],
                                     lambda u, j: PS[32 * u:32 * u + 32, 7, j * S:(j + 1) * S],
                                     V.sem, V.at(f"ctx{g - LAG - 1}", c) if g > LAG else V.prev("ctx7", c),
                                     lambda u, q=g: [(AC.sem, AC.at(f"pt{q - LAG - 1}_{2 + u}", c))] if q > LAG else
                                     [(AC.sem, AC.at("vt0", c))])

        for t in (V, AC, G, PE, SX, WA, WV):
            t.close()
        staged = [staged[i] + len(units[i::SLOTS]) for i in range(SLOTS)]
        if STOP_AFTER == 7:
            return finish()

        NJ = EXPERTS * MIXR // P
        o = W_AT
        w_base = parts(o, KT, D)
        w_down = parts(o + KT * D, KT, EXPERTS * MIXR)
        o += KT * D + KT * EXPERTS * MIXR
        w_up = parts(o, NJ, D)
        w_key = words(o + NJ * D, KT, KEYS)
        keys = words(o + NJ * D + KT * KEYS, EXPERTS)
        o += NJ * D + KT * KEYS + EXPERTS
        x_sum = words(o, KT, CB)
        query = words(o + 32, CB)
        score = words(o + 36, EXPERTS, rows=CB)
        s_top, s_den = words(o + 44, 1, rows=CB), words(o + 45, 1, rows=CB)
        score_t = words(o + 46, CB, rows=EXPERTS)
        mix = words(o + 50, NJ, CB)
        wh = words(o + 66, NJ, CT)
        wh_s = A[:, o + 66 + NJ * CT:o + 66 + 2 * NJ * CT].bitcast(BF16).rearrange("p (two j t) -> p two j t", two=2, j=NJ)
        o += 66 + 2 * NJ * CT
        assert o + SLOTS * STAGE_W <= XS1_AT
        units = []
        for dst, name, n, per in ((w_base, "base3_w", D, 2), (w_down, "down", EXPERTS * MIXR, 4), (w_up, "up", D, 2)):
            units += units_of(dst, T[name].rearrange("p (k n) -> p k n", n=n), n, per, o)
        units = list(enumerate(units))
        SX.layer(["hi", "lo"])
        WA.layer([f"hi{u}" for u, _ in units], 1)
        WV.layer([f"lo{u}" for u, _ in units], 1)
        V.layer(["xsum", "top", "off", "den", "rden", "coef"] + [f"wh{j}" for j in range(NJ)]
                + ["wh_hi", "wh_lo"] + [f"res{m}" for m in range(KT)])
        AC.layer(["query", "exp", "turned", "mix"])
        order = [("base", 0), ("query", 0), ("base", 1), ("score", 0), ("down", 0), ("turn", 0), ("down", 1), ("mix", 0),
                 ("base", 2), ("down", 2), ("down", 3), ("base", 3)]
        for m in range(4, KT):
            order += [("up", m - 4), ("base", m)]
        order += [("up", m) for m in range(4, KT)]
        PE.layer([f"{x}{m}" for x, m in order])
        with nc.Block() as block:
            @block.sync
            def _(sp):
                for u, unit in units:
                    stage_sp(sp, u, unit)
                    if u == 1:
                        sp.dma_start(w_key, T["wq"].rearrange("p (k n) -> p k n", k=KT)).then_inc(w_in[7], 16)
                        sp.dma_start(keys, T["keys"]).then_inc(w_in[7], 16)
                with sp.Fori(0, NC) as c:
                    sp.wait_ge(V.sem, V.at("res7", c))
                    sp.dma_start(T["out"][bass.ds(c, 1)].rearrange("c p w -> p (c w)"),
                                 A[:, bass.ds(c * CW, CW)]).then_inc(out_done, 16)
                sp.wait_ge(out_done, 16 * NC)

            @block.vector
            def _(v):
                for u, unit in units:
                    split_v(v, u, unit)
                with v.Fori(0, NC, 2) as even:
                    for slot in range(2):
                        c = even + slot
                        V.here = 0
                        n = c + (7 * NC + 1)
                        c1 = following(v, c)
                        v.wait_ge(LV.sem, LV.at("out", n - 1))
                        v.tensor_reduce(x_sum, xn.rearrange("p k (b s) -> p k b s", b=CB), AX.X, ALU.add
                                        ).then_inc(V.done("xsum"), 1)
                        ln_v1(v, n, h_chunk(c1))
                        v.wait_ge(PE.sem, PE.at("score0", c))
                        v.tensor_reduce(s_top, PS[0:CB, 1, 8:8 + EXPERTS], AX.X, ALU.max).then_inc(V.done("top"), 1)
                        own(v, V, c)
                        v.tensor_scalar(score, PS[0:CB, 1, 8:8 + EXPERTS], s_top, None, ALU.subtract).then_inc(V.done("off"), 1)
                        v.wait_ge(AC.sem, AC.at("exp", c))
                        v.tensor_reduce(s_den, score, AX.X, ALU.add).then_inc(V.done("den"), 1)
                        own(v, V, c)
                        v.reciprocal(s_den, s_den).then_inc(V.done("rden"), 1)
                        own(v, V, c)
                        v.tensor_scalar(score, score, s_den, None, ALU.mult).then_inc(V.done("coef"), 1)
                        ln_v2(v, n, h_chunk(c1))
                        v.wait_ge(AC.sem, AC.at("mix", c))
                        for j in range(NJ):
                            v.wait_ge(PE.sem, PE.at(f"down{j}", c))
                            v.tensor_tensor(wh[:, j, :].rearrange("p (b s) -> p b s", b=CB),
                                            PS[:, (2, 7)[j % 2], 0:CT].rearrange("p (b s) -> p b s", b=CB),
                                            mix[:, j, :].unsqueeze(2).broadcast_to([P, CB, S]), ALU.mult
                                            ).then_inc(V.done(f"wh{j}"), 1)
                        own(v, V, c)
                        v.tensor_copy(wh_s[:, 0], wh).then_inc(V.done("wh_hi"), 1)
                        own(v, V, c)
                        v.tensor_tensor(wh_s[:, 1], wh, wh_s[:, 0], ALU.subtract).then_inc(V.done("wh_lo"), 1)
                        ln_v3(v, n, sq2)
                        for m in range(KT):
                            v.wait_ge(PE.sem, PE.at(f"up{m}", c))
                            v.tensor_tensor(h_tile(c, m), PS[:, 3 + m % 4, 0:CT], h_tile(c, m), ALU.add
                                            ).then_inc(V.done(f"res{m}"), 1)
                            if m == 3:
                                ln_v4(v, n)
                                ln_v5(v, n)
                                split_xn(v, c, n, 1 - slot)

            @block.scalar
            def _(a):
                for u, unit in units:
                    split_a(a, u, unit)
                with a.Fori(0, NC, 2) as even:
                    for slot in range(2):
                        c = even + slot
                        AC.here = 0
                        n = c + (7 * NC + 1)
                        a.wait_ge(PE.sem, PE.at("query0", c))
                        a.activation(query, PS[:, 1, 0:CB], ACT.Copy, scale=1.0 / S).then_inc(AC.done("query"), 1)
                        a.wait_ge(V.sem, V.at("off", c))
                        a.activation(score, score, ACT.Exp, scale=float(KEYS) ** -0.5).then_inc(AC.done("exp"), 1)
                        a.wait_ge(PE.sem, PE.at("turn0", c))
                        a.activation(score_t, PS[0:EXPERTS, 1, 32:32 + CB], ACT.Copy).then_inc(AC.done("turned"), 1)
                        a.wait_ge(PE.sem, PE.at("mix0", c))
                        a.activation(mix, PS[:, 1, 64:64 + NJ * CB].rearrange("p (j b) -> p j b", j=NJ), ACT.Copy
                                     ).then_inc(AC.done("mix"), 1)
                        ln_a1(a, n, sq2)
                        ln_a2(a, n)

            @block.tensor
            def _(pe):
                pe.wait_ge(w_in[7], 32)
                pe.wait_ge(WV.sem, WV.at(f"lo{KT // 2 - 1}"))
                with pe.Fori(0, NC, 2) as even:
                    for slot in range(2):
                        c = even + slot
                        PE.here = 0
                        n = c + (7 * NC + 1)
                        for what, m in order:
                            bank = PS[:, 3 + m % 4, 0:CT]
                            if what == "query":
                                pe.wait_ge(V.sem, V.at("xsum", c))
                                pe.wait_ge(AC.sem, AC.prev("mix", c))
                                for k in range(KT):
                                    mm = pe.matmul(PS[:, 1, 0:CB], w_key[:, k, :], x_sum[:, k, :], start=k == 0,
                                                   stop=k == KT - 1)
                            elif what == "score":
                                pe.wait_ge(AC.sem, AC.at("query", c))
                                mm = pe.matmul(PS[0:CB, 1, 8:8 + EXPERTS], query, keys, start=True, stop=True)
                            elif what == "turn":
                                mm = pe.transpose(PS[0:EXPERTS, 1, 32:32 + CB], score, const("ident", CB)[:, 0:CB])
                            elif what == "mix":
                                pe.wait_ge(AC.sem, AC.at("turned", c))
                                for j in range(NJ):
                                    mm = pe.matmul(PS[:, 1, 64 + CB * j:64 + CB * j + CB], const(f"mix{j}", EXPERTS), score_t,
                                                   start=True, stop=True)
                            elif what == "down":
                                if m >= 2:
                                    pe.wait_ge(V.sem, V.at(f"wh{m - 2}", c))
                                elif m == 1:
                                    pe.wait_ge(V.sem, V.prev("wh3", c))
                                else:
                                    pe.wait_ge(WV.sem, WV.at(f"lo{len(units) - 1}"))
                                    pe.wait_ge(V.sem, V.at("coef", c))
                                mm = gemm3(pe, PS[:, (2, 7)[m % 2], 0:CT], lambda k, part: w_down[:, k, part, m * P:m * P + P],
                                           of_xs(slot))
                            elif what == "base":
                                if m >= 4:
                                    pe.wait_ge(V.sem, V.at(f"res{m - 4}", c))
                                else:
                                    pe.wait_ge(V.sem, V.prev(f"res{m + 4}", c))
                                if m == 0:
                                    pe.wait_ge(SX.sem, SX.prev("lo", c))
                                mm = gemm3(pe, bank, lambda k, part: w_base[:, k, part, m * P:m * P + P], of_xs(slot),
                                           last=False)
                            else:
                                if m == 0:
                                    pe.wait_ge(V.sem, V.at("wh_lo", c))
                                mm = gemm3(pe, bank, lambda j, part: w_up[:, j, part, m * P:m * P + P],
                                           lambda j, part: wh_s[:, part, j, :], NJ, first=False)
                            mm.then_inc(PE.done(f"{what}{m}"), 1)
                            if (what, m) == ("base", 1):
                                ln_p1(pe, n)
                            if (what, m) == ("up", 0):
                                ln_p2(pe, n)


def rows_first(w):
    k, n = w.shape
    return np.ascontiguousarray(w.reshape(k // P, P, n).transpose(1, 0, 2).reshape(P, -1))


def columns(b):
    return np.ascontiguousarray(b.reshape(-1, P).T)


def lay_out(i):
    x = i["x"]
    t = dict(const=CONST)
    t["x_re"] = np.tile(x[..., 0].transpose(2, 1, 0).reshape(STATES, -1), (2, 1))
    t["x_im"] = np.tile(x[..., 1].transpose(2, 1, 0).reshape(STATES, -1), (2, 1))
    t["abslog"] = np.tile(i["L0_tok_A_abslog"].T, (2, 1))
    t["phase"] = np.tile(i["L0_tok_A_phase"].T, (2, 1))
    t["cls"] = columns(i["cls_tok"].reshape(-1))
    t["qkv_w"] = rows_first(i["L0_attn_qkv_w"])
    t["qkv_b"] = columns(i["L0_attn_qkv_b"])
    t["out_w"] = rows_first(i["L0_attn_out_w"])
    t["out_b"] = columns(i["L0_attn_out_b"])
    t["base0_w"] = rows_first(i["L0_ffn_W_base"].T)
    t["base0_b"] = columns(i["L0_ffn_b_base"])
    t["router0"] = rows_first(i["L0_ffn_W_router"].T)
    t["a0"] = rows_first(i["L0_ffn_A_stack"].reshape(P, D).T)
    t["b0"] = i["L0_ffn_B_stack"].transpose(0, 2, 1).reshape(P, D)
    for n, k in (("q", "bv_q"), ("k", "bv_k"), ("v", "bv_v")):
        t[f"bind_{n}"] = i[f"L1_attn_{k}"]
    t["router1"] = rows_first(i["L1_ffn_route_w"].T)
    t["a1"] = rows_first(i["L1_ffn_A"].reshape(P, D).T)
    t["b1"] = i["L1_ffn_Bw"].transpose(0, 2, 1).reshape(P, D)
    t["a_log"] = rows_first(i["L2_attn_A_log"])
    t["skip"] = columns(i["L2_attn_D"])
    t["xproj"] = rows_first(i["L2_attn_x_proj_w"].T)
    t["dtw"] = i["L2_attn_dt_proj_w"].T
    t["dt_b"] = columns(i["L2_attn_dt_proj_b"])
    t["base2_w"] = rows_first(i["L2_ffn_W_base"].T)
    t["base2_b"] = columns(i["L2_ffn_b_base"])
    enc = np.concatenate([i["L2_ffn_enc0"], i["L2_ffn_enc1"]], 0)
    t["enc"] = rows_first(enc.T)
    coef = np.concatenate([i["L2_ffn_coefs0"], i["L2_ffn_coefs1"]], 2).transpose(1, 0, 2)
    mask = np.concatenate([i["L2_ffn_mask0"], i["L2_ffn_mask1"]], 2).transpose(1, 0, 2)
    t["coef"] = rows_first(coef.reshape(D, -1))
    t["mask"] = rows_first(mask.reshape(D, -1)).view(np.int32)
    t["fourier"] = rows_first(FOURIER)
    order = np.array([(4 * (4 * (t8 // 4) + j) + t8 % 4) * HD + d
                      for t8 in range(8) for j in range(4) for d in range(HD)])
    t["q_w"] = rows_first(i["L3_attn_wq"][:, order])
    t["q_b"] = columns(i["L3_attn_bq"][order])
    t["k_w"] = rows_first(i["L3_attn_wk"])
    t["k_b"] = columns(i["L3_attn_bk"])
    t["v_w"] = rows_first(i["L3_attn_wv"])
    t["v_b"] = columns(i["L3_attn_bv"])
    t["base3_w"] = rows_first(i["L3_ffn_W_org"].T)
    t["down"] = rows_first(i["L3_ffn_lora_down"].transpose(1, 0, 2).reshape(D, EXPERTS * MIXR))
    t["up"] = rows_first(i["L3_ffn_lora_up"].reshape(EXPERTS * MIXR, D))
    t["keys"] = i["L3_ffn_lora_keys"].T
    t["wq"] = rows_first(i["L3_ffn_Wq"].T)
    return {k: np.ascontiguousarray(v) for k, v in t.items()}


def fourier_matrix():
    t, n = np.arange(D, dtype=np.float64), D
    f = np.zeros((D, D))
    f[0] = 1.0 / np.sqrt(n)
    pair = np.sqrt(n / 2.0) * 2.0 / n
    for k in range(1, (n - 1) // 2 + 1):
        f[2 * k - 1] = pair * np.cos(2 * np.pi * k * t / n)
        f[2 * k] = pair * np.sin(2 * np.pi * k * t / n)
    f[n - 1] = np.sqrt(n) / n * (-1.0) ** t
    return f.astype(np.float32)


FOURIER = fourier_matrix()


def kernel(**inputs):
    import concourse.bacc as _bacc
    from concourse.bass_utils import run_bass_kernel_spmd as _run

    nc = _bacc.Bacc("TRN2", target_bir_lowering=False, num_devices=1, dynamic_dma_scratch_size=1024)
    arrays = {f"in_{k}": v for k, v in lay_out({k: np.asarray(v) for k, v in inputs.items()}).items()}
    tensors = {k[3:]: nc.dram_tensor(k, a.shape, mybir.dt.from_np(a.dtype), kind="ExternalInput").ap()
               for k, a in arrays.items()}
    tensors["out"] = nc.dram_tensor("out_h", (NC, P, CW), F32, kind="ExternalOutput").ap()
    build(nc, tensors)
    r = _run(nc, [arrays], core_ids=[0])
    h = r.results[0]["out_h"].reshape(NC, P, KT, CB, S)
    return np.ascontiguousarray(h.transpose(0, 3, 4, 2, 1).reshape(IMAGES, S, D))
```
